# Optimizing a Trainium2 kernel written in Bass

```python
import numpy as np
import jax
import jax.numpy as jnp

def _softmax(x, axis=-1):
    return jax.nn.softmax(x, axis=axis)

def _gelu(x):
    return jax.nn.gelu(x, approximate=True)

def _silu(x):
    return jax.nn.silu(x)

def _sigmoid(x):
    return jax.nn.sigmoid(x)

def _layernorm(x, axis=-1, eps=1e-05):
    m = jnp.mean(x, axis=axis, keepdims=True)
    v = jnp.var(x, axis=axis, keepdims=True)
    return (x - m) / jnp.sqrt(v + eps)

def _scatter_add(tgt, idx, src, axis=0):
    return tgt.at[idx].add(src)

def _segment_sum(src, seg, n):
    return jax.ops.segment_sum(src, seg, n)
kernel_name = 'mk_sandwich_d1_jaxref_r8_e8cfbd'

def setup_inputs(seed: int=0):
    np.random.seed(seed)
    _w = jnp.asarray

    def _L0_attn_setup():
        import jax, jax.numpy as jnp
        import numpy as np
        NUM_HEADS = 16
        key = jax.random.key(seed)
        ks = jax.random.split(key, 11)
        B, S, D = (4, 128, 128)
        M = 128
        hd = D // NUM_HEADS
        s = 0.02
        return {'x': jax.random.normal(ks[0], (B, S, D), jnp.float32), 'Wq': jax.random.normal(ks[1], (D, D), jnp.float32) * s, 'bq': jax.random.normal(ks[2], (D,), jnp.float32) * s, 'Wk': jax.random.normal(ks[3], (D, D), jnp.float32) * s, 'bk': jax.random.normal(ks[4], (D,), jnp.float32) * s, 'Wv': jax.random.normal(ks[5], (D, D), jnp.float32) * s, 'bv': jax.random.normal(ks[6], (D,), jnp.float32) * s, 'Wo': jax.random.normal(ks[7], (D, D), jnp.float32) * s, 'bo': jax.random.normal(ks[8], (D,), jnp.float32) * s, 'rel_k': jax.random.normal(ks[9], (2 * M + 1, hd), jnp.float32), 'rel_v': jax.random.normal(ks[10], (2 * M + 1, hd), jnp.float32)}
    _L0_attn_in = _L0_attn_setup()

    def _L0_ffn_setup():
        import jax, jax.numpy as jnp
        import numpy as np
        E = 16
        H = 128
        F = 256
        TOP_K = 1
        B, S = (2, 128)
        key = jax.random.key(seed)
        ks = jax.random.split(key, 7)
        s = 0.02
        return {'hidden_states': jax.random.normal(ks[0], (B, S, H), jnp.float32), 'w_router': jax.random.normal(ks[1], (E, H), jnp.float32) * s, 'gate_up_proj': jax.random.normal(ks[2], (E, H, 2 * F), jnp.float32) * s, 'down_proj': jax.random.normal(ks[3], (E, F, H), jnp.float32) * s, 'w_gate': jax.random.normal(ks[4], (F, H), jnp.float32) * s, 'w_up': jax.random.normal(ks[5], (F, H), jnp.float32) * s, 'w_down': jax.random.normal(ks[6], (H, F), jnp.float32) * s}
    _L0_ffn_in = _L0_ffn_setup()
    _d = {'L0_attn_x': _L0_attn_in['x'], 'L0_attn_Wq': _L0_attn_in['Wq'], 'L0_attn_bq': _L0_attn_in['bq'], 'L0_attn_Wk': _L0_attn_in['Wk'], 'L0_attn_bk': _L0_attn_in['bk'], 'L0_attn_Wv': _L0_attn_in['Wv'], 'L0_attn_bv': _L0_attn_in['bv'], 'L0_attn_Wo': _L0_attn_in['Wo'], 'L0_attn_bo': _L0_attn_in['bo'], 'L0_attn_rel_k': _L0_attn_in['rel_k'], 'L0_attn_rel_v': _L0_attn_in['rel_v'], 'L0_ffn_w_router': _L0_ffn_in['w_router'], 'L0_ffn_gate_up_proj': _L0_ffn_in['gate_up_proj'], 'L0_ffn_down_proj': _L0_ffn_in['down_proj'], 'L0_ffn_w_gate': _L0_ffn_in['w_gate'], 'L0_ffn_w_up': _L0_ffn_in['w_up'], 'L0_ffn_w_down': _L0_ffn_in['w_down']}
    _x0 = _d['L0_attn_x']
    _d['L0_attn_x'] = jax.random.normal(jax.random.fold_in(jax.random.key(seed), 1), (16, 512, 128), dtype=_x0.dtype)
    del _x0
    return _d

def reference(L0_attn_x, L0_attn_Wq, L0_attn_bq, L0_attn_Wk, L0_attn_bk, L0_attn_Wv, L0_attn_bv, L0_attn_Wo, L0_attn_bo, L0_attn_rel_k, L0_attn_rel_v, L0_ffn_w_router, L0_ffn_gate_up_proj, L0_ffn_down_proj, L0_ffn_w_gate, L0_ffn_w_up, L0_ffn_w_down):

    def _L0_attn_ref(x, Wq, bq, Wk, bk, Wv, bv, Wo, bo, rel_k, rel_v):
        import jax, jax.numpy as jnp
        import numpy as np
        NUM_HEADS = 16
        B, S, D = x.shape
        H = NUM_HEADS
        hd = D // H
        M = (rel_k.shape[0] - 1) // 2

        def proj(W, b):
            return (x @ W.T + b).reshape(B, S, H, hd).transpose(0, 2, 1, 3)
        q = proj(Wq, bq)
        k = proj(Wk, bk)
        v = proj(Wv, bv)
        r = jnp.arange(S)
        idx = jnp.clip(r[None, :] - r[:, None], -M, M) + M
        rpk = rel_k[idx]
        rpv = rel_v[idx]
        content = jnp.einsum('bhqd,bhkd->bhqk', q, k)
        relative = jnp.einsum('bhqd,qkd->bhqk', q, rpk)
        scores = (content + relative) / jnp.sqrt(jnp.float32(hd))
        w = jax.nn.softmax(scores, axis=-1)
        out = jnp.einsum('bhqk,bhkd->bhqd', w, v) + jnp.einsum('bhqk,qkd->bhqd', w, rpv)
        out = out.transpose(0, 2, 1, 3).reshape(B, S, D)
        return out @ Wo.T + bo

    def _L0_ffn_ref(hidden_states, w_router, gate_up_proj, down_proj, w_gate, w_up, w_down):
        import jax, jax.numpy as jnp
        import numpy as np
        E = 16
        H = 128
        F = 256
        TOP_K = 1
        B, S = (2, 128)
        b, s, h = hidden_states.shape
        x = hidden_states.reshape(-1, h)
        logits = x @ w_router.T
        _, top_idx = jax.lax.top_k(logits, TOP_K)
        mask = jax.nn.one_hot(top_idx, E, dtype=logits.dtype).sum(axis=1)
        scores = jax.nn.sigmoid(logits) * mask
        masked_inputs = scores.T[:, :, None] * x[None, :, :]
        gate_up = jnp.einsum('eth,ehf->etf', masked_inputs, gate_up_proj)
        gate, up = jnp.split(gate_up, 2, axis=-1)
        expert_out = jnp.einsum('etf,efh->eth', up * jax.nn.silu(gate), down_proj)
        shared = jax.nn.silu(x @ w_gate.T) * (x @ w_up.T) @ w_down.T
        out = shared + expert_out.sum(axis=0)
        return out.reshape(b, s, h)
    x = L0_attn_x
    x = x + _layernorm(_L0_attn_ref(_layernorm(x, axis=-1), L0_attn_Wq, L0_attn_bq, L0_attn_Wk, L0_attn_bk, L0_attn_Wv, L0_attn_bv, L0_attn_Wo, L0_attn_bo, L0_attn_rel_k, L0_attn_rel_v), axis=-1)
    x = x + _layernorm(_L0_ffn_ref(_layernorm(x, axis=-1), L0_ffn_w_router, L0_ffn_gate_up_proj, L0_ffn_down_proj, L0_ffn_w_gate, L0_ffn_w_up, L0_ffn_w_down), axis=-1)
    return x

_drawn_inputs = setup_inputs


def setup_inputs(seed=0):
    import zlib

    import numpy as np

    out = dict(_drawn_inputs(seed))
    spreads = {}
    factors = {'L0_attn_bq': 3.688, 'L0_attn_Wk': 4.338, 'L0_attn_bk': 8.0}
    for name, (base, spread) in spreads.items():
        noise = np.random.default_rng([zlib.crc32(name.encode()), seed]).standard_normal(out[name].shape)
        drawn = base * np.exp(spread * noise) if base else spread * noise
        out[name] = jnp.asarray(drawn.astype(out[name].dtype))
    for name, factor in factors.items():
        out[name] = (out[name] * factor).astype(out[name].dtype)
    return out
```

```python
from contextlib import ExitStack

import concourse.bass as bass
import numpy as np
from concourse import mybir

F32 = mybir.dt.float32
F16 = mybir.dt.float16
I32 = mybir.dt.int32
U32 = mybir.dt.uint32
ACT = mybir.ActivationFunctionType
ALU = mybir.AluOpType
AX = mybir.AxisListType

B, S, D = 16, 512, 128
H, HD = 16, 8
M = 128
NP = B // 2
P = 128
NT = S // P
E, F = 16, 256
TOK = B * S
TILES = TOK // P
SORTED = TILES + E
EPS = 1e-5

NU, NS, NB = 4, 4, 8
TERMS = ((0, 0), (0, 1), (1, 0))
ROWS_REL = NU * 3 * HD
ROWS_CON = 4 * 3 * HD + 8
NE8 = 8
SLOTS = 2 * NT * NT * NS
MAXSCALE = 2.0 ** -14
XMAX = 12.0

OFF0 = 255
WT_W, WT_0 = 415, 159
WN_W, WN_0 = 367, 127
Z_W, Z_0 = 384, 255


def attention(nc, out, x, Wq, bq, Wk, bk, Wv, bv, Wo, bo, rel_k, rel_v, w_router, gate_up, down, w_gate, w_up, w_down, dbg=None):
    ctx = ExitStack()
    outer = ExitStack()

    def dram(name, shape, dt):
        return nc.dram_tensor(name, shape, dt, kind="Internal").ap()

    qs_d = dram("qs_d", [B * H * HD, 2, S], F16)
    ks_d = dram("ks_d", [B * H * HD, NT, 2, 2, P], F16)
    ms_d = dram("ms_d", [B * H, 2, S], F16)
    vs_d = dram("vs_d", [B, P, NT, 2 * H * 9], F32)
    rvp_d = dram("rvp_d", [512, HD], F32)
    opv_d = dram("opv_d", [B * H * HD, S], F32)
    orl_d = dram("orl_d", [B * H * HD, S], F32)
    os_d = dram("os_d", [B * H, S], F32)
    x1_d = dram("x1_d", [TOK, D], F32)
    xn_d = dram("xn_d", [TOK, 2 * D], F32)
    oh_d = dram("oh_d", [B, P, NT * E], F32)
    xs_d = dram("xs_d", [SORTED * P, 2 * D], F32)
    ys_d = dram("ys_d", [SORTED * P, D], F32)

    with outer:
        def osb(name, shape, dt):
            return outer.enter_context(nc.sbuf_tensor(name, shape, dt))

        ident = osb("ident", [P, P], F32)
        sgu = osb("sgu", [P, 2 * F], F32)
        sdn = osb("sdn", [P, 2, D], F32)
        tri = osb("tri", [P, P], F32)
        ones = osb("ones", [P, P], F32)
        c15 = osb("c15", [P, NT], F32)

        moe_sem = {n: outer.enter_context(nc.semaphore(n)) for n in MOE_SEMS.split()}
        with ctx:
            attention_phase(nc, ctx, locals())
        with ExitStack() as moe_ctx:
            expert_phase(nc, moe_ctx, locals())


def root_guess(nc, dve, step, done, mean_var, half, root):
    nc.vector.tensor_scalar(half[:], mean_var[:, :, 1], EPS, 0.5, ALU.add, ALU.mult).then_inc(step, 1)
    dve.wait_ge(step, done + 1)
    nc.vector.tensor_scalar(root[:].bitcast(I32), half[:].bitcast(I32), 1, None, ALU.logical_shift_right).then_inc(step, 1)
    dve.wait_ge(step, done + 2)
    nc.vector.tensor_scalar(root[:].bitcast(I32), root[:].bitcast(I32), -1.0, float(0x5F3759DF - (1 << 22)), ALU.mult, ALU.add).then_inc(step, 1)


def newton(pool, step, root, half, tmp, c15):
    for it in range(3):
        step(4 * it, pool.tensor_tensor(tmp[:], root[:], root[:], ALU.mult))
        step(4 * it + 1, pool.tensor_tensor(tmp[:], tmp[:], half[:], ALU.mult))
        step(4 * it + 2, pool.tensor_tensor(tmp[:], c15[:], tmp[:], ALU.subtract))
        step(4 * it + 3, pool.tensor_tensor(root[:], root[:], tmp[:], ALU.mult))


def attention_phase(nc, ctx, a):
    (x, Wq, bq, Wk, bk, Wv, bv, Wo, bo, rel_k, rel_v, w_router, w_gate, w_up, w_down) = (
        a[n] for n in "x Wq bq Wk bk Wv bv Wo bo rel_k rel_v w_router w_gate w_up w_down".split())
    (qs_d, ks_d, ms_d, vs_d, rvp_d, opv_d, orl_d, os_d, x1_d, xn_d, oh_d, xs_d) = (
        a[n] for n in "qs_d ks_d ms_d vs_d rvp_d opv_d orl_d os_d x1_d xn_d oh_d xs_d".split())
    ident, sgu, sdn, tri, ones, c15 = (a[n] for n in "ident sgu sdn tri ones c15".split())

    def sb(name, shape, dt=F32):
        return ctx.enter_context(nc.sbuf_tensor(name, shape, dt))

    def pb(name, shape, dt=F32):
        return ctx.enter_context(nc.psum_tensor(name, shape, dt))

    def sem(name):
        return ctx.enter_context(nc.semaphore(name))

    wqT, wkT, wvT, woT = (sb(n, [P, P]) for n in ("wqT", "wkT", "wvT", "woT"))
    wrT = sb("wrT", [P, E])
    bq_s = sb("bq_s", [P, 1])
    kb = sb("kb", [P, 3])
    vb = sb("vb", [P, 3, P])
    bo_s = sb("bo_s", [P, P])
    escale = sb("escale", [P, 1])
    iota_e = sb("iota_e", [P, E])
    Wt = sb("Wt", [ROWS_REL, WT_W + 1], F16)
    Wn = sb("Wn", [P, WN_W + 1], F16)
    Rv = sb("Rv", [P, 32, Z_W // 32, HD])
    hmask = sb("hmask", [P, H])
    KC = [sb(f"KC{j}", [ROWS_CON, 2, 4, 2, P], F16) for j in range(NT)]
    VC = [sb(f"VC{j}", [P, 2, 2, H, 9]) for j in range(NT)]
    QC = [sb(f"QC{r}", [ROWS_CON, 2, 4, 4, P], F16) for r in range(2)]
    QT = [sb(f"QT{r}", [ROWS_REL, NU, 2, H, 32], F16) for r in range(2)]
    w = [sb(f"w{r}", [P, 2, NS, H, NU, NB]) for r in range(2)]
    pv_s = sb("pv_s", [P, 2, 4, P])
    rel_s = sb("rel_s", [P, 2 * H, NU, NB])
    xt = [sb(f"xt{r}", [P, NT, D]) for r in range(2)]
    st = sb("st", [P, NT, 6])
    mv = sb("mv", [P, NT, 2])
    var = sb("var", [P, NT])
    rstd = sb("rstd", [P, NT])
    rtmp = sb("rtmp", [P, NT])
    xn = sb("xn", [P, NT, D])
    xnT = sb("xnT", [P, S])
    qf = sb("qf", [P, S])
    kf = sb("kf", [P, 2, S])
    qs = [sb(f"qs{r}", [P, 2, S], F16) for r in range(2)]
    ks = sb("ks", [P, NT, 2, 2, P], F16)
    vst = sb("vst", [P, NT, 2, H, 9])
    kn = [sb(f"kn{r}", [P, 3, S], F16) for r in range(2)]
    Qb = [sb(f"Qb{r}", [P, NE8, H, 32], F16) for r in range(2)]
    Qn = sb("Qn", [P, NE8, H, NT * 16], F16)
    mx = sb("mx", [P, NT * 16])
    ms = sb("ms", [P, 2, NT * 16], F16)
    oA, oB, oS = (sb(n, [P, S]) for n in ("oA", "oB", "oS"))
    xr = sb("xr", [P, NT, D])
    y = sb("y", [P, NT, D])
    st2 = sb("st2", [P, NT, 6])
    mv2 = sb("mv2", [P, NT, 2])
    var2 = sb("var2", [P, NT])
    rstd2 = sb("rstd2", [P, NT])
    rtmp2 = sb("rtmp2", [P, NT])
    x1 = sb("x1", [P, NT, D])
    x2T = sb("x2T", [P, S])
    xs = sb("xs", [P, NT, 2 * D])
    lg = sb("lg", [P, NT, E])
    lmax = sb("lmax", [P, NT])
    cand = sb("cand", [P, NT, E])
    lidx = sb("lidx", [P, NT])
    oh = sb("oh", [P, NT, E])
    sg = sb("sg", [P, NT])

    sc = [pb(f"sc{r}", [P, S]) for r in range(2)]
    nat = pb("nat", [P, S])
    misc = pb("misc", [P, S])
    pv = [pb(f"pv{r}", [P, S]) for r in range(2)]
    rel = [pb(f"rel{r}", [P, S]) for r in range(2)]

    names = ("w_ld tab pool_set dve_set act_set pe_set sp_set zeroed "
             "x_ld0 x_ld1 xn_step xn_done xT_ps xnT_rdy q_ps q_ev k_ps k_ev v_ps v_ev qsplit ksplit "
             "qs_st ks_st vs_st qb_done qn_ld0 qn_ld1 nat_ps mx_done ms_step ms_done ms_st "
             "qc_ld0 qc_ld1 kc_ld0 kc_ld1 kc_ld2 kc_ld3 s_done exp_done pv_done pv_ev rel_ev o_st "
             "o_ld o_step O_rdy op_ps op_ev ln_step x1_done xn2_done x1_st x2T_ps x2T_ev lg_ps lg_ev "
             "dve_passed pool_passed sp_passed root root2 top_step sg_done xn_step2 xs_done xs_st z_st")
    s = {n: sem(n) for n in names.split()}
    x_ld = [s["x_ld0"], s["x_ld1"]]
    qn_ld = [s["qn_ld0"], s["qn_ld1"]]
    qc_ld = [s["qc_ld0"], s["qc_ld1"]]
    kc_ld = [s[f"kc_ld{j}"] for j in range(NT)]

    def at_least(eng, name, value):
        if not (isinstance(value, int) and value <= 0):
            eng.wait_ge(s[name] if isinstance(name, str) else name, value)

    def turns(eng, body):
        body(0, True, False)
        with eng.Fori(1, NP - 1) as i:
            body(i, False, False)
        body(NP - 1, False, True)

    wraw = [w[0][:, 0].rearrange("p a b c d -> p (a b c d)")[:, P * n:P * n + P] for n in range(4)]
    wg_raw = w[0][:, 1].rearrange("p a b c d -> p (a b c d)")
    wr_raw = wg_raw[0:E, 6 * P:7 * P]
    gu_raw = [wg_raw[:, P * n:P * n + P] for n in range(6)]
    rkT = w[1][0:HD, 0].rearrange("p a b c d -> p (a b c d)")[:, 0:2 * M + 1]
    rpad = w[1][0:HD, 0].rearrange("p a b c d -> p (a b c d)")[:, 512:1024]
    rzero = w[1][0:HD, 0].rearrange("p a b c d -> p (a b c d)")[:, 1024:1024 + P]
    rpart = [qs[0][0:HD, 0, :], qs[0][0:HD, 1, :]]
    sq = w[1][:, 1].rearrange("p a b c d -> p (a b c d)")
    bnd = sq[:, 256:264]
    bmax = sq[:, 264:272]
    pw = sq[:, 272:280]
    bkr = sq[:, 280:284]
    bqr = sq[:, 284:285]
    vraw = sq[:, 512:1024].rearrange("p (a b) -> p a b", b=P)[:, 0:3]

    LOADS = 4 + 6 + 1 + 1 + 4 + 4

    block = ctx.enter_context(nc.Block())

    @block.sync
    def _(sp):
        ld = s["w_ld"]
        for n, W in enumerate((Wq, Wk, Wv, Wo)):
            sp.dma_start(wraw[n], W).then_inc(ld, 16)
        for n in range(2):
            sp.dma_start(gu_raw[n], w_gate[P * n:P * n + P]).then_inc(ld, 16)
            sp.dma_start(gu_raw[2 + n], w_up[P * n:P * n + P]).then_inc(ld, 16)
            sp.dma_start(gu_raw[4 + n], w_down[:, P * n:P * n + P]).then_inc(ld, 16)
        sp.dma_start(wr_raw, w_router).then_inc(ld, 16)
        with nc.allow_non_contiguous_dma(reason="small tables, once"):
            sp.dma_start(rkT, rel_k.rearrange("r d -> d r")).then_inc(ld, 16)
            sp.dma_start(bqr, bq.rearrange("(p o) -> p o", o=1)).then_inc(ld, 16)
            sp.dma_start(bkr[:, 0:1], bk.rearrange("(p o) -> p o", o=1)).then_inc(ld, 16)
            for n, r in ((1, 0), (2, 2 * M)):
                src = rel_k[r:r + 1, :]
                sp.dma_start(bkr[:, n:n + 1], bass.AP(src.tensor, src.offset, [[0, H], [1, HD], [1, 1]])).then_inc(ld, 16)
            sp.dma_start(vraw[:, 0, :], bass.AP(bv.tensor, bv.offset, [[0, P], [1, P]])).then_inc(ld, 16)
            sp.dma_start(bo_s[:], bass.AP(bo.tensor, bo.offset, [[0, P], [1, P]])).then_inc(ld, 16)
            for n, r in ((1, 0), (2, 2 * M)):
                src = rel_v[r:r + 1, :]
                sp.dma_start(vraw[:, n, :].rearrange("p (h d) -> p h d", d=HD),
                             bass.AP(src.tensor, src.offset, [[0, P], [0, H], [1, HD]])).then_inc(ld, 16)
            tab = s["tab"]
            sp.dma_start(rvp_d[127:127 + 2 * M + 1], rel_v).then_inc(tab, 16)
            sp.dma_start(rvp_d[0:127], bass.AP(rel_v.tensor, rel_v.offset, [[0, 127], [1, HD]])).then_inc(tab, 16)
            sp.dma_start(rvp_d[384:512], bass.AP(rel_v.tensor, rel_v.offset + 2 * M * HD, [[0, 128], [1, HD]])).then_inc(tab, 16)
        sp.wait_ge(tab, 48)
        for m in range(Z_W // 32):
            sp.dma_start(Rv[:, :, m, :], bass.AP(rvp_d.tensor, rvp_d.offset + 32 * m * HD,
                                                 [[HD, P], [HD, 32], [1, HD]])).then_inc(s["sp_set"], 16)
        sp.wait_ge(s["dve_set"], RPART_READY)
        for u in range(NU):
            for t, (_, kp) in enumerate(TERMS):
                r = (u * 3 + t) * HD
                c = OFF0 - WT_0 - 32 * u
                sp.dma_start(Wt[r:r + HD, 0:WT_W], rpart[kp][:, c:c + WT_W]).then_inc(s["sp_set"], 16)
        for half in range(2):
            for e in range(NE8):
                c = OFF0 - WN_0 - 16 * e
                sp.dma_start(Wn[64 * half + HD * e:64 * half + HD * e + HD, 0:WN_W], rpart[0][:, c:c + WN_W]).then_inc(s["sp_set"], 16)
        sp.wait_ge(s["zeroed"], ZEROED)
        zsrc = Qn[:].rearrange("p e h k -> p (e h k)").bitcast(F32)
        rows = xs_d.rearrange("(a p) n -> p a n", p=P)
        step = 16
        for c in range(0, SORTED, step):
            sp.dma_start(rows[:, c:c + step], zsrc[:, 0:step * 2 * D].rearrange("p (a n) -> p a n", a=step)).then_inc(s["z_st"], 16)
        sp.wait_ge(s["z_st"], 16 * (SORTED // step))

        def load_x(n, b2):
            at_least(sp, "xn_done", 2 * n + b2 - 1)
            sp.dma_start(xt[b2][:], x[bass.ds(2 * n + b2, 1)].rearrange("o (t p) d -> p (o t) d", p=P)).then_inc(x_ld[b2], 16)

        def store_q(n, b2):
            c = 2 * n + b2
            sp.wait_ge(s["qsplit"], 2 * c + 2)
            sp.dma_start(qs_d[bass.ds(c * P, P)], qs[b2][:]).then_inc(s["qs_st"], 16)
            sp.wait_ge(s["qs_st"], 16 * (c + 1))
            sp.sem_inc(s["sp_passed"], 1)
            at_least(sp, "nat_ps", 64 * (c - 1))
            src = qs_d[bass.ds(c * P, P)].rearrange("(h d) a q -> d h a q", d=HD)
            for e in range(NE8):
                for t in range(NT):
                    r = 64 * b2 + HD * e
                    sp.dma_start(Qn[r:r + HD, e, :, 16 * t:16 * t + 16],
                                 src[:, :, 0, P * t + 16 * e:P * t + 16 * e + 16]).then_inc(qn_ld[b2], 16)

        def store_kv(n, b2):
            c = 2 * n + b2
            sp.wait_ge(s["ksplit"], 2 * c + 2)
            sp.dma_start(ks_d[bass.ds(c * P, P)], ks[:]).then_inc(s["ks_st"], 16)
            sp.wait_ge(s["v_ev"], c + 1)
            sp.dma_start(vs_d[bass.ds(c, 1)].rearrange("o p t n -> p (o t) n"),
                         vst[:].rearrange("p t v h n -> p t (v h n)")).then_inc(s["vs_st"], 16)

        def store_max(n, b2):
            c = 2 * n + b2
            sp.wait_ge(s["ms_done"], c + 1)
            dst = ms_d[bass.ds(c * H, H)].rearrange("h a (t e b) -> e h a t b", t=NT, e=NE8)
            for part in range(2):
                for t in range(NT):
                    sp.dma_start(dst[:, :, part, t], ms[:, part, 16 * t:16 * t + 16]).then_inc(s["ms_st"], 16)

        def load_q(n, t):
            r = t % 2
            at_least(sp, "s_done", n * SLOTS + 32 * (t - 1))
            sp.sem_inc(s["sp_passed"], 1)
            if t == 0:
                sp.wait_ge(s["ms_st"], MS_STORES * (2 * n + 2))
            src = qs_d[bass.ds(2 * n * P, 2 * P)]
            heads4 = src.rearrange("(g hh d) a q -> d hh g a q", hh=4, d=HD)
            for hh in range(4):
                for tm, (qp, _) in enumerate(TERMS):
                    row = (hh * 3 + tm) * HD
                    sp.dma_start(QC[r][row:row + HD, :, :, hh, :].rearrange("d b g q -> d (b g) q"),
                                 heads4[:, hh, :, qp, P * t:P * t + P]).then_inc(qc_ld[r], 16)
            heads = src.rearrange("(bh d) a q -> d bh a q", d=HD)
            for u in range(NU):
                for tm, (qp, _) in enumerate(TERMS):
                    row = (u * 3 + tm) * HD
                    sp.dma_start(QT[r][row:row + HD, u].rearrange("d b h q -> d (b h) q"),
                                 heads[:, :, qp, P * t + 32 * u:P * t + 32 * u + 32]).then_inc(qc_ld[r], 16)
            mrow = ms_d[bass.ds(2 * n * H, 2 * H)].rearrange("(g hh) a q -> hh a g q", hh=4)
            for hh in range(4):
                for part in range(2):
                    row = 4 * 3 * HD + 2 * hh + part
                    sp.dma_start(QC[r][row:row + 1, :, :, hh, :].rearrange("o b g q -> o (b g) q"),
                                 mrow[hh:hh + 1, part, :, P * t:P * t + P]).then_inc(qc_ld[r], 16)

        def load_kv(n, j):
            at_least(sp, "s_done", (n - 1) * SLOTS + 96 + 8 * (j + 1))
            at_least(sp, "pv_done", (n - 1) * SLOTS + 96 + 8 * (j + 1))
            sp.sem_inc(s["sp_passed"], 1)
            sp.wait_ge(s["ks_st"], 32 * n + 32)
            sp.wait_ge(s["vs_st"], 32 * n + 32)
            src = ks_d[bass.ds(2 * n * P, 2 * P)].rearrange("(g hh d) t a v k -> d hh g t a (v k)", hh=4, d=HD)
            for hh in range(4):
                for tm, (_, kp) in enumerate(TERMS):
                    row = (hh * 3 + tm) * HD
                    sp.dma_start(KC[j][row:row + HD].rearrange("d b g v k -> d (b g) (v k)"), src[:, hh, :, j, kp, :]).then_inc(kc_ld[j], 16)
            for b2 in range(2):
                sp.dma_start(VC[j][:, b2].rearrange("p v h n -> p (v h n)"),
                             vs_d[bass.ds(2 * n + b2, 1), :, j, :].rearrange("o p n -> (o p) n")).then_inc(kc_ld[j], 16)

        def store_o(n, t):
            sp.wait_ge(s["pv_ev"], 4 * n + t + 1)
            rows2 = opv_d[bass.ds(2 * n * P, 2 * P)].rearrange("(b g hh d) q -> b g d hh q", b=2, g=4, hh=4)
            sums2 = os_d[bass.ds(2 * n * H, 2 * H)].rearrange("(b g hh) q -> b g hh q", b=2, g=4)
            for b2 in range(2):
                for g in range(4):
                    sp.dma_start(rows2[b2, g, :, :, P * t:P * t + P], pv_s[32 * g:32 * g + HD, b2]).then_inc(s["o_st"], 16)
                    sp.dma_start(sums2[b2, g:g + 1, :, P * t:P * t + P], pv_s[32 * g + HD:32 * g + HD + 1, b2]).then_inc(s["o_st"], 16)
            sp.wait_ge(s["rel_ev"], 4 * n + t + 1)
            dst = orl_d[bass.ds(2 * n * P, 2 * P)].rearrange("(bh d) q -> d bh q", d=HD)
            for sb_ in range(NS):
                for u in range(NU):
                    row = 32 * sb_ + HD * (NU - 1 - u)
                    q0 = P * t + 32 * u + NB * sb_
                    sp.dma_start(dst[:, :, q0:q0 + NB], rel_s[row:row + HD, :, u, :]).then_inc(s["o_st"], 16)

        def load_o(n, b2):
            c = 2 * n + b2
            if b2 == 0:
                sp.wait_ge(s["o_st"], O_STORES * NT * (n + 1))
                sp.sem_inc(s["sp_passed"], 1)
            at_least(sp, "op_ps", c)
            at_least(sp, "x1_done", c)
            sp.sem_inc(s["sp_passed"], 1)
            sp.dma_start(oA[:], opv_d[bass.ds(c * P, P)]).then_inc(s["o_ld"], 16)
            sp.dma_start(oB[:], orl_d[bass.ds(c * P, P)]).then_inc(s["o_ld"], 16)
            for d in range(1):
                src = os_d[bass.ds(c * H, H)]
                src = src.rearrange("h (o q) -> h o q", o=1).broadcast_to([H, HD, S])
                sp.dma_start(oS[:], src).then_inc(s["o_ld"], 16)
            sp.dma_start(xr[:], x[bass.ds(c, 1)].rearrange("o (t p) d -> p (o t) d", p=P)).then_inc(s["o_ld"], 16)

        def store_x1(n, b2):
            c = 2 * n + b2
            sp.wait_ge(s["x1_done"], c + 1)
            sp.dma_start(x1_d[bass.ds(c * S, S)].rearrange("(t p) d -> p t d", p=P), x1[:]).then_inc(s["x1_st"], 16)

        def store_xs(n, b2):
            c = 2 * n + b2
            sp.wait_ge(s["xs_done"], c + 1)
            sp.dma_start(xn_d[bass.ds(c * S, S)].rearrange("(t p) d -> p t d", p=P), xs[:]).then_inc(s["xs_st"], 16)
            sp.dma_start(oh_d[bass.ds(c, 1)].rearrange("o p n -> p (o n)"), oh[:].rearrange("p t e -> p (t e)")).then_inc(s["xs_st"], 16)

        def finish(n, first_slot):
            return {first_slot: lambda: load_o(n, 0), first_slot + 11: lambda: store_x1(n, 0), first_slot + 18: lambda: (store_xs(n, 0), load_o(n, 1)),
                    first_slot + 29: lambda: store_x1(n, 1), first_slot + 36: lambda: store_xs(n, 1)}

        def turn(i, first, last):
            for slot in range(SLOTS):
                if slot == 1:
                    load_q(i, 1)
                if slot in (33, 65):
                    load_q(i, slot // 32 + 1)
                if slot == 1:
                    load_kv(i, 2)
                if slot == 9:
                    load_kv(i, 3)
                if slot % 32 == 10 and not (first and slot < 32):
                    t = slot // 32 - 1
                    store_o(i, t) if t >= 0 else store_o(i - 1, NT - 1)
                if not last:
                    if slot == 0:
                        load_x(i + 1, 0)
                        load_x(i + 1, 1)
                    if slot in (11, 19):
                        store_q(i + 1, slot == 19)
                    if slot in (14, 22):
                        store_kv(i + 1, int(slot == 22))
                    if slot in (75, 121):
                        store_max(i + 1, int(slot == 121))
                    if slot == 122:
                        load_q(i + 1, 0)
                    if slot == 113:
                        load_kv(i + 1, 0)
                    if slot == 124:
                        load_kv(i + 1, 1)
                if not first:
                    step = finish(i - 1, 24).get(slot)
                    if step:
                        step()

        load_x(0, 0)
        load_x(0, 1)
        for b2 in range(2):
            store_q(0, b2)
            store_kv(0, b2)
        for b2 in range(2):
            store_max(0, b2)
        load_q(0, 0)
        load_kv(0, 0)
        load_kv(0, 1)
        turns(sp, turn)
        store_o(NP - 1, NT - 1)
        for slot in range(64):
            step = finish(NP - 1, 0).get(slot)
            if step:
                step()
        sp.wait_ge(s["x1_st"], 16 * B)
        sp.wait_ge(s["xs_st"], 32 * B)

    @block.tensor
    def _(pe):
        def transpose(out_, in_):
            k = in_.shape[0]
            return nc.tensor.transpose(out_, in_, ident[0:k, 0:k])

        pe.wait_ge(s["pool_set"], IDENT_READY)
        pe.wait_ge(s["w_ld"], 16 * LOADS)
        pe.wait_ge(s["dve_set"], SCALED)
        for n in range(4):
            mm = transpose(sc[0][:, P * n:P * n + P], wraw[n])
        for n in range(4):
            mm = transpose(sc[1][:, P * n:P * n + P], gu_raw[n])
        for n in range(2):
            mm = transpose(nat[:, P * n:P * n + P], gu_raw[4 + n])
        mm = transpose(misc[:, 0:E], wr_raw)
        mm.then_inc(s["pe_set"], 1)
        pe.wait_ge(s["act_set"], 1)
        pe.wait_ge(s["sp_set"], 16 * (Z_W // 32 + NU * 3 + 2 * NE8))
        pe.wait_ge(s["zeroed"], ZEROED)
        pe.wait_ge(s["dve_set"], DVE_SET_DONE)

        def prep(n, b2, step):
            c = 2 * n + b2
            if step == 0:
                pe.wait_ge(s["xn_done"], c + 1)
                at_least(pe, "v_ev", c)
                for t in range(NT):
                    mm = transpose(misc[:, P * t:P * t + P], xn[:, t, :])
                mm.then_inc(s["xT_ps"], 1)
            elif step == 1:
                pe.wait_ge(s["xnT_rdy"], c + 1)
                nc.tensor.matmul(misc[:], wqT[:], xnT[:], start=True, stop=True).then_inc(s["q_ps"], 1)
            elif step == 2:
                pe.wait_ge(s["q_ev"], c + 1)
                nc.tensor.matmul(misc[:], wkT[:], xnT[:], start=True, stop=True).then_inc(s["k_ps"], 1)
            else:
                pe.wait_ge(s["k_ev"], c + 1)
                for t in range(NT):
                    mm = nc.tensor.matmul(misc[:, P * t:P * t + P], xnT[:, P * t:P * t + P], wvT[:], start=True, stop=True)
                mm.then_inc(s["v_ps"], 1)

        def natural(n, b2, k):
            c = 2 * n + b2
            if k == 0:
                pe.wait_ge(qn_ld[b2], QN_LOADS * (n + 1))
            if k % 32 == 0:
                pe.wait_ge(s["qb_done"], 2 * c + k // 32 + 1)
            at_least(pe, "mx_done", 64 * c + k)
            t, b = k // 16, k % 16
            lo = max(0, P * t + b - (M - 1))
            hi = min(S, P * t + b + 16 * (NE8 - 1) + M)
            lq = Qb[t // 2][:, :, :, 16 * (t % 2) + b].rearrange("p e h -> p (e h)")
            le = Qn[64 * b2:64 * b2 + 64, :, :, k].rearrange("p e h -> p (e h)")
            x0 = WN_0 - P * t - b
            nc.tensor.matmul(nat[:, lo:hi], lq, kn[b2][:, 0, lo:hi], start=True, stop=False, skip_group_check=True)
            mm = nc.tensor.matmul(nat[:, lo:hi], le, Wn[64 * b2:64 * b2 + 64, x0 + lo:x0 + hi], start=False, stop=True, skip_group_check=True)
            if lo > 0:
                mm = nc.tensor.matmul(nat[:, 0:lo], lq, kn[b2][:, 1, 0:lo], start=False, stop=True, skip_group_check=True)
            if hi < S:
                mm = nc.tensor.matmul(nat[:, hi:S], lq, kn[b2][:, 2, hi:S], start=False, stop=True, skip_group_check=True)
            mm.then_inc(s["nat_ps"], 1)

        def scores(i, slot):
            t, j, b2, q8 = slot // 32, slot // 8 % 4, slot // 4 % 2, slot % 4
            if slot % 32 == 0:
                pe.wait_ge(qc_ld[t % 2], QC_LOADS * (2 * i + t // 2 + 1))
            if t == 0 and slot % 8 == 0:
                pe.wait_ge(kc_ld[j], KC_LOADS * (i + 1))
            at_least(pe, "exp_done", SLOTS * i + slot - 1)
            near = abs(t - j) <= 1
            bank = sc[slot % 2]
            qc = QC[t % 2][:, b2].rearrange("p g h (u s b) -> p g h u s b", u=NU, s=NS)
            for g in range(4):
                mm = nc.tensor.matmul(bank[:, P * g:P * g + P], KC[j][:, b2, g, 0 if near else 1, :], qc[:, g, :, :, q8, :],
                                      start=(g == 0), stop=not near, skip_group_check=True)
            if near:
                view = bank[:].rearrange("p (h u b) -> p h u b", h=H, u=NU)
                qt = QT[t % 2][:, :, b2].rearrange("p u h q -> p h u q")
                for b in range(NB):
                    x0 = WT_0 + P * (j - t) - NB * q8 - b
                    mm = nc.tensor.matmul(view[:, :, :, b], Wt[:, x0:x0 + P], qt[:, :, :, NB * q8 + b], start=False, stop=(b == NB - 1), skip_group_check=True)
            mm.then_inc(s["s_done"], 1)

        def values(i, tile, k):
            t, j = tile // 4, tile % 4
            near = abs(t - j) <= 1
            wt = w[tile % 2]
            if k == 0:
                pe.wait_ge(s["exp_done"], SLOTS * i + 8 * (tile + 1))
                if j == 0:
                    at_least(pe, "pv_ev", 4 * i + t)
                if j == max(0, t - 1):
                    at_least(pe, "rel_ev", 4 * i + t)
            b2, hh = k // 4, k % 4
            for g in range(4):
                h = 4 * g + hh
                mm = nc.tensor.matmul(pv[b2][32 * g:32 * g + 9, P * hh:P * hh + P], VC[j][:, b2, 0 if near else 1, h, :],
                                      wt[:, b2, :, h].rearrange("p s u b -> p u s b"),
                                      start=(j == 0 and hh == 0), stop=(j == NT - 1), skip_group_check=True)
            if near:
                for q8 in range(NS):
                    z0 = Z_0 + P * (j - t) - NB * q8 - k - 32 * (NU - 1)
                    lv = Rv[:, z0 % 32, z0 // 32:z0 // 32 + NU, :].rearrange("p u d -> p (u d)")
                    mm = nc.tensor.matmul(rel[k // 4][32 * q8:32 * q8 + 32, P * (k % 4):P * (k % 4) + P], lv,
                                          wt[:, :, q8, :, :, k], start=(j == max(0, t - 1) and k % 4 == 0),
                                          stop=(j == min(NT - 1, t + 1)), skip_group_check=True)
            mm.then_inc(s["pv_done"], 1)

        def finish(n, b2, step, misc_free):
            c = 2 * n + b2
            if step == 0:
                pe.wait_ge(s["O_rdy"], c + 1)
                misc_free()
                for t in range(NT):
                    mm = nc.tensor.matmul(misc[:, P * t:P * t + P], oA[:, P * t:P * t + P], woT[:], start=True, stop=True)
                mm.then_inc(s["op_ps"], 1)
            elif step == 1:
                pe.wait_ge(s["xn2_done"], c + 1)
                for t in range(NT):
                    mm = transpose(misc[:, P * t:P * t + P], xs[:, t, 0:D])
                mm.then_inc(s["x2T_ps"], 1)
            else:
                pe.wait_ge(s["x2T_ev"], c + 1)
                for t in range(NT):
                    mm = nc.tensor.matmul(misc[:, E * t:E * t + E], x2T[:, P * t:P * t + P], wrT[:], start=True, stop=True)
                mm.then_inc(s["lg_ps"], 1)

        prep_at = {6: (0, 0), 8: (0, 1), 10: (0, 2), 12: (0, 3), 14: (1, 0), 16: (1, 1), 18: (1, 2), 20: (1, 3)}
        finish_at = {30: (0, 0), 35: (0, 1), 39: (0, 2), 48: (1, 0), 53: (1, 1), 57: (1, 2)}

        def turn(i, first, last):
            done = 0
            for slot in range(SLOTS):
                scores(i, slot)
                if not last:
                    if slot in prep_at:
                        b2, step = prep_at[slot]
                        if (b2, step) == (0, 0) and not first:
                            pe.wait_ge(s["lg_ev"], 2 * (i - 1))
                        prep(i + 1, b2, step)
                    while done < min(128, max(0, (slot - 23) * 4 // 3)):
                        natural(i + 1, done // 64, done % 64)
                        done += 1
                if slot >= 8:
                    values(i, slot // 8 - 1, slot % 8)
                elif not first:
                    values(i - 1, 15, slot)
                if not first and slot in finish_at:
                    b2, step = finish_at[slot]

                    def misc_free():
                        if b2 == 0 and not last:
                            pe.wait_ge(s["v_ev"], 2 * (i + 2))
                        else:
                            at_least(pe, "lg_ev", 2 * (i - 1) + b2)
                    finish(i - 1, b2, step, misc_free)

        for b2 in range(2):
            for step in range(4):
                prep(0, b2, step)
        for k in range(128):
            natural(0, k // 64, k % 64)
        turns(pe, turn)
        for k in range(8):
            values(NP - 1, 15, k)
        for b2 in range(2):
            for step in range(3):
                finish(NP - 1, b2, step, lambda: pe.wait_ge(s["lg_ev"], 2 * (NP - 1) + b2))

    @block.scalar
    def _(act):
        act.wait_ge(s["pe_set"], 1)
        for dst, src in ((wqT, sc[0][:, 0:P]), (wkT, sc[0][:, P:2 * P]), (wvT, sc[0][:, 2 * P:3 * P]), (woT, sc[0][:, 3 * P:4 * P]),
                         (sgu, sc[1][:]), (sdn, nat[:, 0:2 * P]), (wrT, misc[:, 0:E])):
            view = dst[:].rearrange("p a b -> p (a b)") if len(dst.shape) == 3 else dst[:]
            last_copy = nc.scalar.copy(view, src)
        last_copy.then_inc(s["act_set"], 1)
        act.wait_ge(s["dve_set"], DVE_SET_DONE)

        def prep(n, b2, step):
            c = 2 * n + b2
            if step == 0:
                act.wait_ge(s["xT_ps"], c + 1)
                at_least(act, "v_ps", c)
                nc.scalar.copy(xnT[:], misc[:]).then_inc(s["xnT_rdy"], 1)
            elif step == 1:
                act.wait_ge(s["q_ps"], c + 1)
                at_least(act, "qsplit", 2 * c)
                nc.scalar.activation(qf[:], misc[:], ACT.Identity, bias=bq_s[:, 0:1]).then_inc(s["q_ev"], 1)
            else:
                act.wait_ge(s["k_ps"], c + 1)
                at_least(act, "nat_ps", 64 * (c - 1))
                at_least(act, "ksplit", 2 * c)
                for v in range(3):
                    nc.scalar.activation(kn[b2][:, v, :], misc[:], ACT.Identity, bias=kb[:, v:v + 1])
                nc.scalar.activation(kf[:, 0, :], misc[:], ACT.Identity, bias=kb[:, 0:1])
                nc.scalar.activation(kf[:, 1, 0:S // 2], misc[:, 0:S // 2], ACT.Identity, bias=kb[:, 1:2])
                nc.scalar.activation(kf[:, 1, S // 2:S], misc[:, S // 2:S], ACT.Identity, bias=kb[:, 2:3]).then_inc(s["k_ev"], 1)

        def by_head(n, b2, half, heads):
            c = 2 * n + b2
            if heads[0] == 0:
                act.wait_ge(s["qsplit"], 2 * c + 1)
                at_least(act, "nat_ps", 64 * (c - 1) + 32 * (half + 1))
            src = qs[b2][:, 0, S // 2 * half:S // 2 * (half + 1)].rearrange("p (t e b) -> p e t b", t=2, e=NE8)
            for h in heads:
                ins = nc.scalar.activation(Qb[half][:, :, h, :].rearrange("p e (t b) -> p e t b", t=2), src, ACT.Copy, scale=hmask[:, h:h + 1])
            if heads[-1] == H - 1:
                ins.then_inc(s["qb_done"], 1)

        def exponentials(i, slot):
            tile = slot // 8
            act.wait_ge(s["s_done"], SLOTS * i + slot + 1)
            if slot % 8 == 0:
                at_least(act, "pv_done", SLOTS * i + 8 * (tile - 1))
            nc.scalar.activation(w[tile % 2][:, slot // 4 % 2, slot % 4].rearrange("p h u b -> p (h u b)"), sc[slot % 2][:], ACT.Exp,
                                 scale=escale[:, 0:1]).then_inc(s["exp_done"], 1)

        def outputs(n, t):
            act.wait_ge(s["pv_done"], SLOTS * n + 32 * (t + 1))
            at_least(act, "o_st", O_STORES * (NT * n + t))
            nc.scalar.copy(pv_s[:, 0].rearrange("p h q -> p (h q)"), pv[0][:])
            nc.scalar.copy(pv_s[:, 1].rearrange("p h q -> p (h q)"), pv[1][:]).then_inc(s["pv_ev"], 1)

        def finish(n, b2, step):
            c = 2 * n + b2
            if step == 0:
                act.wait_ge(s["x2T_ps"], c + 1)
                at_least(act, "lg_ps", c)
                nc.scalar.copy(x2T[:], misc[:]).then_inc(s["x2T_ev"], 1)
            else:
                act.wait_ge(s["lg_ev"], c + 1)
                nc.scalar.activation(sg[:], lmax[:], ACT.Exp, scale=-1.0).then_inc(s["sg_done"], 1)

        prep_at = {6: (0, 0), 8: (0, 1), 10: (0, 2), 14: (1, 0), 16: (1, 1), 18: (1, 2)}
        by_head_at = {12: (0, 0), 24: (0, 1), 52: (1, 0), 75: (1, 1)}
        finish_at = {36: (0, 0), 42: (0, 1), 54: (1, 0), 60: (1, 1)}

        def turn(i, first, last):
            for slot in range(SLOTS):
                exponentials(i, slot)
                if slot % 32 == 7:
                    if slot > 32:
                        outputs(i, slot // 32 - 1)
                    elif not first:
                        outputs(i - 1, NT - 1)
                if not last and slot in prep_at:
                    prep(i + 1, *prep_at[slot])
                for start, (b2, half) in by_head_at.items():
                    if not last and 0 <= slot - start < H // 2:
                        by_head(i + 1, b2, half, (2 * (slot - start), 2 * (slot - start) + 1))
                if not first and slot in finish_at:
                    finish(i - 1, *finish_at[slot])

        for b2 in range(2):
            for step in range(3):
                prep(0, b2, step)
        for b2 in range(2):
            for half in range(2):
                by_head(0, b2, half, range(H))
        turns(act, turn)
        outputs(NP - 1, NT - 1)
        for b2 in range(2):
            for step in range(2):
                finish(NP - 1, b2, step)

    @block.vector
    def _(dve):
        count = [0]

        def link(ins):
            count[0] += 1
            ins.then_inc(s["dve_set"], 1)
            dve.wait_ge(s["dve_set"], count[0])

        dve.wait_ge(s["w_ld"], 16 * LOADS)
        link(nc.vector.memset(bnd[:], 0.0))
        for n, bias in ((0, bqr), (1, bkr[:, 0:1])):
            link(nc.vector.tensor_reduce(bnd[:, 4:5], wraw[n], AX.X, ALU.add, apply_absolute_value=True))
            link(nc.vector.tensor_reduce(bnd[:, 5:6], bias, AX.X, ALU.max, apply_absolute_value=True))
            link(nc.vector.scalar_tensor_tensor(out=bnd[:, n:n + 1], in0=bnd[:, 4:5], scalar=XMAX, in1=bnd[:, 5:6],
                                                op0=ALU.mult, op1=ALU.add))
        link(nc.vector.tensor_reduce(bnd[0:HD, 2:3], rkT, AX.X, ALU.max, apply_absolute_value=True))
        assert count[0] == BOUNDS
        dve.wait_ge(s["pool_set"], BOUNDS_MAX)
        link(nc.vector.tensor_copy(bnd[:, 4:5], bmax[:, 0:1]))
        link(nc.vector.tensor_tensor(bnd[:, 5:6], bmax[:, 1:2], bmax[:, 2:3], ALU.add))
        link(nc.vector.tensor_scalar(bnd[:, 6:8], bnd[:, 4:6], 2.0 ** -100, 2.0 ** 100, ALU.max, ALU.min))
        link(nc.vector.tensor_scalar(pw[:, 0:2].bitcast(I32), bnd[:, 6:8].bitcast(I32), 0x7F800000, None, ALU.bitwise_and))
        link(nc.vector.tensor_scalar(pw[:, 2:4].bitcast(I32), pw[:, 0:2].bitcast(I32), -1.0, float(266 << 23), ALU.mult, ALU.add))
        link(nc.vector.tensor_scalar(wraw[0], wraw[0], pw[:, 2:3], None, ALU.mult))
        link(nc.vector.tensor_scalar(wraw[1], wraw[1], pw[:, 3:4], None, ALU.mult))
        assert count[0] == SCALED
        link(nc.vector.tensor_scalar(rkT, rkT, pw[0:HD, 3:4], None, ALU.mult))
        link(nc.vector.memset(rzero, 0.0))
        link(nc.vector.tensor_scalar(rpad[:, 0:OFF0 - M], rzero[:, 0:OFF0 - M], rkT[:, 0:1], None, ALU.add))
        link(nc.vector.tensor_copy(rpad[:, OFF0 - M:OFF0 + M + 1], rkT))
        link(nc.vector.tensor_scalar(rpad[:, OFF0 + M + 1:512], rzero[:, 0:512 - OFF0 - M - 1], rkT[:, 2 * M:2 * M + 1], None, ALU.add))
        link(nc.vector.tensor_copy(rpart[0], rpad))
        link(nc.vector.tensor_tensor(rpart[1], rpad, rpart[0], ALU.subtract))
        assert count[0] == RPART_READY
        link(nc.vector.tensor_scalar(bq_s[:], bqr, pw[:, 2:3], None, ALU.mult))
        link(nc.vector.tensor_scalar(kb[:, 0:1], bkr[:, 0:1], pw[:, 3:4], None, ALU.mult))
        for n in (1, 2):
            link(nc.vector.tensor_scalar(bnd[:, n:n + 1], bkr[:, n:n + 1], pw[:, 3:4], None, ALU.mult))
            link(nc.vector.tensor_tensor(kb[:, n:n + 1], kb[:, 0:1], bnd[:, n:n + 1], ALU.add))
        link(nc.vector.tensor_tensor(bnd[:, 3:4], pw[:, 2:3], pw[:, 3:4], ALU.mult))
        link(nc.vector.reciprocal(bnd[:, 4:5], bnd[:, 3:4]))
        link(nc.vector.tensor_scalar(escale[:], bnd[:, 4:5], HD ** -0.5, None, ALU.mult))
        link(nc.vector.tensor_copy(vb[:, 0, :], vraw[:, 0, :]))
        for n in (1, 2):
            link(nc.vector.tensor_tensor(vb[:, n, :], vraw[:, 0, :], vraw[:, n, :], ALU.add))
        for bank in (*pv, *rel):
            link(nc.vector.memset(bank[:], 0.0))
        assert count[0] == DVE_SET_DONE

        def layernorm(src, stats, mean_var, ve, rs, write, base, step, root, roots):
            for t in range(NT):
                ins = nc.vector.bn_stats(stats[:, t, :], src[:, t, :])
            ins.then_inc(s[step], 1)
            dve.wait_ge(s[step], base + 1)
            dve.sem_inc(s["dve_passed"], 1)
            for t in range(NT):
                ins = nc.vector.bn_aggr(mean_var[:, t, :], stats[:, t, :])
            ins.then_inc(s[step], 1)
            dve.wait_ge(s[step], base + 2)
            root_guess(nc, dve, s[step], base + 2, mean_var, ve, rs)
            dve.wait_ge(s[root], ROOT_STEPS * (roots + 1))
            for t in range(NT):
                ins = write(t, mean_var[:, t, 0:1], rs[:, t:t + 1])
            return ins

        def prep(n, b2, step):
            c = 2 * n + b2
            if step == 0:
                dve.wait_ge(x_ld[b2], 16 * (n + 1))
                at_least(dve, "xT_ps", c)
                layernorm(xt[b2], st, mv, var, rstd,
                          lambda t, m, r: nc.vector.tensor_scalar(xn[:, t, :], xt[b2][:, t, :], m, r, ALU.subtract, ALU.mult),
                          5 * c, "xn_step", "root", c).then_inc(s["xn_done"], 1)
            else:
                dve.wait_ge(s["v_ps"], c + 1)
                at_least(dve, "vs_st", 16 * c)
                src = misc[:].rearrange("p (t h d) -> p t h d", t=NT, h=H)
                for v, tiles, far in ((0, slice(0, NT), 0), (1, slice(0, 2), 1), (2, slice(2, NT), 1)):
                    nt = tiles.stop - tiles.start
                    bias = vb[:, v:v + 1, :].rearrange("p o (h d) -> p o h d", d=HD).broadcast_to([P, nt, H, HD])
                    ins = nc.vector.tensor_tensor(vst[:, tiles, far, :, 0:HD], src[:, tiles], bias, ALU.add)
                ins.then_inc(s["v_ev"], 1)

        def row_max(n, b2, k):
            c = 2 * n + b2
            if k == 0:
                at_least(dve, "ms_done", c)
            dve.wait_ge(s["nat_ps"], 64 * c + k + 1)
            nc.vector.tensor_reduce(mx[:, k:k + 1], nat[:], AX.X, ALU.max).then_inc(s["mx_done"], 1)
            if k == 63:
                dve.wait_ge(s["mx_done"], 64 * (c + 1))
                at_least(dve, "ms_st", MS_STORES * c)
                nc.vector.tensor_scalar(ms[:, 0, :], mx[:], MAXSCALE, None, ALU.mult).then_inc(s["ms_step"], 1)
                dve.wait_ge(s["ms_step"], c + 1)
                nc.vector.scalar_tensor_tensor(out=ms[:, 1, :], in0=mx[:], scalar=MAXSCALE, in1=ms[:, 0, :],
                                               op0=ALU.mult, op1=ALU.subtract).then_inc(s["ms_done"], 1)

        def outputs(n, t):
            dve.wait_ge(s["pv_done"], SLOTS * n + 32 * (t + 1))
            at_least(dve, "o_st", O_STORES * (NT * n + t))
            for half in range(2):
                ins = nc.vector.tensor_copy(rel_s[:, :, :, 4 * half:4 * half + 4].rearrange("p h u b -> p (h u) b"),
                                            rel[half][:].rearrange("p (b c) -> p c b", b=4))
            ins.then_inc(s["rel_ev"], 1)

        def finish(n, b2, step):
            c = 2 * n + b2
            if step == 0:
                dve.wait_ge(s["o_ld"], 64 * (c + 1))
                nc.vector.tensor_tensor(oA[:], oA[:], oB[:], ALU.add).then_inc(s["o_step"], 1)
                nc.vector.reciprocal(oS[:], oS[:]).then_inc(s["o_step"], 1)
                dve.wait_ge(s["o_step"], 2 * c + 2)
                nc.vector.tensor_tensor(oA[:], oA[:], oS[:], ALU.mult).then_inc(s["O_rdy"], 1)
            elif step == 1:
                dve.wait_ge(s["op_ps"], c + 1)
                base = 12 * c
                nc.vector.tensor_tensor(y[:], misc[:].rearrange("p (t d) -> p t d", t=NT),
                                        bo_s[:].rearrange("p (o d) -> p o d", o=1).broadcast_to([P, NT, D]), ALU.add).then_inc(s["ln_step"], 1)
                dve.wait_ge(s["ln_step"], base + 1)
                layernorm(y, st2, mv2, var2, rstd2,
                          lambda t, m, r: nc.vector.tensor_scalar(y[:, t, :], y[:, t, :], m, r, ALU.subtract, ALU.mult),
                          base + 1, "ln_step", "root2", 2 * c).then_inc(s["ln_step"], 1)
                dve.wait_ge(s["ln_step"], base + 7)
                at_least(dve, "x1_st", 16 * c)
                nc.vector.tensor_tensor(x1[:], xr[:], y[:], ALU.add).then_inc(s["x1_done"], 1)
                dve.wait_ge(s["x1_done"], c + 1)
                at_least(dve, "xs_st", 32 * c)
                layernorm(x1, st2, mv2, var2, rstd2,
                          lambda t, m, r: nc.vector.tensor_scalar(xs[:, t, 0:D], x1[:, t, :], m, r, ALU.subtract, ALU.mult),
                          base + 7, "ln_step", "root2", 2 * c + 1).then_inc(s["xn2_done"], 1)
            elif step == 2:
                dve.wait_ge(s["lg_ps"], c + 1)
                base = 4 * c
                lps = misc[:, 0:NT * E].rearrange("p (t e) -> p t e", t=NT)
                nc.vector.tensor_copy(lg[:], lps).then_inc(s["top_step"], 1)
                dve.wait_ge(s["top_step"], base + 1)
                nc.vector.tensor_reduce(lmax[:], lg[:], AX.X, ALU.max).then_inc(s["lg_ev"], 1)
                dve.wait_ge(s["lg_ev"], c + 1)
                nc.vector.tensor_tensor(cand[:], lg[:], lmax[:].rearrange("p (t o) -> p t o", o=1).broadcast_to([P, NT, E]), ALU.is_ge).then_inc(s["top_step"], 1)
                dve.wait_ge(s["top_step"], base + 2)
                iota = iota_e[:].rearrange("p (o e) -> p o e", o=1).broadcast_to([P, NT, E])
                nc.vector.tensor_tensor(cand[:], cand[:], iota, ALU.mult).then_inc(s["top_step"], 1)
                dve.wait_ge(s["top_step"], base + 3)
                nc.vector.tensor_reduce(lidx[:], cand[:], AX.X, ALU.min).then_inc(s["top_step"], 1)
                dve.wait_ge(s["top_step"], base + 4)
                nc.vector.tensor_tensor(oh[:], iota, lidx[:].rearrange("p (t o) -> p t o", o=1).broadcast_to([P, NT, E]), ALU.is_equal)
            else:
                dve.wait_ge(s["sg_done"], c + 1)
                base = 2 * c
                nc.vector.tensor_scalar(sg[:], sg[:], 1.0, None, ALU.add).then_inc(s["xn_step2"], 1)
                dve.wait_ge(s["xn_step2"], base + 1)
                nc.vector.reciprocal(sg[:], sg[:]).then_inc(s["xn_step2"], 1)
                dve.wait_ge(s["xn_step2"], base + 2)
                for t in range(NT):
                    ins = nc.vector.tensor_scalar(xs[:, t, D:2 * D], xs[:, t, 0:D], sg[:, t:t + 1], None, ALU.mult)
                ins.then_inc(s["xs_done"], 1)

        prep_at = {3: (0, 0), 7: (1, 0), 13: (0, 1), 21: (1, 1)}
        finish_at = {27: (0, 0), 32: (0, 1), 40: (0, 2), 43: (0, 3), 45: (1, 0), 50: (1, 1), 58: (1, 2), 61: (1, 3)}

        def turn(i, first, last):
            done = 0
            for slot in range(SLOTS):
                if not last and slot in prep_at:
                    prep(i + 1, *prep_at[slot])
                if slot % 32 == 8:
                    if slot > 32:
                        outputs(i, slot // 32 - 1)
                    elif not first:
                        outputs(i - 1, NT - 1)
                if not first and slot in finish_at:
                    finish(i - 1, *finish_at[slot])
                if not last:
                    while done < min(128, max(0, (slot - 23) * 4 // 3)):
                        row_max(i + 1, done // 64, done % 64)
                        done += 1

        dve.wait_ge(s["zeroed"], ZEROED)
        prep(0, 0, 0)
        prep(0, 1, 0)
        prep(0, 0, 1)
        prep(0, 1, 1)
        for k in range(128):
            row_max(0, k // 64, k % 64)
        turns(dve, turn)
        outputs(NP - 1, NT - 1)
        for b2 in range(2):
            for step in range(4):
                finish(NP - 1, b2, step)

    @block.gpsimd
    def _(pool):
        ps_ = s["pool_set"]
        pool.memset(ident[:], 0.0).then_inc(ps_, 1)
        pool.memset(ones[:], 1.0).then_inc(ps_, 1)
        pool.wait_ge(ps_, 2)
        pool.affine_select(out=ident[:], in_=ident[:], compare_op=ALU.not_equal, fill=1.0, base=0,
                           pattern=[[-1, P]], channel_multiplier=1).then_inc(ps_, 1)
        pool.affine_select(out=tri[:], in_=ones[:], compare_op=ALU.is_gt, fill=0.0, base=0,
                           pattern=[[1, P]], channel_multiplier=-1).then_inc(ps_, 1)
        pool.affine_select(out=hmask[:], in_=ones[:, 0:H], compare_op=ALU.is_ge, fill=0.0, base=0,
                           pattern=[[-HD, H]], channel_multiplier=1).then_inc(ps_, 1)
        pool.wait_ge(ps_, 5)
        pool.affine_select(out=hmask[:], in_=hmask[:], compare_op=ALU.is_ge, fill=0.0, base=HD - 1,
                           pattern=[[HD, H]], channel_multiplier=-1).then_inc(ps_, 1)
        pool.wait_ge(s["dve_set"], BOUNDS)
        for n in range(3):
            pool.partition_all_reduce(bmax[:, n:n + 1], bnd[:, n:n + 1], P, bass.bass_isa.ReduceOp.max).then_inc(ps_, 1)
        z = s["zeroed"]
        for buf in (*QC, *QT, Qn):
            flat = buf[:].rearrange({5: "p a b c d -> p (a b c d)", 4: "p a b c -> p (a b c)", 3: "p a b -> p (a b)"}[len(buf.shape)])
            pool.memset(flat.bitcast(F32), 0.0).then_inc(z, 1)
        pool.wait_ge(z, 5)
        for j in range(NT):
            pool.memset(KC[j][96:ROWS_CON].rearrange("p a b c d -> p (a b c d)"), -1.0 / MAXSCALE).then_inc(z, 1)
        pool.wait_ge(z, 5 + NT)
        pool.memset(vst[:, :, :, :, HD:HD + 1].rearrange("p a b c o -> p (a b) (c o)"), 1.0).then_inc(z, 1)
        pool.memset(c15[:], 1.5).then_inc(z, 1)
        for e in range(E):
            pool.memset(iota_e[:, e:e + 1], float(e - E)).then_inc(z, 1)

        def split(n, b2):
            c = 2 * n + b2
            pool.wait_ge(s["q_ev"], c + 1)
            at_least(pool, "qs_st", 16 * (c - 1))
            at_least(pool, "qb_done", 2 * (c - 1))
            pool.sem_inc(s["pool_passed"], 1)
            pool.tensor_copy(qs[b2][:, 0, :], qf[:]).then_inc(s["qsplit"], 1)
            pool.wait_ge(s["qsplit"], 2 * c + 1)
            pool.tensor_tensor(qs[b2][:, 1, :], qf[:], qs[b2][:, 0, :], ALU.subtract).then_inc(s["qsplit"], 1)
            pool.wait_ge(s["k_ev"], c + 1)
            at_least(pool, "ks_st", 16 * c)
            pool.sem_inc(s["pool_passed"], 1)
            src = kf[:].rearrange("p v (t k) -> p t v k", t=NT)
            pool.tensor_copy(ks[:, :, 0], src).then_inc(s["ksplit"], 1)
            pool.wait_ge(s["ksplit"], 2 * c + 1)
            pool.tensor_tensor(ks[:, :, 1], src, ks[:, :, 0], ALU.subtract).then_inc(s["ksplit"], 1)

        def refine(root, ve, tmp, name, n):
            done = ROOT_STEPS * n

            def step(k, ins):
                ins.then_inc(s[name], 1)
                pool.wait_ge(s[name], done + k + 1)
            newton(pool, step, root, ve, tmp, c15)

        def root(n, b2):
            c = 2 * n + b2
            pool.wait_ge(s["xn_step"], 5 * c + 5)
            refine(rstd, var, rtmp, "root", c)

        def roots2(n, b2):
            c = 2 * n + b2
            for k, done in enumerate((12 * c + 6, 12 * c + 12)):
                pool.wait_ge(s["ln_step"], done)
                refine(rstd2, var2, rtmp2, "root2", 2 * c + k)

        def prepare(n):
            for b2 in range(2):
                root(n, b2)
            for b2 in range(2):
                split(n, b2)

        def finish(n):
            for b2 in range(2):
                roots2(n, b2)

        def turn(i, first, last):
            if not last:
                prepare(i + 1)
            if not first:
                finish(i - 1)

        pool.wait_ge(s["sp_set"], 16 * (Z_W // 32 + NU * 3 + 2 * NE8))
        prepare(0)
        turns(pool, turn)
        finish(NP - 1)


IDENT_READY = 3
BOUNDS = 8
BOUNDS_MAX = 9
SCALED = BOUNDS + 7
RPART_READY = SCALED + 7
DVE_SET_DONE = RPART_READY + 6 + 3 + 3 + 4
ZEROED = 5 + NT + 2 + E
MS_STORES = 16 * 2 * NT
ROOT_STEPS = 12
QN_LOADS = 16 * NE8 * NT
QC_LOADS = 16 * (12 + 12 + 8)
KC_LOADS = 16 * (12 + 2)
O_STORES = 16 * (16 + 16)


MOE_SEMS = ("gu_ld oh_ld cnt_ps cnt_step slot_rdy eid_rdy xn_ld0 xn_ld1 xn_ld2 xn_ld3 idx scat0 scat1 scat2 scat3 "
            "xs_ld0 xs_ld1 xs_ld2 xs_ld3 sT_ps sT_ev gu_ps ex_done gate_step h_done hT_ps hT_ev y_ps y_ev ys_st0 ys_st1 "
            "gidx gat0 gat1 x1_ld0 x1_ld1 dve_passed2 pool_passed2 fin_step root3 out_rdy out_st0 out_st1")
RING = 4
GROUP = 4


def expert_phase(nc, ctx, a):
    s = a["moe_sem"]
    x1_d, xn_d, oh_d, xs_d, ys_d, out = (a[n] for n in "x1_d xn_d oh_d xs_d ys_d out".split())
    gate_up, down = a["gate_up"], a["down"]
    ident, sgu, sdn, tri, ones, c15 = (a[n] for n in "ident sgu sdn tri ones c15".split())

    def sb(name, shape, dt=F32):
        return ctx.enter_context(nc.sbuf_tensor(name, shape, dt))

    def pb(name, shape, dt=F32):
        return ctx.enter_context(nc.psum_tensor(name, shape, dt))

    GU = sb("GU", [P, E, 2 * F])
    DN = sb("DN", [P, E, 2, D])
    OH = sb("OH", [P, TILES, E])
    rank = sb("rank", [P, TILES, E])
    tot = sb("tot", [P, TILES, E])
    pref = [sb(f"pref{r}", [P, TILES, E]) for r in range(2)]
    ntile = sb("ntile", [P, E])
    ntile_i = sb("ntile_i", [P, E], I32)
    end = [sb(f"end{r}", [P, E]) for r in range(2)]
    start = sb("start", [P, E])
    slot_f = sb("slot_f", [P, TILES])
    slot_u = sb("slot_u", [P, TILES], U32)
    tau_i = sb("tau_i", [1, SORTED], I32)
    tau = sb("tau", [1, SORTED])
    past = sb("past", [1, SORTED, E])
    eid_f = sb("eid_f", [1, SORTED])
    eid = sb("eid", [1, SORTED], I32)
    xrow = [sb(f"xrow{r}", [P, 2 * D]) for r in range(RING)]
    idx = [sb(f"idx{r}", [P, 1], U32) for r in range(RING)]
    srow = [sb(f"srow{r}", [P, 2 * D]) for r in range(RING)]
    sT = [sb(f"sT{r}", [P, 2, P]) for r in range(2)]
    ee = [sb(f"ee{r}", [P, 2, F]) for r in range(2)]
    h = [sb(f"h{r}", [P, 4, P]) for r in range(2)]
    hT = [sb(f"hT{r}", [P, 4, P]) for r in range(2)]
    ysb = [sb(f"ysb{r}", [P, D]) for r in range(2)]
    gidx = [sb(f"gidx{r}", [P, GROUP], U32) for r in range(2)]
    yg = [sb(f"yg{r}", [P, GROUP, D]) for r in range(2)]
    x1g = [sb(f"x1g{r}", [P, GROUP, D]) for r in range(2)]
    st3 = sb("st3", [P, GROUP, 6])
    mv3 = sb("mv3", [P, GROUP, 2])
    var3, rstd3, rtmp3 = (sb(n, [P, GROUP]) for n in ("var3", "rstd3", "rtmp3"))
    og = [sb(f"og{r}", [P, GROUP, D]) for r in range(2)]

    gu = [pb(f"gu{r}", [P, 2, 2 * F]) for r in range(2)]
    tr = [pb(f"tr{r}", [P, 2, P]) for r in range(2)]
    hT_p = pb("hT_p", [P, 4, P])
    y_p = pb("y_p", [P, D])

    def ring(name, n):
        return [s[f"{name}{r}"] for r in range(n)]

    xn_ld, scat, xs_ld, ys_st = ring("xn_ld", RING), ring("scat", RING), ring("xs_ld", RING), ring("ys_st", 2)
    gat, x1_ld, out_st = ring("gat", 2), ring("x1_ld", 2), ring("out_st", 2)

    def at_least(eng, semaphore, value):
        if not (isinstance(value, int) and value <= 0):
            eng.wait_ge(semaphore, value)

    def loop(eng, count, body):
        body(0, True, False)
        with eng.Fori(1, count - 1) as g:
            body(g, False, False)
        body(count - 1, False, True)

    block = ctx.enter_context(nc.Block())

    @block.sync
    def _(sp):
        sp.dma_start(OH[:].rearrange("p (c t) e -> p c (t e)", t=NT), oh_d.rearrange("c p n -> p c n")).then_inc(s["oh_ld"], 16)

        def load_row(g, k):
            at_least(sp, scat[k], 16 * g)
            sp.dma_start(xrow[k][:], xn_d[bass.ds((RING * g + k) * P, P)]).then_inc(xn_ld[k], 16)

        for k in range(RING):
            load_row(0, k)
        sp.dma_start(GU[:], gate_up.rearrange("e h f -> h e f")).then_inc(s["gu_ld"], 16)
        for c in range(2):
            sp.dma_start(DN[:, :, c, :], down[:, P * c:P * c + P, :].rearrange("e f d -> f e d")).then_inc(s["gu_ld"], 16)
        with sp.Fori(1, TILES // RING) as g:
            for k in range(RING):
                load_row(g, k)
        for k in range(RING):
            sp.wait_ge(scat[k], 16 * (TILES // RING))

        def load_sorted(g, k):
            n = RING * g + k
            at_least(sp, s["sT_ps"], n - RING + 1)
            sp.dma_start(srow[k][:], xs_d[bass.ds(n * P, P)]).then_inc(xs_ld[k], 16)

        def store_y(n, r):
            sp.wait_ge(s["y_ev"], n + 1)
            sp.dma_start(ys_d[bass.ds(n * P, P)], ysb[r][:]).then_inc(ys_st[r], 16)

        for k in range(2):
            load_sorted(0, k)

        def sorted_tiles(g, first, last):
            for k in range(RING):
                n = RING * g + k
                if not (last and k >= RING - 2):
                    load_sorted(g + (k + 2) // RING, (k + 2) % RING)
                if not (first and k < 3):
                    store_y(n - 3, (k - 3) % 2)
        loop(sp, SORTED // RING, sorted_tiles)
        for n in range(SORTED - 3, SORTED):
            store_y(n, n % 2)

        def load_x1(g, r):
            at_least(sp, s["out_rdy"], g - 1)
            sp.dma_start(x1g[r][:], x1_d[bass.ds(g * GROUP * P, GROUP * P)].rearrange("(t p) d -> p t d", p=P)).then_inc(x1_ld[r], 16)

        def store_out(g, r):
            sp.wait_ge(s["out_rdy"], g + 1)
            dst = out.rearrange("b s d -> (b s) d")[bass.ds(g * GROUP * P, GROUP * P)]
            sp.dma_start(dst.rearrange("(t p) d -> p t d", p=P), og[r][:]).then_inc(out_st[r], 16)

        load_x1(0, 0)

        def groups(i, first, last):
            for r in range(2):
                if not (last and r == 1):
                    load_x1(2 * i + r + 1, 1 - r)
                store_out(2 * i + r, r)
        loop(sp, TILES // GROUP // 2, groups)
        for r in range(2):
            sp.wait_ge(out_st[r], 16 * (TILES // GROUP // 2))

    @block.gpsimd
    def _(pool):
        pool.iota(tau_i[:], [[1, SORTED]], base=0, channel_multiplier=0).then_inc(s["idx"], 1)
        pool.wait_ge(s["slot_rdy"], 1)

        def scatter(g, k):
            n = RING * g + k
            at_least(pool, scat[k], 16 * g)
            pool.sem_inc(s["pool_passed2"], 1)
            pool.tensor_copy(idx[k][:], slot_u[:, bass.ds(n, 1)]).then_inc(s["idx"], 1)
            pool.wait_ge(s["idx"], n + 2)
            pool.wait_ge(xn_ld[k], 16 * (g + 1))
            pool.sem_inc(s["pool_passed2"], 1)
            pool.indirect_dma_start(xs_d, bass.IndirectOffsetOnAxis(ap=idx[k][:], axis=0), xrow[k][:], None).then_inc(scat[k], 16)

        for k in range(RING):
            scatter(0, k)
        with pool.Fori(1, TILES // RING) as g:
            for k in range(RING):
                scatter(g, k)

        for r in range(2):
            pool.wait_ge(ys_st[r], 16 * (SORTED // 2))

        def gather(g, r):
            at_least(pool, s["out_rdy"], g - 1)
            pool.sem_inc(s["pool_passed2"], 1)
            pool.tensor_copy(gidx[r][:], slot_u[:, bass.ds(g * GROUP, GROUP)]).then_inc(s["gidx"], 1)
            pool.wait_ge(s["gidx"], g + 1)
            pool.sem_inc(s["pool_passed2"], 1)
            for t in range(GROUP):
                pool.indirect_dma_start(yg[r][:, t, :], None, ys_d, bass.IndirectOffsetOnAxis(ap=gidx[r][:, t:t + 1], axis=0)).then_inc(gat[r], 16)

        def refine(g):
            pool.wait_ge(s["fin_step"], 6 * g + 5)

            def step(k, ins):
                ins.then_inc(s["root3"], 1)
                pool.wait_ge(s["root3"], ROOT_STEPS * g + k + 1)
            newton(pool, step, rstd3, var3, rtmp3, c15)

        gather(0, 0)

        def groups(i, first, last):
            for r in range(2):
                if not (last and r == 1):
                    gather(2 * i + r + 1, 1 - r)
                refine(2 * i + r)
        loop(pool, TILES // GROUP // 2, groups)

    @block.tensor
    def _(pe):
        pe.wait_ge(s["oh_ld"], 16)
        for half in range(2):
            rhs = OH[:, TILES // 2 * half:TILES // 2 * (half + 1), :].rearrange("p t e -> p (t e)")
            nc.tensor.matmul(gu[0][:, half, :], tri[:], rhs, start=True, stop=True)
            mm = nc.tensor.matmul(gu[1][:, half, :], ones[:], rhs, start=True, stop=True)
        mm.then_inc(s["cnt_ps"], 1)
        pe.wait_ge(s["eid_rdy"], 1)
        pe.wait_ge(s["gu_ld"], 48)

        def transposes(n, k):
            pe.wait_ge(xs_ld[k], 16 * ((n - k) // RING + 1) if isinstance(n, int) else 16 * (n - k) // RING + 16)
            at_least(pe, s["sT_ev"], n - 1)
            for c in range(2):
                mm = nc.tensor.transpose(tr[k % 2][:, c, :], srow[k][:, D * c:D * c + D], ident[:])
            mm.then_inc(s["sT_ps"], 1)

        def gate_ups(n, k, e):
            pe.wait_ge(s["sT_ev"], n + 1)
            at_least(pe, s["h_done"], n - 1)
            for c in range(2):
                w_e = GU[:, bass.ds(e, 1), F * c:F * (c + 1)].rearrange("p o f -> p (o f)")
                nc.tensor.matmul(gu[k % 2][:, c, 0:F], sT[k % 2][:, 1, :], w_e, start=True, stop=True)
                mm = nc.tensor.matmul(gu[k % 2][:, c, F:2 * F], sT[k % 2][:, 0, :], sgu[:, F * c:F * (c + 1)], start=True, stop=True)
            mm.then_inc(s["gu_ps"], 1)

        def hidden_transposes(n, k):
            pe.wait_ge(s["h_done"], n + 1)
            at_least(pe, s["hT_ev"], n)
            for c in range(4):
                mm = nc.tensor.transpose(hT_p[:, c, :], h[k % 2][:, c, :], ident[:])
            mm.then_inc(s["hT_ps"], 1)

        def downs(n, k, e):
            pe.wait_ge(s["hT_ev"], n + 1)
            at_least(pe, s["y_ev"], n)
            for c in range(2):
                nc.tensor.matmul(y_p[:], hT[k % 2][:, c, :], DN[:, bass.ds(e, 1), c, :].rearrange("p o d -> p (o d)"), start=(c == 0), stop=False)
            for c in range(2):
                mm = nc.tensor.matmul(y_p[:], hT[k % 2][:, 2 + c, :], sdn[:, c, :], start=False, stop=(c == 1))
            mm.then_inc(s["y_ps"], 1)

        def expert(n):
            return pe.value_load(eid[0:1, bass.ds(n, 1)], min_val=0, max_val=E - 1)

        transposes(0, 0)

        def sorted_tiles(g, first, last):
            for k in range(RING):
                n = RING * g + k
                if not (last and k == RING - 1):
                    transposes(n + 1, (k + 1) % RING)
                gate_ups(n, k, expert(n))
                if not (first and k < 1):
                    hidden_transposes(n - 1, k - 1)
                if not (first and k < 2):
                    downs(n - 2, k - 2, expert(n - 2))
        loop(pe, SORTED // RING, sorted_tiles)
        hidden_transposes(SORTED - 1, RING - 1)
        for n in (SORTED - 2, SORTED - 1):
            downs(n, n % RING, expert(n))

    @block.scalar
    def _(act):
        def copy_rows(n, k):
            act.wait_ge(s["sT_ps"], n + 1)
            at_least(act, s["gu_ps"], n - 1)
            nc.scalar.copy(sT[k % 2][:], tr[k % 2][:]).then_inc(s["sT_ev"], 1)

        def exps(n, k):
            act.wait_ge(s["gu_ps"], n + 1)
            at_least(act, s["h_done"], n - 1)
            nc.scalar.activation(ee[k % 2][:], gu[k % 2][:, 0, :].rearrange("p (c f) -> p c f", c=2), ACT.Exp, scale=-1.0).then_inc(s["ex_done"], 1)

        def copy_hidden(n, k):
            act.wait_ge(s["hT_ps"], n + 1)
            at_least(act, s["y_ps"], n - 1)
            nc.scalar.copy(hT[k % 2][:], hT_p[:]).then_inc(s["hT_ev"], 1)

        def copy_y(n, k):
            act.wait_ge(s["y_ps"], n + 1)
            at_least(act, ys_st[k % 2], 16 * (n // 2) if isinstance(n, int) else 8 * (n - k % 2))
            nc.scalar.copy(ysb[k % 2][:], y_p[:]).then_inc(s["y_ev"], 1)

        copy_rows(0, 0)

        def sorted_tiles(g, first, last):
            for k in range(RING):
                n = RING * g + k
                if not (last and k == RING - 1):
                    copy_rows(n + 1, (k + 1) % RING)
                exps(n, k)
                if not (first and k < 1):
                    copy_hidden(n - 1, k - 1)
                if not (first and k < 2):
                    copy_y(n - 2, k % 2)
        loop(act, SORTED // RING, sorted_tiles)
        copy_hidden(SORTED - 1, 1)
        for n in (SORTED - 2, SORTED - 1):
            copy_y(n, n % 2)

    @block.vector
    def _(dve):
        count = [0]

        def link(ins):
            count[0] += 1
            ins.then_inc(s["cnt_step"], 1)
            dve.wait_ge(s["cnt_step"], count[0])

        dve.wait_ge(s["oh_ld"], 16)
        dve.wait_ge(s["cnt_ps"], 1)
        half = TILES // 2
        for c in range(2):
            nc.vector.tensor_copy(rank[:, half * c:half * (c + 1), :].rearrange("p t e -> p (t e)"), gu[0][:, c, :])
            link(nc.vector.tensor_copy(tot[:, half * c:half * (c + 1), :].rearrange("p t e -> p (t e)"), gu[1][:, c, :]))
        src, step, flip = tot, 1, 0
        while step < TILES:
            dst = pref[flip]
            link(nc.vector.tensor_copy(dst[:, 0:step, :], src[:, 0:step, :]))
            link(nc.vector.tensor_tensor(dst[:, step:, :], src[:, step:, :], src[:, 0:TILES - step, :], ALU.add))
            src, step, flip = dst, 2 * step, 1 - flip
        total = src
        link(nc.vector.tensor_scalar(ntile[:], total[:, TILES - 1, :], float(P - 1), None, ALU.add))
        link(nc.vector.tensor_copy(ntile_i[:], ntile[:]))
        link(nc.vector.tensor_scalar(ntile_i[:], ntile_i[:], P.bit_length() - 1, None, ALU.logical_shift_right))
        link(nc.vector.tensor_copy(ntile[:], ntile_i[:]))
        src_e, step, flip_e = ntile, 1, 0
        while step < E:
            dst_e = end[flip_e]
            link(nc.vector.tensor_copy(dst_e[:, 0:step], src_e[:, 0:step]))
            link(nc.vector.tensor_tensor(dst_e[:, step:], src_e[:, step:], src_e[:, 0:E - step], ALU.add))
            src_e, step, flip_e = dst_e, 2 * step, 1 - flip_e
        ends = src_e
        dve.wait_ge(s["idx"], 1)
        link(nc.vector.tensor_copy(tau[:], tau_i[:]))
        link(nc.vector.tensor_tensor(past[:], ends[0:1, :].rearrange("p (o e) -> p o e", o=1).broadcast_to([1, SORTED, E]),
                                     tau[:].rearrange("p (t o) -> p t o", o=1).broadcast_to([1, SORTED, E]), ALU.is_le))
        link(nc.vector.tensor_reduce(eid_f[:], past[:], AX.X, ALU.add))
        link(nc.vector.tensor_scalar(eid_f[:], eid_f[:], float(E - 1), None, ALU.min))
        nc.vector.tensor_copy(eid[:], eid_f[:]).then_inc(s["eid_rdy"], 1)
        link(nc.vector.tensor_tensor(start[:], ends[:], ntile[:], ALU.subtract))
        link(nc.vector.tensor_scalar(start[:], start[:], float(P), None, ALU.mult))
        link(nc.vector.tensor_tensor(tot[:], total[:], tot[:], ALU.subtract))
        link(nc.vector.tensor_tensor(tot[:], tot[:], rank[:], ALU.add))
        link(nc.vector.tensor_tensor(tot[:], tot[:], start[:].rearrange("p (o e) -> p o e", o=1).broadcast_to([P, TILES, E]), ALU.add))
        link(nc.vector.tensor_tensor(tot[:], tot[:], OH[:], ALU.mult))
        link(nc.vector.tensor_reduce(slot_f[:], tot[:], AX.X, ALU.add))
        nc.vector.tensor_copy(slot_u[:], slot_f[:]).then_inc(s["slot_rdy"], 1)

        def hidden(n, k):
            r = k % 2
            dve.wait_ge(s["ex_done"], n + 1)
            at_least(dve, s["h_done"], n - 1)
            nc.vector.tensor_scalar(ee[r][:], ee[r][:], 1.0, None, ALU.add).then_inc(s["gate_step"], 1)
            dve.wait_ge(s["gate_step"], 3 * n + 1)
            nc.vector.reciprocal(ee[r][:], ee[r][:]).then_inc(s["gate_step"], 1)
            dve.wait_ge(s["gate_step"], 3 * n + 2)
            flat = ee[r][:].rearrange("p c f -> p (c f)")
            nc.vector.tensor_tensor(flat, flat, gu[r][:, 0, :], ALU.mult).then_inc(s["gate_step"], 1)
            dve.wait_ge(s["gate_step"], 3 * n + 3)
            at_least(dve, s["hT_ps"], n - 1)
            nc.vector.tensor_tensor(h[r][:].rearrange("p c f -> p (c f)"), flat, gu[r][:, 1, :], ALU.mult).then_inc(s["h_done"], 1)

        def sorted_tiles(g, first, last):
            for k in range(RING):
                hidden(RING * g + k, k)
        loop(dve, SORTED // RING, sorted_tiles)

        def last_norm(g, r):
            dve.wait_ge(gat[r], 16 * GROUP * ((g - r) // 2 + 1) if isinstance(g, int) else 8 * GROUP * (g - r) + 16 * GROUP)
            at_least(dve, s["out_rdy"], g)
            base = 6 * g
            for t in range(GROUP):
                ins = nc.vector.bn_stats(st3[:, t, :], yg[r][:, t, :])
            ins.then_inc(s["fin_step"], 1)
            dve.wait_ge(s["fin_step"], base + 1)
            dve.sem_inc(s["dve_passed2"], 1)
            for t in range(GROUP):
                ins = nc.vector.bn_aggr(mv3[:, t, :], st3[:, t, :])
            ins.then_inc(s["fin_step"], 1)
            dve.wait_ge(s["fin_step"], base + 2)
            root_guess(nc, dve, s["fin_step"], base + 2, mv3, var3, rstd3)
            dve.wait_ge(s["root3"], ROOT_STEPS * (g + 1))
            for t in range(GROUP):
                ins = nc.vector.tensor_scalar(yg[r][:, t, :], yg[r][:, t, :], mv3[:, t, 0:1], rstd3[:, t:t + 1], ALU.subtract, ALU.mult)
            ins.then_inc(s["fin_step"], 1)
            dve.wait_ge(s["fin_step"], base + 6)
            dve.wait_ge(x1_ld[r], 16 * ((g - r) // 2 + 1) if isinstance(g, int) else 8 * (g - r) + 16)
            at_least(dve, out_st[r], 16 * ((g - r) // 2) if isinstance(g, int) else 8 * (g - r))
            nc.vector.tensor_tensor(og[r][:], x1g[r][:], yg[r][:], ALU.add).then_inc(s["out_rdy"], 1)

        def groups(i, first, last):
            for r in range(2):
                last_norm(2 * i + r, r)
        loop(dve, TILES // GROUP // 2, groups)


_INS = ["L0_attn_x", "L0_attn_Wq", "L0_attn_bq", "L0_attn_Wk", "L0_attn_bk", "L0_attn_Wv", "L0_attn_bv", "L0_attn_Wo", "L0_attn_bo",
        "L0_attn_rel_k", "L0_attn_rel_v", "L0_ffn_w_router", "L0_ffn_gate_up_proj", "L0_ffn_down_proj",
        "L0_ffn_w_gate", "L0_ffn_w_up", "L0_ffn_w_down"]
_OUTS = [((16, 512, 128), "float32")]


def kernel(**inputs):
    import numpy as _np
    import concourse.bacc as _bacc
    from concourse import mybir as _mybir
    from concourse.bass_utils import run_bass_kernel_spmd as _run

    nc = _bacc.Bacc("TRN2", target_bir_lowering=False, num_devices=1)
    arrays, args = {}, []
    for name in _INS:
        a = _np.ascontiguousarray(inputs[name])
        arrays[f"in_{name}_dram"] = a
        args.append(nc.dram_tensor(f"in_{name}_dram", a.shape, _mybir.dt.from_np(a.dtype), kind="ExternalInput").ap())
    outs = []
    for i, (shape, dtype) in enumerate(_OUTS):
        dt = _mybir.dt.from_np(_np.dtype(dtype))
        outs.append(nc.dram_tensor(f"out_{i}_dram", shape, dt, kind="ExternalOutput").ap())
    attention(nc, *outs, *args)
    r = _run(nc, [arrays], core_ids=[0])
    got = tuple(r.results[0][f"out_{i}_dram"] for i in range(len(_OUTS)))
    return got[0]
```

```python
from contextlib import ExitStack

import concourse.bass as bass
import numpy as np
from concourse import mybir

F32 = mybir.dt.float32
F16 = mybir.dt.float16
I32 = mybir.dt.int32
U32 = mybir.dt.uint32
ACT = mybir.ActivationFunctionType
ALU = mybir.AluOpType
AX = mybir.AxisListType

B, S, D = 16, 512, 128
H, HD = 16, 8
M = 128
NP = B // 2
P = 128
NT = S // P
E, F = 16, 256
TOK = B * S
TILES = TOK // P
SORTED = TILES + E
EPS = 1e-5

NU, NS, NB = 4, 4, 8
TERMS = ((0, 0), (0, 1), (1, 0))
ROWS_TERM = 3 * HD
ROWS_HEAD = ROWS_TERM + 2
ROWS_REL = NU * ROWS_TERM
ROWS_CON = 4 * ROWS_HEAD
NE8 = 8
SLOTS = 2 * NT * NT * NS
MAXSCALE = 2.0 ** -14
XMAX = 12.0

OFF0 = 255
WT_W, WT_0 = 415, 159
WN_W, WN_0 = 367, 127
Z_W, Z_0 = 384, 255


def attention(nc, out, x, Wq, bq, Wk, bk, Wv, bv, Wo, bo, rel_k, rel_v, w_router, gate_up, down, w_gate, w_up, w_down, dbg=None):
    ctx = ExitStack()
    outer = ExitStack()

    def dram(name, shape, dt):
        return nc.dram_tensor(name, shape, dt, kind="Internal").ap()

    qt_d = dram("qt_d", [B * H, ROWS_HEAD, S], F16)
    qn_d = dram("qn_d", [B * P, NE8 * NT * 16], F16)
    kt_d = dram("kt_d", [B * H, ROWS_TERM, NT, 2, P], F16)
    vs_d = dram("vs_d", [B, P, NT, 2 * H * 9], F32)
    rvp_d = dram("rvp_d", [512, HD], F32)
    opv_d = dram("opv_d", [B * H, HD + 1, S], F32)
    orl_d = dram("orl_d", [B * H * HD, S], F32)
    xn_d = dram("xn_d", [TOK, ROW], F32)
    oh_d = dram("oh_d", [B, P, NT * E], F32)
    xs_d = dram("xs_d", [SORTED * P, ROW], F32)

    with outer:
        def osb(name, shape, dt):
            return outer.enter_context(nc.sbuf_tensor(name, shape, dt))

        ident = osb("ident", [P, P], F32)
        sgu = osb("sgu", [P, 2 * F], F32)
        sdn = osb("sdn", [P, 2, D], F32)
        tri = osb("tri", [P, P], F32)
        ones = osb("ones", [P, P], F32)
        c15 = osb("c15", [P, NT], F32)

        moe_sem = {n: outer.enter_context(nc.semaphore(n)) for n in MOE_SEMS.split()}
        with ctx:
            attention_phase(nc, ctx, locals())
        with ExitStack() as moe_ctx:
            expert_phase(nc, moe_ctx, locals())


def root_guess(nc, dve, step, done, mean_var, half, root):
    nc.vector.tensor_scalar(half[:], mean_var[:, :, 1], EPS, 0.5, ALU.add, ALU.mult).then_inc(step, 1)
    dve.wait_ge(step, done + 1)
    nc.vector.tensor_scalar(root[:].bitcast(I32), half[:].bitcast(I32), 1, None, ALU.logical_shift_right).then_inc(step, 1)
    dve.wait_ge(step, done + 2)
    nc.vector.tensor_scalar(root[:].bitcast(I32), root[:].bitcast(I32), -1.0, float(0x5F3759DF - (1 << 22)), ALU.mult, ALU.add).then_inc(step, 1)


def newton(pool, step, root, half, tmp, c15):
    for it in range(3):
        step(4 * it, pool.tensor_tensor(tmp[:], root[:], root[:], ALU.mult))
        step(4 * it + 1, pool.tensor_tensor(tmp[:], tmp[:], half[:], ALU.mult))
        step(4 * it + 2, pool.tensor_tensor(tmp[:], c15[:], tmp[:], ALU.subtract))
        step(4 * it + 3, pool.tensor_tensor(root[:], root[:], tmp[:], ALU.mult))


def attention_phase(nc, ctx, a):
    (x, Wq, bq, Wk, bk, Wv, bv, Wo, bo, rel_k, rel_v, w_router, w_gate, w_up, w_down) = (
        a[n] for n in "x Wq bq Wk bk Wv bv Wo bo rel_k rel_v w_router w_gate w_up w_down".split())
    (qt_d, qn_d, kt_d, vs_d, rvp_d, opv_d, orl_d, xn_d, oh_d, xs_d) = (
        a[n] for n in "qt_d qn_d kt_d vs_d rvp_d opv_d orl_d xn_d oh_d xs_d".split())
    ident, sgu, sdn, tri, ones, c15 = (a[n] for n in "ident sgu sdn tri ones c15".split())

    def sb(name, shape, dt=F32):
        return ctx.enter_context(nc.sbuf_tensor(name, shape, dt))

    def pb(name, shape, dt=F32):
        return ctx.enter_context(nc.psum_tensor(name, shape, dt))

    def sem(name):
        return ctx.enter_context(nc.semaphore(name))

    wqT, wkT, wvT, woT = (sb(n, [P, P]) for n in ("wqT", "wkT", "wvT", "woT"))
    wrT = sb("wrT", [P, E])
    bq_s = sb("bq_s", [P, 1])
    kb = sb("kb", [P, 3])
    vb = sb("vb", [P, 3, P])
    bo_s = sb("bo_s", [P, P])
    escale = sb("escale", [P, 1])
    iota_e = sb("iota_e", [P, E])
    Wt = sb("Wt", [ROWS_REL, WT_W + 1], F16)
    Wn = sb("Wn", [P, WN_W + 1], F16)
    Rv = sb("Rv", [P, 32, Z_W // 32, HD])
    hmask = sb("hmask", [P, H])
    KC = [sb(f"KC{j}", [ROWS_CON, 2, 4, 2, P], F16) for j in range(NT)]
    VC = [sb(f"VC{j}", [P, 2, 2, H, 9]) for j in range(NT)]
    QC = [sb(f"QC{r}", [ROWS_CON, 2, 4, 4, P], F16) for r in range(2)]
    QT = [sb(f"QT{r}", [ROWS_REL, NU, 2, H, 32], F16) for r in range(2)]
    w = [sb(f"w{r}", [P, 2, NS, H, NU, NB]) for r in range(2)]
    pv_s = sb("pv_s", [P, 2, 4, P])
    rel_s = sb("rel_s", [P, 2 * H, NU, NB])
    xt = [sb(f"xt{r}", [P, NT, D]) for r in range(2)]
    st = sb("st", [P, NT, 6])
    mv = sb("mv", [P, NT, 2])
    var = sb("var", [P, NT])
    rstd = sb("rstd", [P, NT])
    rtmp = sb("rtmp", [P, NT])
    xn = sb("xn", [P, NT, D])
    xnT = sb("xnT", [P, S])
    qf = sb("qf", [P, S])
    kf = sb("kf", [P, 2, S])
    qs = sb("qs", [P, 2, S], F16)
    qp = [sb(f"qp{r}", [P, NE8, NT, 16], F16) for r in range(2)]
    ks = sb("ks", [P, 2, NT, 2, P], F16)
    zrow = sb("zrow", [P, ROW])
    number_i = sb("number_i", [P, NT], I32)
    number = sb("number", [P, NT])
    vst = sb("vst", [P, NT, 2, H, 9])
    kn = [sb(f"kn{r}", [P, 3, S], F16) for r in range(2)]
    Qb = [sb(f"Qb{r}", [P, NE8, H, 32], F16) for r in range(2)]
    Qn = sb("Qn", [P, NE8, H, NT * 16], F16)
    mx = sb("mx", [P, NT * 16])
    ms = sb("ms", [P, 2, NT * 16], F16)
    oA, oB, oS = (sb(n, [P, S]) for n in ("oA", "oB", "oS"))
    xr = sb("xr", [P, NT, D])
    y = sb("y", [P, NT, D])
    st2 = sb("st2", [P, NT, 6])
    mv2 = sb("mv2", [P, NT, 2])
    var2 = sb("var2", [P, NT])
    rstd2 = sb("rstd2", [P, NT])
    rtmp2 = sb("rtmp2", [P, NT])
    x2T = sb("x2T", [P, S])
    xs = sb("xs", [P, NT, ROW])
    lg = sb("lg", [P, NT, E])
    lmax = sb("lmax", [P, NT])
    cand = sb("cand", [P, NT, E])
    lidx = sb("lidx", [P, NT])
    oh = sb("oh", [P, NT, E])
    sg = sb("sg", [P, NT])

    sc = [pb(f"sc{r}", [P, S]) for r in range(2)]
    mix = [pb(f"mix{r}", [P, S]) for r in range(2)]
    pv = [pb(f"pv{r}", [P, S]) for r in range(2)]
    rel = [pb(f"rel{r}", [P, S]) for r in range(2)]

    names = ("w_ld tab pool_set dve_set act_set pe_set sp_set zeroed "
             "x_ld0 x_ld1 xn_step xn_done xT_ps xnT_rdy q_ps q_ev k_ps k_read k_ev v_ps v_ev qsplit ksplit "
             "qs_st qn_st ks_st vs_st qb_done qn_ld0 qn_ld1 nat_ps mx_done ms_step ms_done ms_st "
             "qc_ld0 qc_ld1 kc_ld0 kc_ld1 kc_ld2 kc_ld3 s_done exp_done pv_done pv_ev rel_ev o_st "
             "o_ld o_step O_rdy op_ps op_ev ln_step x1_done xn2_done x2T_ps x2T_ev lg_ps lg_ev "
             "dve_passed pool_passed sp_passed root root2 top_step sg_done number_step sg_step xs_done xs_st z_st")
    s = {n: sem(n) for n in names.split()}
    x_ld = [s["x_ld0"], s["x_ld1"]]
    qn_ld = [s["qn_ld0"], s["qn_ld1"]]
    qc_ld = [s["qc_ld0"], s["qc_ld1"]]
    kc_ld = [s[f"kc_ld{j}"] for j in range(NT)]

    def at_least(eng, name, value):
        if not (isinstance(value, int) and value <= 0):
            eng.wait_ge(s[name] if isinstance(name, str) else name, value)

    def turns(eng, body):
        body(0, False, True, True)
        body(1, True, True, True)
        with eng.Fori(2, NP - 2) as i:
            body(i, True, True, True)
        body(NP - 2, True, True, False)
        body(NP - 1, True, False, False)

    shared = []
    for slot in range(SLOTS):
        shared.append(("row max", slot))
        for half in range(2):
            if slot - 64 * half in PREPARE_PE:
                shared.append(("prepare", half, PREPARE_PE[slot - 64 * half]))
        for b2 in range(2):
            if slot - FINISH[b2] in FINISH_PE:
                shared.append(("finish", b2, FINISH_PE[slot - FINISH[b2]]))
    assert len(shared) % 2 == 0
    place = {job: n for n, job in enumerate(shared)}

    def bank(*job):
        return mix[place[job] % 2]

    def wait_for_bank(pe, job, i, prev, nxt, nxt2):
        n, turns_back = place[job] - 2, 0
        while True:
            if n < 0:
                if isinstance(i, int) and i == 0:
                    return
                n, turns_back = n + len(shared), 1
                nxt, nxt2 = True, nxt
                prev = not isinstance(i, int) or i > 1
            what, turn = shared[n], i - turns_back
            if what[0] == "row max" and nxt:
                pe.wait_ge(s["mx_done"], 128 * (turn + 1) + what[1] + 1)
                return
            if what[0] == "prepare" and (nxt2 if what[1] else nxt):
                c = 2 * turn + (4 if what[1] else 3)
                pe.wait_ge(s[("xnT_rdy", "q_ev", "k_read", "v_ev")[what[2]]], c + 1)
                return
            if what[0] == "finish" and prev:
                c = 2 * (turn - 1) + what[1]
                pe.wait_ge(*((s["ln_step"], 12 * c + 1), (s["x2T_ev"], c + 1), (s["lg_ev"], c + 1))[what[2]])
                return
            n -= 2

    wraw = [w[0][:, 0].rearrange("p a b c d -> p (a b c d)")[:, P * n:P * n + P] for n in range(4)]
    wg_raw = w[0][:, 1].rearrange("p a b c d -> p (a b c d)")
    wr_raw = wg_raw[0:E, 6 * P:7 * P]
    gu_raw = [wg_raw[:, P * n:P * n + P] for n in range(6)]
    rkT = w[1][0:HD, 0].rearrange("p a b c d -> p (a b c d)")[:, 0:2 * M + 1]
    rpad = w[1][0:HD, 0].rearrange("p a b c d -> p (a b c d)")[:, 512:1024]
    rzero = w[1][0:HD, 0].rearrange("p a b c d -> p (a b c d)")[:, 1024:1024 + P]
    rpart = [qs[0:HD, 0, :], qs[0:HD, 1, :]]
    sq = w[1][:, 1].rearrange("p a b c d -> p (a b c d)")
    bnd = sq[:, 256:264]
    bmax = sq[:, 264:272]
    pw = sq[:, 272:280]
    bkr = sq[:, 280:284]
    bqr = sq[:, 284:285]
    vraw = sq[:, 512:1024].rearrange("p (a b) -> p a b", b=P)[:, 0:3]

    LOADS = 4 + 6 + 1 + 1 + 4 + 4

    block = ctx.enter_context(nc.Block())

    @block.sync
    def _(sp):
        def load_x(n, b2):
            at_least(sp, "xn_done", 2 * n + b2 - 1)
            sp.dma_start(xt[b2][:], x[bass.ds(2 * n + b2, 1)].rearrange("o (t p) d -> p (o t) d", p=P)).then_inc(x_ld[b2], 16)

        load_x(0, 0)
        load_x(0, 1)
        ld = s["w_ld"]
        for n, W in enumerate((Wq, Wk, Wv, Wo)):
            sp.dma_start(wraw[n], W).then_inc(ld, 16)
        for n in range(2):
            sp.dma_start(gu_raw[n], w_gate[P * n:P * n + P]).then_inc(ld, 16)
            sp.dma_start(gu_raw[2 + n], w_up[P * n:P * n + P]).then_inc(ld, 16)
            sp.dma_start(gu_raw[4 + n], w_down[:, P * n:P * n + P]).then_inc(ld, 16)
        sp.dma_start(wr_raw, w_router).then_inc(ld, 16)
        with nc.allow_non_contiguous_dma(reason="small tables, once"):
            sp.dma_start(rkT, rel_k.rearrange("r d -> d r")).then_inc(ld, 16)
            sp.dma_start(bqr, bq.rearrange("(p o) -> p o", o=1)).then_inc(ld, 16)
            sp.dma_start(bkr[:, 0:1], bk.rearrange("(p o) -> p o", o=1)).then_inc(ld, 16)
            for n, r in ((1, 0), (2, 2 * M)):
                src = rel_k[r:r + 1, :]
                sp.dma_start(bkr[:, n:n + 1], bass.AP(src.tensor, src.offset, [[0, H], [1, HD], [1, 1]])).then_inc(ld, 16)
            sp.dma_start(vraw[:, 0, :], bass.AP(bv.tensor, bv.offset, [[0, P], [1, P]])).then_inc(ld, 16)
            sp.dma_start(bo_s[:], bass.AP(bo.tensor, bo.offset, [[0, P], [1, P]])).then_inc(ld, 16)
            for n, r in ((1, 0), (2, 2 * M)):
                src = rel_v[r:r + 1, :]
                sp.dma_start(vraw[:, n, :].rearrange("p (h d) -> p h d", d=HD),
                             bass.AP(src.tensor, src.offset, [[0, P], [0, H], [1, HD]])).then_inc(ld, 16)
            tab = s["tab"]
            sp.dma_start(rvp_d[127:127 + 2 * M + 1], rel_v).then_inc(tab, 16)
            sp.dma_start(rvp_d[0:127], bass.AP(rel_v.tensor, rel_v.offset, [[0, 127], [1, HD]])).then_inc(tab, 16)
            sp.dma_start(rvp_d[384:512], bass.AP(rel_v.tensor, rel_v.offset + 2 * M * HD, [[0, 128], [1, HD]])).then_inc(tab, 16)
        sp.wait_ge(tab, 48)
        for m in range(Z_W // 32):
            sp.dma_start(Rv[:, :, m, :], bass.AP(rvp_d.tensor, rvp_d.offset + 32 * m * HD,
                                                 [[HD, P], [HD, 32], [1, HD]])).then_inc(s["sp_set"], 16)
        sp.wait_ge(s["dve_set"], RPART_READY)
        for u in range(NU):
            for t, (_, kp) in enumerate(TERMS):
                r = (u * 3 + t) * HD
                c = OFF0 - WT_0 - 32 * u
                sp.dma_start(Wt[r:r + HD, 0:WT_W], rpart[kp][:, c:c + WT_W]).then_inc(s["sp_set"], 16)
        for half in range(2):
            for e in range(NE8):
                c = OFF0 - WN_0 - 16 * e
                sp.dma_start(Wn[64 * half + HD * e:64 * half + HD * e + HD, 0:WN_W], rpart[0][:, c:c + WN_W]).then_inc(s["sp_set"], 16)
        def zero_sorted():
            rows = xs_d.rearrange("(a p) n -> p a n", p=P)
            for c in range(0, SORTED, ZERO_TILES):
                sp.dma_start(rows[:, c:c + ZERO_TILES],
                             zrow[:].rearrange("p (o n) -> p o n", o=1).broadcast_to([P, ZERO_TILES, ROW])).then_inc(s["z_st"], 16)

        def store_q(n, b2):
            c = 2 * n + b2
            sp.wait_ge(s["qsplit"], 3 * c + 3)
            sp.dma_start(qn_d[bass.ds(c * P, P)], qp[b2][:].rearrange("p e t b -> p (e t b)")).then_inc(s["qn_st"], 16)
            for tm, (qpart, _) in enumerate(TERMS):
                sp.dma_start(qt_d[bass.ds(c * H, H), HD * tm:HD * tm + HD, :], qs[:, qpart, :]).then_inc(s["qs_st"], 16)
            sp.wait_ge(s["qn_st"], 16 * (c + 1))
            sp.sem_inc(s["sp_passed"], 1)
            at_least(sp, "nat_ps", 64 * (c - 1))
            sp.sem_inc(s["sp_passed"], 1)
            src = qn_d[bass.ds(c * P, P)].rearrange("(h d) (e k) -> e d h k", d=HD, e=NE8)
            for e in range(NE8):
                row = 64 * b2 + HD * e
                sp.dma_start(Qn[row:row + HD, e, :, :], src[e]).then_inc(qn_ld[b2], 16)

        def store_kv(n, b2):
            c = 2 * n + b2
            sp.wait_ge(s["ksplit"], 2 * c + 2)
            for tm, (_, kpart) in enumerate(TERMS):
                sp.dma_start(kt_d[bass.ds(c * H, H), HD * tm:HD * tm + HD].rearrange("h d t v k -> h d (t v k)"),
                             ks[:, kpart].rearrange("p t v k -> p (t v k)")).then_inc(s["ks_st"], 16)
            sp.wait_ge(s["v_ev"], c + 1)
            sp.dma_start(vs_d[bass.ds(c, 1)].rearrange("o p t n -> p (o t) n"),
                         vst[:].rearrange("p t v h n -> p t (v h n)")).then_inc(s["vs_st"], 16)

        def store_max(n, b2, t):
            group = NT * (2 * n + b2) + t
            sp.wait_ge(s["ms_done"], group + 1)
            sp.sem_inc(s["sp_passed"], 1)
            at_least(sp, "ms_st", 32 * group)
            dst = qt_d[bass.ds((2 * n + b2) * H, H)].rearrange("h r (t e b) -> r t e h b", t=NT, e=NE8)
            for part in range(2):
                sp.dma_start(dst[ROWS_TERM + part, t], ms[:, part, 16 * t:16 * t + 16]).then_inc(s["ms_st"], 16)

        def load_q(n, t):
            r = t % 2
            at_least(sp, "s_done", n * SLOTS + 32 * (t - 1))
            sp.sem_inc(s["sp_passed"], 1)
            if t == 0:
                sp.wait_ge(s["qs_st"], 48 * (2 * n + 2))
            sp.wait_ge(s["ms_st"], 32 * (NT * (2 * n + 1) + t + 1))
            sp.sem_inc(s["sp_passed"], 1)
            src = qt_d[bass.ds(2 * n * H, 2 * H)]
            heads4 = src.rearrange("(bg hh) r q -> hh r bg q", hh=4)
            for hh in range(4):
                row = ROWS_HEAD * hh
                sp.dma_start(QC[r][row:row + ROWS_HEAD, :, :, hh, :].rearrange("r b g q -> r (b g) q"),
                             heads4[hh, :, :, P * t:P * t + P]).then_inc(qc_ld[r], 16)
            heads = src.rearrange("bh r q -> r bh q")
            for u in range(NU):
                row = ROWS_TERM * u
                sp.dma_start(QT[r][row:row + ROWS_TERM, u].rearrange("r b h q -> r (b h) q"),
                             heads[0:ROWS_TERM, :, P * t + 32 * u:P * t + 32 * u + 32]).then_inc(qc_ld[r], 16)

        def load_kv(n, j):
            at_least(sp, "s_done", (n - 1) * SLOTS + 96 + 8 * (j + 1))
            sp.sem_inc(s["sp_passed"], 1)
            at_least(sp, "pv_done", (n - 1) * SLOTS + 96 + 8 * (j + 1))
            sp.sem_inc(s["sp_passed"], 1)
            sp.wait_ge(s["ks_st"], 48 * (2 * n + 2))
            sp.sem_inc(s["sp_passed"], 1)
            sp.wait_ge(s["vs_st"], 16 * (2 * n + 2))
            sp.sem_inc(s["sp_passed"], 1)
            src = kt_d[bass.ds(2 * n * H, 2 * H)].rearrange("(bg hh) r t v k -> hh r bg t (v k)", hh=4)
            for hh in range(4):
                row = ROWS_HEAD * hh
                sp.dma_start(KC[j][row:row + ROWS_TERM].rearrange("r b g v k -> r (b g) (v k)"), src[hh, :, :, j, :]).then_inc(kc_ld[j], 16)
            sp.dma_start(VC[j][:].rearrange("p b v h n -> p b (v h n)"),
                         vs_d[bass.ds(2 * n, 2), :, j, :].rearrange("b p n -> p b n")).then_inc(kc_ld[j], 16)

        def store_o(n, t):
            sp.wait_ge(s["pv_ev"], 4 * n + t + 1)
            rows = opv_d[bass.ds(2 * n * H, 2 * H)].rearrange("(b g hh) d q -> b g d hh q", b=2, g=4)
            for b2 in range(2):
                for g in range(4):
                    sp.dma_start(rows[b2, g, :, :, P * t:P * t + P], pv_s[32 * g:32 * g + HD + 1, b2]).then_inc(s["o_st"], 16)
            sp.wait_ge(s["rel_ev"], 4 * n + t + 1)
            dst = orl_d[bass.ds(2 * n * P, 2 * P)].rearrange("(bh d) q -> d bh q", d=HD)
            for sb_ in range(NS):
                for u in range(NU):
                    row = 32 * sb_ + HD * (NU - 1 - u)
                    q0 = P * t + 32 * u + NB * sb_
                    sp.dma_start(dst[:, :, q0:q0 + NB], rel_s[row:row + HD, :, u, :]).then_inc(s["o_st"], 16)

        def load_o(n, b2):
            c = 2 * n + b2
            if b2 == 0:
                sp.wait_ge(s["o_st"], O_STORES * NT * (n + 1))
                sp.sem_inc(s["sp_passed"], 1)
            at_least(sp, "op_ps", c)
            at_least(sp, "x1_done", c)
            sp.sem_inc(s["sp_passed"], 1)
            sp.dma_start(oA[:], opv_d[bass.ds(c * H, H), 0:HD, :]).then_inc(s["o_ld"], 16)
            sp.dma_start(oB[:], orl_d[bass.ds(c * P, P)]).then_inc(s["o_ld"], 16)
            sp.dma_start(oS[:], opv_d[bass.ds(c * H, H), HD:HD + 1, :].broadcast_to([H, HD, S])).then_inc(s["o_ld"], 16)
            sp.dma_start(xr[:], x[bass.ds(c, 1)].rearrange("o (t p) d -> p (o t) d", p=P)).then_inc(s["o_ld"], 16)

        def store_xs(n, b2):
            c = 2 * n + b2
            sp.wait_ge(s["xs_done"], c + 1)
            sp.dma_start(xn_d[bass.ds(c * S, S)].rearrange("(t p) d -> p t d", p=P), xs[:]).then_inc(s["xs_st"], 16)
            sp.dma_start(oh_d[bass.ds(c, 1)].rearrange("o p n -> p (o n)"), oh[:].rearrange("p t e -> p (t e)")).then_inc(s["xs_st"], 16)

        finish_at = {0: load_o, 34: store_xs}

        def turn(i, prev, nxt, nxt2):
            for slot in range(SLOTS):
                if slot == 1:
                    if prev:
                        store_max(i, 1, NT - 1)
                    load_q(i, 1)
                    load_kv(i, 2)
                if slot in (33, 65):
                    load_q(i, slot // 32 + 1)
                if slot == 9:
                    load_kv(i, 3)
                if slot % 32 == 10 and (prev or slot > 32):
                    t = slot // 32 - 1
                    store_o(i, t) if t >= 0 else store_o(i - 1, NT - 1)
                if nxt2 and slot in (2, 60):
                    load_x(i + 2, slot // 60)
                if nxt:
                    if slot == 14:
                        store_q(i + 1, 1)
                    if slot == 22:
                        store_kv(i + 1, 1)
                    if slot % 16 == 1 and slot > 1:
                        store_max(i + 1, (slot // 16 - 1) // NT, (slot // 16 - 1) % NT)
                    if slot == 100:
                        load_q(i + 1, 0)
                    if slot == 113:
                        load_kv(i + 1, 0)
                    if slot == 124:
                        load_kv(i + 1, 1)
                if nxt2:
                    if slot == 64 + 14:
                        store_q(i + 2, 0)
                    if slot == 64 + 22:
                        store_kv(i + 2, 0)
                if prev:
                    for b2 in range(2):
                        if slot - FINISH[b2] in finish_at:
                            finish_at[slot - FINISH[b2]](i - 1, b2)
                elif slot == 40:
                    zero_sorted()

        for b2 in range(2):
            store_q(0, b2)
            store_kv(0, b2)
        load_x(1, 0)
        load_x(1, 1)
        for b2 in range(2):
            for t in range(NT):
                store_max(0, b2, t)
        load_q(0, 0)
        load_kv(0, 0)
        load_kv(0, 1)
        store_q(1, 0)
        store_kv(1, 0)
        turns(sp, turn)
        store_o(NP - 1, NT - 1)
        for b2 in range(2):
            for step in finish_at.values():
                step(NP - 1, b2)
        sp.wait_ge(s["z_st"], 16 * (SORTED // ZERO_TILES))
        sp.wait_ge(s["xs_st"], 32 * B)

    @block.tensor
    def _(pe):
        def transpose(out_, in_):
            k = in_.shape[0]
            return nc.tensor.transpose(out_, in_, ident[0:k, 0:k])

        pe.wait_ge(s["pool_set"], IDENT_READY)
        pe.wait_ge(s["w_ld"], 16 * LOADS)
        pe.wait_ge(s["dve_set"], SCALED)
        for n in range(4):
            mm = transpose(sc[0][:, P * n:P * n + P], wraw[n])
        for n in range(4):
            mm = transpose(sc[1][:, P * n:P * n + P], gu_raw[n])
        for n in range(2):
            mm = transpose(mix[0][:, P * n:P * n + P], gu_raw[4 + n])
        mm = transpose(mix[1][:, 0:E], wr_raw)
        mm.then_inc(s["pe_set"], 1)
        pe.wait_ge(s["act_set"], 1)
        pe.wait_ge(s["dve_set"], DVE_SET_DONE)

        def prep(n, b2, step, mix):
            c = 2 * n + b2
            if step == 0:
                pe.wait_ge(s["xn_done"], c + 1)
                for t in range(NT):
                    mm = transpose(mix[:, P * t:P * t + P], xn[:, t, :])
                mm.then_inc(s["xT_ps"], 1)
            elif step == 1:
                pe.wait_ge(s["xnT_rdy"], c + 1)
                nc.tensor.matmul(mix[:], wqT[:], xnT[:], start=True, stop=True).then_inc(s["q_ps"], 1)
            elif step == 2:
                nc.tensor.matmul(mix[:], wkT[:], xnT[:], start=True, stop=True).then_inc(s["k_ps"], 1)
            else:
                for t in range(NT):
                    mm = nc.tensor.matmul(mix[:, P * t:P * t + P], xnT[:, P * t:P * t + P], wvT[:], start=True, stop=True)
                mm.then_inc(s["v_ps"], 1)

        def natural(n, b2, k, nat):
            c = 2 * n + b2
            if k == 0:
                pe.wait_ge(s["k_ev"], c + 1)
                pe.wait_ge(qn_ld[b2], QN_LOADS * (n + 1))
            if k % 32 == 0:
                pe.wait_ge(s["qb_done"], 2 * c + k // 32 + 1)
            t, b = k // 16, k % 16
            lo = max(0, P * t + b - (M - 1))
            hi = min(S, P * t + b + 16 * (NE8 - 1) + M)
            lq = Qb[t // 2][:, :, :, 16 * (t % 2) + b].rearrange("p e h -> p (e h)")
            le = Qn[64 * b2:64 * b2 + 64, :, :, k].rearrange("p e h -> p (e h)")
            x0 = WN_0 - P * t - b
            nc.tensor.matmul(nat[:, lo:hi], lq, kn[b2][:, 0, lo:hi], start=True, stop=False, skip_group_check=True)
            mm = nc.tensor.matmul(nat[:, lo:hi], le, Wn[64 * b2:64 * b2 + 64, x0 + lo:x0 + hi], start=False, stop=True, skip_group_check=True)
            if lo > 0:
                mm = nc.tensor.matmul(nat[:, 0:lo], lq, kn[b2][:, 1, 0:lo], start=False, stop=True, skip_group_check=True)
            if hi < S:
                mm = nc.tensor.matmul(nat[:, hi:S], lq, kn[b2][:, 2, hi:S], start=False, stop=True, skip_group_check=True)
            mm.then_inc(s["nat_ps"], 1)

        def scores(i, slot):
            t, j, b2, q8 = slot // 32, slot // 8 % 4, slot // 4 % 2, slot % 4
            if slot % 32 == 0:
                pe.wait_ge(qc_ld[t % 2], QC_LOADS * (2 * i + t // 2 + 1))
            if t == 0 and slot % 8 == 0:
                pe.wait_ge(kc_ld[j], KC_LOADS * (i + 1))
            at_least(pe, "exp_done", SLOTS * i + slot - 1)
            near = abs(t - j) <= 1
            bank = sc[slot % 2]
            qc = QC[t % 2][:, b2].rearrange("p g h (u s b) -> p g h u s b", u=NU, s=NS)
            for g in range(4):
                mm = nc.tensor.matmul(bank[:, P * g:P * g + P], KC[j][:, b2, g, 0 if near else 1, :], qc[:, g, :, :, q8, :],
                                      start=(g == 0), stop=not near, skip_group_check=True)
            if near:
                view = bank[:].rearrange("p (h u b) -> p h u b", h=H, u=NU)
                qt = QT[t % 2][:, :, b2].rearrange("p u h q -> p h u q")
                for b in range(NB):
                    x0 = WT_0 + P * (j - t) - NB * q8 - b
                    mm = nc.tensor.matmul(view[:, :, :, b], Wt[:, x0:x0 + P], qt[:, :, :, NB * q8 + b], start=False, stop=(b == NB - 1), skip_group_check=True)
            mm.then_inc(s["s_done"], 1)

        def values(i, tile, k):
            t, j = tile // 4, tile % 4
            near = abs(t - j) <= 1
            wt = w[tile % 2]
            if k == 0:
                pe.wait_ge(s["exp_done"], SLOTS * i + 8 * (tile + 1))
                if j == 0:
                    at_least(pe, "pv_ev", 4 * i + t)
                if j == max(0, t - 1):
                    at_least(pe, "rel_ev", 4 * i + t)
            b2, hh = k // 4, k % 4
            for g in range(4):
                h = 4 * g + hh
                mm = nc.tensor.matmul(pv[b2][32 * g:32 * g + 9, P * hh:P * hh + P], VC[j][:, b2, 0 if near else 1, h, :],
                                      wt[:, b2, :, h].rearrange("p s u b -> p u s b"),
                                      start=(j == 0 and hh == 0), stop=(j == NT - 1), skip_group_check=True)
            if near:
                for q8 in range(NS):
                    z0 = Z_0 + P * (j - t) - NB * q8 - k - 32 * (NU - 1)
                    lv = Rv[:, z0 % 32, z0 // 32:z0 // 32 + NU, :].rearrange("p u d -> p (u d)")
                    mm = nc.tensor.matmul(rel[k // 4][32 * q8:32 * q8 + 32, P * (k % 4):P * (k % 4) + P], lv,
                                          wt[:, :, q8, :, :, k], start=(j == max(0, t - 1) and k % 4 == 0),
                                          stop=(j == min(NT - 1, t + 1)), skip_group_check=True)
            mm.then_inc(s["pv_done"], 1)

        def finish(n, b2, step, mix):
            c = 2 * n + b2
            if step == 0:
                pe.wait_ge(s["O_rdy"], c + 1)
                for t in range(NT):
                    mm = nc.tensor.matmul(mix[:, P * t:P * t + P], oA[:, P * t:P * t + P], woT[:], start=True, stop=True)
                mm.then_inc(s["op_ps"], 1)
            elif step == 1:
                pe.wait_ge(s["xn2_done"], c + 1)
                for t in range(NT):
                    mm = transpose(mix[:, P * t:P * t + P], xs[:, t, 0:D])
                mm.then_inc(s["x2T_ps"], 1)
            else:
                pe.wait_ge(s["x2T_ev"], c + 1)
                for t in range(NT):
                    mm = nc.tensor.matmul(mix[:, E * t:E * t + E], x2T[:, P * t:P * t + P], wrT[:], start=True, stop=True)
                mm.then_inc(s["lg_ps"], 1)

        def turn(i, prev, nxt, nxt2):
            for slot in range(SLOTS):
                scores(i, slot)
                if nxt:
                    wait_for_bank(pe, ("row max", slot), i, prev, nxt, nxt2)
                    natural(i + 1, slot // 64, slot % 64, bank("row max", slot))
                for half in range(2):
                    if (nxt2 if half else nxt) and slot - 64 * half in PREPARE_PE:
                        job = ("prepare", half, PREPARE_PE[slot - 64 * half])
                        wait_for_bank(pe, job, i, prev, nxt, nxt2)
                        prep(i + 1 + half, 1 - half, job[2], bank(*job))
                if slot >= 8:
                    values(i, slot // 8 - 1, slot % 8)
                elif prev:
                    values(i - 1, 15, slot)
                for b2 in range(2):
                    if prev and slot - FINISH[b2] in FINISH_PE:
                        job = ("finish", b2, FINISH_PE[slot - FINISH[b2]])
                        wait_for_bank(pe, job, i, prev, nxt, nxt2)
                        finish(i - 1, b2, job[2], bank(*job))

        def prologue(n, b2, mix):
            c = 2 * n + b2
            for step in range(4):
                if step == 2:
                    pe.wait_ge(s["q_ev"], c + 1)
                if step == 3:
                    pe.wait_ge(s["k_read"], c + 1)
                prep(n, b2, step, mix)

        prologue(0, 0, mix[0])
        prologue(0, 1, mix[1])
        pe.wait_ge(s["sp_set"], 16 * TABLE_LOADS)
        pe.wait_ge(s["zeroed"], ZEROED)
        pe.wait_ge(s["v_ev"], 2)
        for k in range(128):
            at_least(pe, "mx_done", k - 3)
            natural(0, k // 64, k % 64, (*mix, *sc)[k % 4])
        pe.wait_ge(s["mx_done"], 128)
        prologue(1, 0, mix[0])
        pe.wait_ge(s["v_ev"], 3)
        turns(pe, turn)
        for k in range(8):
            values(NP - 1, 15, k)
        for b2 in range(2):
            for step in range(3):
                if step == 0:
                    pe.wait_ge(s["lg_ev"], 2 * (NP - 1) + b2)
                finish(NP - 1, b2, step, mix[0])

    @block.scalar
    def _(act):
        act.wait_ge(s["pe_set"], 1)
        for dst, src in ((wqT, sc[0][:, 0:P]), (wkT, sc[0][:, P:2 * P]), (wvT, sc[0][:, 2 * P:3 * P]), (woT, sc[0][:, 3 * P:4 * P]),
                         (sgu, sc[1][:]), (sdn, mix[0][:, 0:2 * P]), (wrT, mix[1][:, 0:E])):
            view = dst[:].rearrange("p a b -> p (a b)") if len(dst.shape) == 3 else dst[:]
            last_copy = nc.scalar.copy(view, src)
        last_copy.then_inc(s["act_set"], 1)
        act.wait_ge(s["dve_set"], DVE_SET_DONE)

        def prep(n, b2, step, mix):
            c = 2 * n + b2
            if step == 0:
                act.wait_ge(s["xT_ps"], c + 1)
                at_least(act, "v_ps", c)
                nc.scalar.copy(xnT[:], mix[:]).then_inc(s["xnT_rdy"], 1)
            elif step == 1:
                act.wait_ge(s["q_ps"], c + 1)
                at_least(act, "qsplit", 3 * c - 1)
                nc.scalar.activation(qf[:], mix[:], ACT.Identity, bias=bq_s[:, 0:1]).then_inc(s["q_ev"], 1)
            elif step == 2:
                act.wait_ge(s["k_ps"], c + 1)
                at_least(act, "ksplit", 2 * c)
                nc.scalar.activation(kf[:, 0, :], mix[:], ACT.Identity, bias=kb[:, 0:1]).then_inc(s["k_read"], 1)
            elif step == 3:
                act.wait_ge(s["k_read"], c + 1)
                at_least(act, "nat_ps", 64 * (c - 1))
                nc.scalar.copy(kn[b2][:, 0, :], kf[:, 0, :])
                for v in (1, 2):
                    nc.scalar.activation(kn[b2][:, v, :], kf[:, 0, :], ACT.Identity, bias=kb[:, v:v + 1])
            else:
                nc.scalar.activation(kf[:, 1, 0:S // 2], kf[:, 0, 0:S // 2], ACT.Identity, bias=kb[:, 1:2])
                nc.scalar.activation(kf[:, 1, S // 2:S], kf[:, 0, S // 2:S], ACT.Identity, bias=kb[:, 2:3]).then_inc(s["k_ev"], 1)

        def by_head(n, b2, half, heads):
            c = 2 * n + b2
            if heads[0] == 0:
                act.wait_ge(s["qsplit"], 3 * c + 3)
                at_least(act, "nat_ps", 64 * (c - 1) + 32 * (half + 1))
            src = qp[b2][:, :, 2 * half:2 * half + 2, :]
            for h in heads:
                ins = nc.scalar.activation(Qb[half][:, :, h, :].rearrange("p e (t b) -> p e t b", t=2), src, ACT.Copy, scale=hmask[:, h:h + 1])
            if heads[-1] == H - 1:
                ins.then_inc(s["qb_done"], 1)

        def exponentials(i, slot):
            tile = slot // 8
            act.wait_ge(s["s_done"], SLOTS * i + slot + 1)
            if slot % 8 == 0:
                at_least(act, "pv_done", SLOTS * i + 8 * (tile - 1))
            nc.scalar.activation(w[tile % 2][:, slot // 4 % 2, slot % 4].rearrange("p h u b -> p (h u b)"), sc[slot % 2][:], ACT.Exp,
                                 scale=escale[:, 0:1]).then_inc(s["exp_done"], 1)

        def outputs(n, t):
            act.wait_ge(s["pv_done"], SLOTS * n + 32 * (t + 1))
            at_least(act, "o_st", O_STORES * (NT * n + t))
            nc.scalar.copy(pv_s[:, 0].rearrange("p h q -> p (h q)"), pv[0][:])
            nc.scalar.copy(pv_s[:, 1].rearrange("p h q -> p (h q)"), pv[1][:]).then_inc(s["pv_ev"], 1)

        def finish(n, b2, step, mix):
            c = 2 * n + b2
            if step == 0:
                act.wait_ge(s["x2T_ps"], c + 1)
                at_least(act, "lg_ps", c)
                nc.scalar.copy(x2T[:], mix[:]).then_inc(s["x2T_ev"], 1)
            else:
                act.wait_ge(s["lg_ev"], c + 1)
                nc.scalar.activation(sg[:], lmax[:], ACT.Exp, scale=-1.0).then_inc(s["sg_done"], 1)

        prep_at = {7: 0, 10: 1, 13: 2, 14: 3, 15: 4}
        finish_at = {24: 0, 30: 1}

        def turn(i, prev, nxt, nxt2):
            for slot in range(SLOTS):
                exponentials(i, slot)
                if slot % 32 == 7:
                    if slot > 32:
                        outputs(i, slot // 32 - 1)
                    elif prev:
                        outputs(i - 1, NT - 1)
                for half in range(2):
                    if (nxt2 if half else nxt) and slot - 64 * half in prep_at:
                        step = prep_at[slot - 64 * half]
                        prep(i + 1 + half, 1 - half, step, bank("prepare", half, min(step, 2)))
                head = slot % 32 - 1
                if 0 <= head < H:
                    ahead = slot // 32 + 1
                    if ahead < 4 and nxt:
                        by_head(i + 1, ahead // 2, ahead % 2, (head,))
                    if ahead == 4 and nxt2:
                        by_head(i + 2, 0, 0, (head,))
                for b2 in range(2):
                    if prev and slot - FINISH[b2] in finish_at:
                        finish(i - 1, b2, finish_at[slot - FINISH[b2]], bank("finish", b2, 1))

        for b2 in range(2):
            for step in range(5):
                prep(0, b2, step, mix[b2])
        for b2 in range(2):
            for half in range(2):
                by_head(0, b2, half, range(H))
        for step in range(5):
            prep(1, 0, step, mix[0])
        by_head(1, 0, 0, range(H))
        turns(act, turn)
        outputs(NP - 1, NT - 1)
        for b2 in range(2):
            for step in range(2):
                finish(NP - 1, b2, step, mix[0])

    @block.vector
    def _(dve):
        count = [0]

        def link(ins):
            count[0] += 1
            ins.then_inc(s["dve_set"], 1)
            dve.wait_ge(s["dve_set"], count[0])

        dve.wait_ge(s["w_ld"], 16 * LOADS)
        link(nc.vector.memset(bnd[:], 0.0))
        for n, bias in ((0, bqr), (1, bkr[:, 0:1])):
            link(nc.vector.tensor_reduce(bnd[:, 4:5], wraw[n], AX.X, ALU.add, apply_absolute_value=True))
            link(nc.vector.tensor_reduce(bnd[:, 5:6], bias, AX.X, ALU.max, apply_absolute_value=True))
            link(nc.vector.scalar_tensor_tensor(out=bnd[:, n:n + 1], in0=bnd[:, 4:5], scalar=XMAX, in1=bnd[:, 5:6],
                                                op0=ALU.mult, op1=ALU.add))
        link(nc.vector.tensor_reduce(bnd[0:HD, 2:3], rkT, AX.X, ALU.max, apply_absolute_value=True))
        assert count[0] == BOUNDS
        dve.wait_ge(s["pool_set"], BOUNDS_MAX)
        link(nc.vector.tensor_copy(bnd[:, 4:5], bmax[:, 0:1]))
        link(nc.vector.tensor_tensor(bnd[:, 5:6], bmax[:, 1:2], bmax[:, 2:3], ALU.add))
        link(nc.vector.tensor_scalar(bnd[:, 6:8], bnd[:, 4:6], 2.0 ** -100, 2.0 ** 100, ALU.max, ALU.min))
        link(nc.vector.tensor_scalar(pw[:, 0:2].bitcast(I32), bnd[:, 6:8].bitcast(I32), 0x7F800000, None, ALU.bitwise_and))
        link(nc.vector.tensor_scalar(pw[:, 2:4].bitcast(I32), pw[:, 0:2].bitcast(I32), -1.0, float(266 << 23), ALU.mult, ALU.add))
        link(nc.vector.tensor_scalar(wraw[0], wraw[0], pw[:, 2:3], None, ALU.mult))
        link(nc.vector.tensor_scalar(wraw[1], wraw[1], pw[:, 3:4], None, ALU.mult))
        assert count[0] == SCALED
        link(nc.vector.tensor_scalar(rkT, rkT, pw[0:HD, 3:4], None, ALU.mult))
        link(nc.vector.memset(rzero, 0.0))
        link(nc.vector.tensor_scalar(rpad[:, 0:OFF0 - M], rzero[:, 0:OFF0 - M], rkT[:, 0:1], None, ALU.add))
        link(nc.vector.tensor_copy(rpad[:, OFF0 - M:OFF0 + M + 1], rkT))
        link(nc.vector.tensor_scalar(rpad[:, OFF0 + M + 1:512], rzero[:, 0:512 - OFF0 - M - 1], rkT[:, 2 * M:2 * M + 1], None, ALU.add))
        link(nc.vector.tensor_copy(rpart[0], rpad))
        link(nc.vector.tensor_tensor(rpart[1], rpad, rpart[0], ALU.subtract))
        assert count[0] == RPART_READY
        link(nc.vector.tensor_scalar(bq_s[:], bqr, pw[:, 2:3], None, ALU.mult))
        link(nc.vector.tensor_scalar(kb[:, 0:1], bkr[:, 0:1], pw[:, 3:4], None, ALU.mult))
        link(nc.vector.tensor_scalar(kb[:, 1:3], bkr[:, 1:3], pw[:, 3:4], None, ALU.mult))
        link(nc.vector.tensor_tensor(bnd[:, 3:4], pw[:, 2:3], pw[:, 3:4], ALU.mult))
        link(nc.vector.reciprocal(bnd[:, 4:5], bnd[:, 3:4]))
        link(nc.vector.tensor_scalar(escale[:], bnd[:, 4:5], HD ** -0.5, None, ALU.mult))
        link(nc.vector.tensor_copy(vb[:, 0, :], vraw[:, 0, :]))
        for n in (1, 2):
            link(nc.vector.tensor_tensor(vb[:, n, :], vraw[:, 0, :], vraw[:, n, :], ALU.add))
        link(nc.vector.tensor_copy(number[:], number_i[:]))
        for out_bank in (*pv, *rel):
            link(nc.vector.memset(out_bank[:], 0.0))
        assert count[0] == DVE_SET_DONE

        def moments(src, stats, mean_var, half, rs, base, step):
            for t in range(NT):
                ins = nc.vector.bn_stats(stats[:, t, :], src[:, t, :])
            ins.then_inc(s[step], 1)
            dve.wait_ge(s[step], base + 1)
            dve.sem_inc(s["dve_passed"], 1)
            for t in range(NT):
                ins = nc.vector.bn_aggr(mean_var[:, t, :], stats[:, t, :])
            ins.then_inc(s[step], 1)
            dve.wait_ge(s[step], base + 2)
            root_guess(nc, dve, s[step], base + 2, mean_var, half, rs)

        def normalize(dst, src, mean_var, rs, root, roots):
            dve.wait_ge(s[root], ROOT_STEPS * (roots + 1))
            for t in range(NT):
                ins = nc.vector.tensor_scalar(dst[:, t, :], src[:, t, :], mean_var[:, t, 0:1], rs[:, t:t + 1], ALU.subtract, ALU.mult)
            return ins

        def prep(n, b2, step, mix=None):
            c = 2 * n + b2
            if step == 0:
                dve.wait_ge(x_ld[b2], 16 * (n + 1))
                moments(xt[b2], st, mv, var, rstd, 5 * c, "xn_step")
            elif step == 1:
                at_least(dve, "xT_ps", c)
                normalize(xn, xt[b2], mv, rstd, "root", c).then_inc(s["xn_done"], 1)
            else:
                dve.wait_ge(s["v_ps"], c + 1)
                at_least(dve, "vs_st", 16 * c)
                src = mix[:].rearrange("p (t h d) -> p t h d", t=NT, h=H)
                for v, tiles, far in ((0, slice(0, NT), 0), (1, slice(0, 2), 1), (2, slice(2, NT), 1)):
                    nt = tiles.stop - tiles.start
                    bias = vb[:, v:v + 1, :].rearrange("p o (h d) -> p o h d", d=HD).broadcast_to([P, nt, H, HD])
                    ins = nc.vector.tensor_tensor(vst[:, tiles, far, :, 0:HD], src[:, tiles], bias, ALU.add)
                ins.then_inc(s["v_ev"], 1)

        def row_max(n, b2, k, nat):
            c = 2 * n + b2
            t = k // 16
            if k % 16 == 0:
                at_least(dve, "ms_done", NT * (c - 1) + t + 1)
            dve.wait_ge(s["nat_ps"], 64 * c + k + 1)
            nc.vector.tensor_reduce(mx[:, k:k + 1], nat[:], AX.X, ALU.max).then_inc(s["mx_done"], 1)
            if k % 16 == 15:
                group = NT * c + t
                cols = slice(16 * t, 16 * t + 16)
                dve.wait_ge(s["mx_done"], 64 * c + k + 1)
                at_least(dve, "ms_st", 32 * (group - NT + 1))
                nc.vector.tensor_scalar(ms[:, 0, cols], mx[:, cols], MAXSCALE, None, ALU.mult).then_inc(s["ms_step"], 1)
                dve.wait_ge(s["ms_step"], group + 1)
                nc.vector.scalar_tensor_tensor(out=ms[:, 1, cols], in0=mx[:, cols], scalar=MAXSCALE, in1=ms[:, 0, cols],
                                               op0=ALU.mult, op1=ALU.subtract).then_inc(s["ms_done"], 1)

        def outputs(n, t):
            dve.wait_ge(s["pv_done"], SLOTS * n + 32 * (t + 1))
            at_least(dve, "o_st", O_STORES * (NT * n + t))
            for half in range(2):
                ins = nc.vector.tensor_copy(rel_s[:, :, :, 4 * half:4 * half + 4].rearrange("p h u b -> p (h u) b"),
                                            rel[half][:].rearrange("p (b c) -> p c b", b=4))
            ins.then_inc(s["rel_ev"], 1)

        def finish(n, b2, step, mix):
            c = 2 * n + b2
            base = 12 * c
            if step == 0:
                dve.wait_ge(s["o_ld"], 64 * (c + 1))
                nc.vector.tensor_tensor(oA[:], oA[:], oB[:], ALU.add).then_inc(s["o_step"], 1)
            elif step < 5:
                cols = slice(P * (step - 1), P * step)
                ins = nc.vector.reciprocal(oS[:, cols], oS[:, cols])
                if step == 4:
                    ins.then_inc(s["o_step"], 1)
            elif step == 5:
                dve.wait_ge(s["o_step"], 2 * c + 2)
                nc.vector.tensor_tensor(oA[:], oA[:], oS[:], ALU.mult).then_inc(s["O_rdy"], 1)
            elif step == 6:
                dve.wait_ge(s["op_ps"], c + 1)
                nc.vector.tensor_tensor(y[:], mix[:].rearrange("p (t d) -> p t d", t=NT),
                                        bo_s[:].rearrange("p (o d) -> p o d", o=1).broadcast_to([P, NT, D]), ALU.add).then_inc(s["ln_step"], 1)
                dve.wait_ge(s["ln_step"], base + 1)
                moments(y, st2, mv2, var2, rstd2, base + 1, "ln_step")
            elif step == 7:
                normalize(y, y, mv2, rstd2, "root2", 2 * c).then_inc(s["ln_step"], 1)
                dve.wait_ge(s["ln_step"], base + 7)
                at_least(dve, "xs_st", 32 * c)
                nc.vector.tensor_tensor(xs[:, :, HALF:HALF + D], xr[:], y[:], ALU.add).then_inc(s["x1_done"], 1)
                dve.wait_ge(s["x1_done"], c + 1)
                moments(xs[:, :, HALF:HALF + D], st2, mv2, var2, rstd2, base + 7, "ln_step")
            elif step == 8:
                normalize(xs[:, :, 0:D], xs[:, :, HALF:HALF + D], mv2, rstd2, "root2", 2 * c + 1).then_inc(s["xn2_done"], 1)
            elif step == 9:
                dve.wait_ge(s["lg_ps"], c + 1)
                base = 4 * c
                lps = mix[:, 0:NT * E].rearrange("p (t e) -> p t e", t=NT)
                nc.vector.tensor_copy(lg[:], lps).then_inc(s["top_step"], 1)
                dve.wait_ge(s["top_step"], base + 1)
                nc.vector.tensor_reduce(lmax[:], lg[:], AX.X, ALU.max).then_inc(s["lg_ev"], 1)
                dve.wait_ge(s["lg_ev"], c + 1)
                nc.vector.tensor_tensor(cand[:], lg[:], lmax[:].rearrange("p (t o) -> p t o", o=1).broadcast_to([P, NT, E]), ALU.is_ge).then_inc(s["top_step"], 1)
                dve.wait_ge(s["top_step"], base + 2)
                iota = iota_e[:].rearrange("p (o e) -> p o e", o=1).broadcast_to([P, NT, E])
                nc.vector.tensor_tensor(cand[:], cand[:], iota, ALU.mult).then_inc(s["top_step"], 1)
                dve.wait_ge(s["top_step"], base + 3)
                nc.vector.tensor_reduce(lidx[:], cand[:], AX.X, ALU.min).then_inc(s["top_step"], 1)
                dve.wait_ge(s["top_step"], base + 4)
                nc.vector.tensor_tensor(oh[:], iota, lidx[:].rearrange("p (t o) -> p t o", o=1).broadcast_to([P, NT, E]), ALU.is_equal)
            else:
                dve.wait_ge(s["sg_done"], c + 1)
                nc.vector.tensor_scalar(sg[:], sg[:], 1.0, None, ALU.add).then_inc(s["sg_step"], 1)
                dve.wait_ge(s["sg_step"], c + 1)
                nc.vector.reciprocal(xs[:, :, D], sg[:])
                at_least(dve, "number_step", c)
                nc.vector.tensor_copy(xs[:, :, 2 * D + 1], number[:]).then_inc(s["xs_done"], 1)
                dve.wait_ge(s["xs_done"], c + 1)
                nc.vector.tensor_scalar(number[:], number[:], float(S), None, ALU.add).then_inc(s["number_step"], 1)

        prep_at = {0: 0, 4: 1, 18: 2}
        finish_at = {4: 0, 5: 1, 6: 2, 7: 3, 8: 4, 9: 5, 12: 6, 17: 7, 21: 8, 27: 9, 32: 10}

        def turn(i, prev, nxt, nxt2):
            for slot in range(SLOTS):
                if slot % 32 == 8:
                    if slot > 32:
                        outputs(i, slot // 32 - 1)
                    elif prev:
                        outputs(i - 1, NT - 1)
                if nxt:
                    row_max(i + 1, slot // 64, slot % 64, bank("row max", slot))
                for half in range(2):
                    if (nxt2 if half else nxt) and slot - 64 * half in prep_at:
                        prep(i + 1 + half, 1 - half, prep_at[slot - 64 * half], bank("prepare", half, 3))
                for b2 in range(2):
                    if prev and slot - FINISH[b2] in finish_at:
                        step = finish_at[slot - FINISH[b2]]
                        finish(i - 1, b2, step, bank("finish", b2, 0 if step == 6 else 2))

        prep(0, 0, 0)
        prep(0, 0, 1)
        prep(0, 1, 0)
        prep(0, 1, 1)
        dve.wait_ge(s["zeroed"], ZEROED)
        prep(0, 0, 2, mix[0])
        prep(0, 1, 2, mix[1])
        prep(1, 0, 0)
        for k in range(128):
            row_max(0, k // 64, k % 64, (*mix, *sc)[k % 4])
        prep(1, 0, 1)
        prep(1, 0, 2, mix[0])
        turns(dve, turn)
        outputs(NP - 1, NT - 1)
        for b2 in range(2):
            for step in finish_at.values():
                finish(NP - 1, b2, step, mix[0])

    @block.gpsimd
    def _(pool):
        ps_ = s["pool_set"]
        pool.memset(ident[:], 0.0).then_inc(ps_, 1)
        pool.memset(ones[:], 1.0).then_inc(ps_, 1)
        pool.wait_ge(ps_, 2)
        pool.affine_select(out=ident[:], in_=ident[:], compare_op=ALU.not_equal, fill=1.0, base=0,
                           pattern=[[-1, P]], channel_multiplier=1).then_inc(ps_, 1)
        pool.affine_select(out=tri[:], in_=ones[:], compare_op=ALU.is_gt, fill=0.0, base=0,
                           pattern=[[1, P]], channel_multiplier=-1).then_inc(ps_, 1)
        pool.affine_select(out=hmask[:], in_=ones[:, 0:H], compare_op=ALU.is_ge, fill=0.0, base=0,
                           pattern=[[-HD, H]], channel_multiplier=1).then_inc(ps_, 1)
        pool.wait_ge(ps_, 5)
        pool.affine_select(out=hmask[:], in_=hmask[:], compare_op=ALU.is_ge, fill=0.0, base=HD - 1,
                           pattern=[[HD, H]], channel_multiplier=-1).then_inc(ps_, 1)
        pool.iota(number_i[:], [[P, NT]], base=1, channel_multiplier=1).then_inc(ps_, 1)
        pool.wait_ge(s["dve_set"], BOUNDS)
        for n in range(3):
            pool.partition_all_reduce(bmax[:, n:n + 1], bnd[:, n:n + 1], P, bass.bass_isa.ReduceOp.max).then_inc(ps_, 1)
        z = s["zeroed"]
        for buf in (*QC, *QT, Qn):
            flat = buf[:].rearrange({5: "p a b c d -> p (a b c d)", 4: "p a b c -> p (a b c)", 3: "p a b -> p (a b)"}[len(buf.shape)])
            pool.memset(flat.bitcast(F32), 0.0).then_inc(z, 1)
        for j in range(NT):
            pool.memset(KC[j][:].rearrange("p a b c d -> p (a b c d)"), -1.0 / MAXSCALE).then_inc(z, 1)
        pool.memset(vst[:, :, :, :, HD:HD + 1].rearrange("p a b c o -> p (a b) (c o)"), 1.0).then_inc(z, 1)
        pool.memset(zrow[:], 0.0).then_inc(z, 1)
        pool.memset(c15[:], 1.5).then_inc(z, 1)
        for e in range(E):
            pool.memset(iota_e[:, e:e + 1], float(e - E)).then_inc(z, 1)

        def split(n, b2):
            c = 2 * n + b2
            pool.wait_ge(s["q_ev"], c + 1)
            at_least(pool, "qs_st", 48 * c)
            at_least(pool, "qn_st", 16 * (c - 1))
            at_least(pool, "qb_done", 2 * (c - 1))
            pool.sem_inc(s["pool_passed"], 1)
            pool.tensor_copy(qs[:, 0, :], qf[:]).then_inc(s["qsplit"], 1)
            pool.wait_ge(s["qsplit"], 3 * c + 1)
            pool.tensor_tensor(qs[:, 1, :], qf[:], qs[:, 0, :], ALU.subtract).then_inc(s["qsplit"], 1)
            pool.tensor_copy(qp[b2][:], qs[:, 0, :].rearrange("p (t e b) -> p e t b", t=NT, e=NE8)).then_inc(s["qsplit"], 1)
            pool.wait_ge(s["k_ev"], c + 1)
            at_least(pool, "ks_st", 48 * c)
            pool.sem_inc(s["pool_passed"], 1)
            src = kf[:].rearrange("p v (t k) -> p t v k", t=NT)
            pool.tensor_copy(ks[:, 0], src).then_inc(s["ksplit"], 1)
            pool.wait_ge(s["ksplit"], 2 * c + 1)
            pool.tensor_tensor(ks[:, 1], src, ks[:, 0], ALU.subtract).then_inc(s["ksplit"], 1)

        def refine(root, ve, tmp, name, n):
            done = ROOT_STEPS * n

            def step(k, ins):
                ins.then_inc(s[name], 1)
                pool.wait_ge(s[name], done + k + 1)
            newton(pool, step, root, ve, tmp, c15)

        def root(n, b2):
            c = 2 * n + b2
            pool.wait_ge(s["xn_step"], 5 * c + 5)
            refine(rstd, var, rtmp, "root", c)

        def roots2(n, b2):
            c = 2 * n + b2
            for k, done in enumerate((12 * c + 6, 12 * c + 12)):
                pool.wait_ge(s["ln_step"], done)
                refine(rstd2, var2, rtmp2, "root2", 2 * c + k)

        def prepare(n, b2):
            root(n, b2)
            split(n, b2)

        def turn(i, prev, nxt, nxt2):
            if nxt:
                prepare(i + 1, 1)
            if prev:
                roots2(i - 1, 0)
            if nxt2:
                prepare(i + 2, 0)
            if prev:
                roots2(i - 1, 1)

        root(0, 0)
        root(0, 1)
        pool.wait_ge(s["sp_set"], 16 * TABLE_LOADS)
        split(0, 0)
        split(0, 1)
        prepare(1, 0)
        turns(pool, turn)
        for b2 in range(2):
            roots2(NP - 1, b2)


IDENT_READY = 3
BOUNDS = 8
BOUNDS_MAX = 10
SCALED = BOUNDS + 7
RPART_READY = SCALED + 7
DVE_SET_DONE = RPART_READY + 3 + 3 + 3 + 1 + 4
ZEROED = 5 + NT + 3 + E
MS_STORES = 16 * 2 * NT
ROOT_STEPS = 12
QN_LOADS = 16 * NE8
QC_LOADS = 16 * 8
KC_LOADS = 16 * 5
O_STORES = 16 * (8 + 16)
TABLE_LOADS = Z_W // 32 + NU * 3 + 2 * NE8
ZERO_TILES = 16
PREPARE_PE = {6: 0, 9: 1, 12: 2, 17: 3}
FINISH_PE = {11: 0, 23: 1, 26: 2}
FINISH = (24, 88)


MOE_SEMS = ("w_ld2 oh_ld cnt_ps cnt_step slot_rdy eid_rdy iotas xn_ld0 xn_ld1 xn_ld2 xn_ld3 idx scat0 scat1 scat2 scat3 "
            "xs_ld0 xs_ld1 x1_ld0 x1_ld1 sx_done sT_ps sT_ev we_done gu_ps silu_done h_done y_ps y_ev "
            "dve_passed2 pool_passed2 fin_step root3 oidx_step oidx_rdy out_rdy out_st0 out_st1")
RING = 4
GROUP = 4
GROUPS = SORTED // GROUP
ROW = 2 * D + 2
HALF = D + 1
NOWHERE = 1 << 20


def expert_phase(nc, ctx, a):
    s = a["moe_sem"]
    xn_d, oh_d, xs_d, out = (a[n] for n in "xn_d oh_d xs_d out".split())
    gate_up, down = a["gate_up"], a["down"]
    ident, sgu, sdn, tri, ones, c15 = (a[n] for n in "ident sgu sdn tri ones c15".split())

    def sb(name, shape, dt=F32):
        return ctx.enter_context(nc.sbuf_tensor(name, shape, dt))

    def pb(name, shape, dt=F32):
        return ctx.enter_context(nc.psum_tensor(name, shape, dt))

    WE = sb("WE", [P, E, 2 * F + 2 * D])
    OH = sb("OH", [P, TILES, E])
    rank = sb("rank", [P, TILES, E])
    tot = sb("tot", [P, TILES, E])
    pref = [sb(f"pref{r}", [P, TILES, E]) for r in range(2)]
    ntile = sb("ntile", [P, E])
    ntile_i = sb("ntile_i", [P, E], I32)
    end = [sb(f"end{r}", [P, E]) for r in range(2)]
    start = sb("start", [P, E])
    slot_f = sb("slot_f", [P, TILES])
    slot_u = sb("slot_u", [P, TILES], U32)
    tau_i = sb("tau_i", [1, SORTED], I32)
    tau = sb("tau", [1, SORTED])
    pad_i = sb("pad_i", [P, GROUP], I32)
    pad = sb("pad", [P, GROUP])
    past = sb("past", [1, SORTED, E])
    eid_f = sb("eid_f", [1, SORTED])
    eid = sb("eid", [1, SORTED], I32)
    xrow = [sb(f"xrow{r}", [P, ROW]) for r in range(RING)]
    idx = [sb(f"idx{r}", [P, 1], U32) for r in range(RING)]
    srow = [sb(f"srow{r}", [P, GROUP, HALF]) for r in range(2)]
    x1g = [sb(f"x1g{r}", [P, GROUP, HALF]) for r in range(2)]
    sx = [sb(f"sx{r}", [P, D]) for r in range(2)]
    sT = [sb(f"sT{r}", [P, 2, P]) for r in range(2)]
    we = [sb(f"we{r}", [P, 2 * F + 2 * D]) for r in range(2)]
    act_s = [sb(f"act_s{r}", [P, 4, P]) for r in range(2)]
    hT = [sb(f"hT{r}", [P, 4, P]) for r in range(2)]
    yg = [sb(f"yg{r}", [P, GROUP, D]) for r in range(2)]
    st3 = sb("st3", [P, GROUP, 6])
    mv3 = sb("mv3", [P, GROUP, 2])
    var3, rstd3, rtmp3 = (sb(n, [P, GROUP]) for n in ("var3", "rstd3", "rtmp3"))
    og = [sb(f"og{r}", [P, GROUP, D]) for r in range(2)]
    oidx_f = [sb(f"oidx_f{r}", [P, GROUP]) for r in range(2)]
    oidx = [sb(f"oidx{r}", [P, GROUP], U32) for r in range(2)]

    gate = [pb(f"gate{r}", [P, 4, P]) for r in range(2)]
    up = [pb(f"up{r}", [P, 4, P]) for r in range(2)]
    tr = [pb(f"tr{r}", [P, 2, P]) for r in range(2)]
    y_p = [pb(f"y_p{r}", [P, D]) for r in range(2)]

    def ring(name, n):
        return [s[f"{name}{r}"] for r in range(n)]

    xn_ld, scat, xs_ld, x1_ld, out_st = ring("xn_ld", RING), ring("scat", RING), ring("xs_ld", 2), ring("x1_ld", 2), ring("out_st", 2)

    def at_least(eng, semaphore, value):
        if not (isinstance(value, int) and value <= 0):
            eng.wait_ge(semaphore, value)

    def loop(eng, body):
        body(0, True, False)
        with eng.Fori(1, GROUPS // 2 - 1) as i:
            body(i, False, False)
        body(GROUPS // 2 - 1, False, True)

    block = ctx.enter_context(nc.Block())

    @block.sync
    def _(sp):
        sp.dma_start(OH[:].rearrange("p (c t) e -> p c (t e)", t=NT), oh_d.rearrange("c p n -> p c n")).then_inc(s["oh_ld"], 16)

        def load_row(g, k):
            at_least(sp, scat[k], 16 * g)
            sp.dma_start(xrow[k][:], xn_d[bass.ds((RING * g + k) * P, P)]).then_inc(xn_ld[k], 16)

        for k in range(RING):
            load_row(0, k)
        sp.dma_start(WE[:, :, 0:2 * F], gate_up.rearrange("e h f -> h e f")).then_inc(s["w_ld2"], 16)
        for c in range(2):
            sp.dma_start(WE[:, :, 2 * F + D * c:2 * F + D * c + D], down[:, P * c:P * c + P, :].rearrange("e f d -> f e d")).then_inc(s["w_ld2"], 16)
        with sp.Fori(1, TILES // RING) as g:
            for k in range(RING):
                load_row(g, k)
        for k in range(RING):
            sp.wait_ge(scat[k], 16 * (TILES // RING))

        def load_rows(g, r):
            at_least(sp, s["sT_ps"], GROUP * (g - 1))
            src = xs_d[bass.ds(g * GROUP * P, GROUP * P), 0:HALF].rearrange("(k p) n -> p k n", p=P)
            sp.dma_start(srow[r][:], src).then_inc(xs_ld[r], 16)

        def load_x1(g, r):
            at_least(sp, s["out_rdy"], g - 1)
            src = xs_d[bass.ds(g * GROUP * P, GROUP * P), HALF:ROW].rearrange("(k p) n -> p k n", p=P)
            sp.dma_start(x1g[r][:], src).then_inc(x1_ld[r], 16)

        load_rows(0, 0)

        def groups(i, first, last):
            for r in range(2):
                if not (last and r == 1):
                    load_rows(2 * i + r + 1, 1 - r)
                load_x1(2 * i + r, r)
        loop(sp, groups)

    @block.gpsimd
    def _(pool):
        pool.iota(tau_i[:], [[1, SORTED]], base=0, channel_multiplier=0).then_inc(s["iotas"], 1)
        pool.iota(pad_i[:], [[P, GROUP]], base=NOWHERE, channel_multiplier=1).then_inc(s["iotas"], 1)
        pool.wait_ge(s["slot_rdy"], 1)

        def scatter(g, k):
            n = RING * g + k
            at_least(pool, scat[k], 16 * g)
            pool.sem_inc(s["pool_passed2"], 1)
            pool.tensor_copy(idx[k][:], slot_u[:, bass.ds(n, 1)]).then_inc(s["idx"], 1)
            pool.wait_ge(s["idx"], n + 1)
            pool.wait_ge(xn_ld[k], 16 * (g + 1))
            pool.sem_inc(s["pool_passed2"], 1)
            pool.indirect_dma_start(xs_d, bass.IndirectOffsetOnAxis(ap=idx[k][:], axis=0), xrow[k][:], None).then_inc(scat[k], 16)

        for k in range(RING):
            scatter(0, k)
        with pool.Fori(1, TILES // RING) as g:
            for k in range(RING):
                scatter(g, k)

        def refine(g):
            pool.wait_ge(s["fin_step"], 6 * g + 5)

            def step(k, ins):
                ins.then_inc(s["root3"], 1)
                pool.wait_ge(s["root3"], ROOT_STEPS * g + k + 1)
            newton(pool, step, rstd3, var3, rtmp3, c15)

        def store(g, r):
            pool.wait_ge(s["out_rdy"], g + 1)
            pool.wait_ge(s["oidx_rdy"], g + 1)
            pool.sem_inc(s["pool_passed2"], 1)
            for k in range(GROUP):
                pool.indirect_dma_start(out.rearrange("b s d -> (b s) d"), bass.IndirectOffsetOnAxis(ap=oidx[r][:, k:k + 1], axis=0),
                                        og[r][:, k, :], None, bounds_check=TOK - 1, oob_is_err=False).then_inc(out_st[r], 16)

        def groups(i, first, last):
            for r in range(2):
                refine(2 * i + r)
                store(2 * i + r, r)
        loop(pool, groups)
        for r in range(2):
            pool.wait_ge(out_st[r], 16 * GROUP * (GROUPS // 2))

    @block.tensor
    def _(pe):
        pe.wait_ge(s["oh_ld"], 16)
        for half in range(2):
            rhs = OH[:, TILES // 2 * half:TILES // 2 * (half + 1), :].rearrange("p t e -> p (t e)")
            nc.tensor.matmul(gate[half][:].rearrange("p c n -> p (c n)"), tri[:], rhs, start=True, stop=True)
            mm = nc.tensor.matmul(up[half][:].rearrange("p c n -> p (c n)"), ones[:], rhs, start=True, stop=True)
        mm.then_inc(s["cnt_ps"], 1)
        pe.wait_ge(s["eid_rdy"], 1)

        def transposes(n, k, r):
            pe.wait_ge(s["sx_done"], n + 1)
            at_least(pe, s["sT_ev"], n - 1)
            nc.tensor.transpose(tr[k % 2][:, 0, :], srow[r][:, k, 0:D], ident[:])
            nc.tensor.transpose(tr[k % 2][:, 1, :], sx[k % 2][:], ident[:]).then_inc(s["sT_ps"], 1)

        def gates_and_ups(n, k):
            b = k % 2
            pe.wait_ge(s["sT_ev"], n + 1)
            pe.wait_ge(s["we_done"], n + 1)
            at_least(pe, s["h_done"], n - 1)
            for bank, c0 in ((gate, 0), (up, F)):
                for c in range(2):
                    mm = nc.tensor.matmul(bank[b][:, c, :], we[b][:, c0 + P * c:c0 + P * c + P], sT[b][:, 1, :], start=True, stop=True)
                for c in range(2):
                    mm = nc.tensor.matmul(bank[b][:, 2 + c, :], sgu[:, c0 + P * c:c0 + P * c + P], sT[b][:, 0, :], start=True, stop=True)
            mm.then_inc(s["gu_ps"], 1)

        def downs(n, k):
            b = k % 2
            pe.wait_ge(s["h_done"], n + 1)
            at_least(pe, s["y_ev"], n - 1)
            for c in range(2):
                nc.tensor.matmul(y_p[b][:], hT[b][:, c, :], we[b][:, 2 * F + D * c:2 * F + D * c + D], start=(c == 0), stop=False)
            for c in range(2):
                mm = nc.tensor.matmul(y_p[b][:], hT[b][:, 2 + c, :], sdn[:, c, :], start=False, stop=(c == 1))
            mm.then_inc(s["y_ps"], 1)

        transposes(0, 0, 0)

        def groups(i, first, last):
            for m in range(2 * GROUP):
                n = 2 * GROUP * i + m
                if not (last and m == 2 * GROUP - 1):
                    transposes(n + 1, (m + 1) % GROUP, (m + 1) // GROUP % 2)
                gates_and_ups(n, m % GROUP)
                if not (first and m == 0):
                    downs(n - 1, (m - 1) % GROUP)
        loop(pe, groups)
        downs(SORTED - 1, GROUP - 1)

    @block.scalar
    def _(act):
        act.wait_ge(s["w_ld2"], 48)
        act.wait_ge(s["eid_rdy"], 1)

        def weights(n, k):
            at_least(act, s["y_ps"], n - 1)
            e = act.value_load(eid[0:1, bass.ds(n, 1)], min_val=0, max_val=E - 1)
            nc.scalar.copy(we[k % 2][:], WE[:, bass.ds(e, 1), :].rearrange("p o n -> p (o n)")).then_inc(s["we_done"], 1)

        def copy_rows(n, k):
            act.wait_ge(s["sT_ps"], n + 1)
            at_least(act, s["gu_ps"], n - 1)
            nc.scalar.copy(sT[k % 2][:], tr[k % 2][:]).then_inc(s["sT_ev"], 1)

        def silu(n, k):
            act.wait_ge(s["gu_ps"], n + 1)
            at_least(act, s["h_done"], n - 1)
            nc.scalar.activation(act_s[k % 2][:], gate[k % 2][:], ACT.Silu).then_inc(s["silu_done"], 1)

        def copy_y(n, k, r):
            act.wait_ge(s["y_ps"], n + 1)
            nc.scalar.copy(yg[r][:, k, :], y_p[k % 2][:]).then_inc(s["y_ev"], 1)

        weights(0, 0)
        weights(1, 1)
        copy_rows(0, 0)

        def groups(i, first, last):
            for m in range(2 * GROUP):
                n = 2 * GROUP * i + m
                if not (last and m == 2 * GROUP - 1):
                    copy_rows(n + 1, (m + 1) % GROUP)
                silu(n, m % GROUP)
                if not (first and m == 0):
                    k, r = (m - 1) % GROUP, (m - 1) // GROUP % 2
                    if k == 0:
                        at_least(act, s["out_rdy"], 2 * i + r - 1)
                    copy_y(n - 1, k, r)
                if not (first and m == 0) and not (last and m == 2 * GROUP - 1):
                    weights(n + 1, (m + 1) % GROUP)

        loop(act, groups)
        copy_y(SORTED - 1, GROUP - 1, 1)

    @block.vector
    def _(dve):
        count = [0]

        def link(ins):
            count[0] += 1
            ins.then_inc(s["cnt_step"], 1)
            dve.wait_ge(s["cnt_step"], count[0])

        dve.wait_ge(s["oh_ld"], 16)
        dve.wait_ge(s["cnt_ps"], 1)
        half = TILES // 2
        for c in range(2):
            nc.vector.tensor_copy(rank[:, half * c:half * (c + 1), :].rearrange("p t e -> p (t e)"), gate[c][:].rearrange("p c n -> p (c n)"))
            link(nc.vector.tensor_copy(tot[:, half * c:half * (c + 1), :].rearrange("p t e -> p (t e)"), up[c][:].rearrange("p c n -> p (c n)")))
        src, step, flip = tot, 1, 0
        while step < TILES:
            dst = pref[flip]
            nc.vector.tensor_copy(dst[:, 0:step, :], src[:, 0:step, :])
            link(nc.vector.tensor_tensor(dst[:, step:, :], src[:, step:, :], src[:, 0:TILES - step, :], ALU.add))
            src, step, flip = dst, 2 * step, 1 - flip
        total = src
        link(nc.vector.tensor_scalar(ntile[:], total[:, TILES - 1, :], float(P - 1), None, ALU.add))
        link(nc.vector.tensor_copy(ntile_i[:], ntile[:]))
        link(nc.vector.tensor_scalar(ntile_i[:], ntile_i[:], P.bit_length() - 1, None, ALU.logical_shift_right))
        link(nc.vector.tensor_copy(ntile[:], ntile_i[:]))
        src_e, step, flip_e = ntile, 1, 0
        while step < E:
            dst_e = end[flip_e]
            nc.vector.tensor_copy(dst_e[:, 0:step], src_e[:, 0:step])
            link(nc.vector.tensor_tensor(dst_e[:, step:], src_e[:, step:], src_e[:, 0:E - step], ALU.add))
            src_e, step, flip_e = dst_e, 2 * step, 1 - flip_e
        ends = src_e
        link(nc.vector.tensor_tensor(start[:], ends[:], ntile[:], ALU.subtract))
        link(nc.vector.tensor_scalar(start[:], start[:], float(P), None, ALU.mult))
        link(nc.vector.tensor_tensor(tot[:], total[:], tot[:], ALU.subtract))
        link(nc.vector.tensor_tensor(tot[:], tot[:], rank[:], ALU.add))
        link(nc.vector.tensor_tensor(tot[:], tot[:], start[:].rearrange("p (o e) -> p o e", o=1).broadcast_to([P, TILES, E]), ALU.add))
        link(nc.vector.tensor_tensor(tot[:], tot[:], OH[:], ALU.mult))
        link(nc.vector.tensor_reduce(slot_f[:], tot[:], AX.X, ALU.add))
        nc.vector.tensor_copy(slot_u[:], slot_f[:]).then_inc(s["slot_rdy"], 1)
        dve.wait_ge(s["iotas"], 2)
        link(nc.vector.tensor_copy(pad[:], pad_i[:]))
        link(nc.vector.tensor_copy(tau[:], tau_i[:]))
        link(nc.vector.tensor_tensor(past[:], ends[0:1, :].rearrange("p (o e) -> p o e", o=1).broadcast_to([1, SORTED, E]),
                                     tau[:].rearrange("p (t o) -> p t o", o=1).broadcast_to([1, SORTED, E]), ALU.is_le))
        link(nc.vector.tensor_reduce(eid_f[:], past[:], AX.X, ALU.add))
        link(nc.vector.tensor_scalar(eid_f[:], eid_f[:], float(E - 1), None, ALU.min))
        nc.vector.tensor_copy(eid[:], eid_f[:]).then_inc(s["eid_rdy"], 1)

        def scaled(n, k, r, i):
            if k == 0:
                dve.wait_ge(xs_ld[r], 16 * (i + 1))
            at_least(dve, s["sT_ps"], n - 1)
            nc.vector.tensor_scalar(sx[k % 2][:], srow[r][:, k, 0:D], srow[r][:, k, D:D + 1], None, ALU.mult).then_inc(s["sx_done"], 1)

        def places(g, r):
            num = x1g[r][:, :, D]
            dve.wait_ge(x1_ld[r], 16 * (g // 2 + 1) if isinstance(g, int) else 8 * (g - r) + 16)
            at_least(dve, out_st[r], 16 * GROUP * (g // 2) if isinstance(g, int) else 8 * GROUP * (g - r))
            nc.vector.scalar_tensor_tensor(out=oidx_f[r][:], in0=num, scalar=0.0, in1=pad[:], op0=ALU.is_equal, op1=ALU.mult).then_inc(s["oidx_step"], 1)
            dve.wait_ge(s["oidx_step"], 2 * g + 1)
            nc.vector.scalar_tensor_tensor(out=oidx_f[r][:], in0=num, scalar=1.0, in1=oidx_f[r][:], op0=ALU.subtract, op1=ALU.max).then_inc(s["oidx_step"], 1)
            dve.wait_ge(s["oidx_step"], 2 * g + 2)
            nc.vector.tensor_copy(oidx[r][:], oidx_f[r][:]).then_inc(s["oidx_rdy"], 1)

        def hidden(n, k):
            b = k % 2
            dve.wait_ge(s["silu_done"], n + 1)
            at_least(dve, s["y_ps"], n - 1)
            nc.vector.tensor_tensor(hT[b][:], act_s[b][:], up[b][:], ALU.mult).then_inc(s["h_done"], 1)

        def moments(g, r):
            dve.wait_ge(s["y_ev"], GROUP * (g + 1))
            base = 6 * g
            for k in range(GROUP):
                ins = nc.vector.bn_stats(st3[:, k, :], yg[r][:, k, :])
            ins.then_inc(s["fin_step"], 1)
            dve.wait_ge(s["fin_step"], base + 1)
            dve.sem_inc(s["dve_passed2"], 1)
            for k in range(GROUP):
                ins = nc.vector.bn_aggr(mv3[:, k, :], st3[:, k, :])
            ins.then_inc(s["fin_step"], 1)
            dve.wait_ge(s["fin_step"], base + 2)
            root_guess(nc, dve, s["fin_step"], base + 2, mv3, var3, rstd3)

        def last_norm(g, r):
            dve.wait_ge(s["root3"], ROOT_STEPS * (g + 1))
            at_least(dve, out_st[r], 16 * GROUP * (g // 2) if isinstance(g, int) else 8 * GROUP * (g - r))
            for k in range(GROUP):
                ins = nc.vector.tensor_scalar(og[r][:, k, :], yg[r][:, k, :], mv3[:, k, 0:1], rstd3[:, k:k + 1], ALU.subtract, ALU.mult)
            ins.then_inc(s["fin_step"], 1)
            dve.wait_ge(s["fin_step"], 6 * g + 6)
            nc.vector.tensor_tensor(og[r][:], og[r][:], x1g[r][:, :, 0:D], ALU.add).then_inc(s["out_rdy"], 1)

        scaled(0, 0, 0, 0)
        scaled(1, 1, 0, 0)

        def groups(i, first, last):
            for m in range(2 * GROUP):
                n, k, r = 2 * GROUP * i + m, m % GROUP, m // GROUP
                if not (last and m + 2 >= 2 * GROUP):
                    scaled(n + 2, (m + 2) % GROUP, (m + 2) // GROUP % 2, i + (m + 2) // (2 * GROUP))
                hidden(n, k)
                if not (first and r == 0):
                    if k == 1:
                        moments(2 * i + r - 1, 1 - r)
                    if k == 2:
                        places(2 * i + r - 1, 1 - r)
                    if k == 3:
                        last_norm(2 * i + r - 1, 1 - r)
        loop(dve, groups)
        moments(GROUPS - 1, 1)
        places(GROUPS - 1, 1)
        last_norm(GROUPS - 1, 1)


_INS = ["L0_attn_x", "L0_attn_Wq", "L0_attn_bq", "L0_attn_Wk", "L0_attn_bk", "L0_attn_Wv", "L0_attn_bv", "L0_attn_Wo", "L0_attn_bo",
        "L0_attn_rel_k", "L0_attn_rel_v", "L0_ffn_w_router", "L0_ffn_gate_up_proj", "L0_ffn_down_proj",
        "L0_ffn_w_gate", "L0_ffn_w_up", "L0_ffn_w_down"]
_OUTS = [((16, 512, 128), "float32")]


def kernel(**inputs):
    import numpy as _np
    import concourse.bacc as _bacc
    from concourse import mybir as _mybir
    from concourse.bass_utils import run_bass_kernel_spmd as _run

    nc = _bacc.Bacc("TRN2", target_bir_lowering=False, num_devices=1)
    arrays, args = {}, []
    for name in _INS:
        a = _np.ascontiguousarray(inputs[name])
        arrays[f"in_{name}_dram"] = a
        args.append(nc.dram_tensor(f"in_{name}_dram", a.shape, _mybir.dt.from_np(a.dtype), kind="ExternalInput").ap())
    outs = []
    for i, (shape, dtype) in enumerate(_OUTS):
        dt = _mybir.dt.from_np(_np.dtype(dtype))
        outs.append(nc.dram_tensor(f"out_{i}_dram", shape, dt, kind="ExternalOutput").ap())
    attention(nc, *outs, *args)
    r = _run(nc, [arrays], core_ids=[0])
    got = tuple(r.results[0][f"out_{i}_dram"] for i in range(len(_OUTS)))
    return got[0]
```

```python
from contextlib import ExitStack

import concourse.bass as bass
import numpy as np
from concourse import mybir

F32 = mybir.dt.float32
F16 = mybir.dt.float16
I32 = mybir.dt.int32
U32 = mybir.dt.uint32
ACT = mybir.ActivationFunctionType
ALU = mybir.AluOpType
AX = mybir.AxisListType

B, S, D = 16, 512, 128
H, HD = 16, 8
M = 128
NP = B // 2
P = 128
NT = S // P
E, F = 16, 256
TOK = B * S
TILES = TOK // P
UNITS = 2 * NP
SORTED = TILES + E
EPS = 1e-5

NU, NS, NB = 4, 4, 8
TERMS = ((0, 0), (0, 1), (1, 0))
ROWS_TERM = 3 * HD
ROWS_HEAD = ROWS_TERM + 2
ROWS_REL = NU * ROWS_TERM
ROWS_CON = 4 * ROWS_HEAD
NE8 = 8
SLOTS = 2 * NT * NT * NS
MAXSCALE = 2.0 ** -14
XMAX = 12.0

OFF0 = 255
WT_W, WT_0 = 415, 159
WN_W, WN_0 = 367, 127
Z_W, Z_0 = 384, 255


def attention(nc, out, x, Wq, bq, Wk, bk, Wv, bv, Wo, bo, rel_k, rel_v, w_router, gate_up, down, w_gate, w_up, w_down):
    ctx = ExitStack()
    outer = ExitStack()

    def dram(name, shape, dt):
        return nc.dram_tensor(name, shape, dt, kind="Internal").ap()

    qt_d = dram("qt_d", [B * H, ROWS_HEAD, S], F16)
    qn_d = dram("qn_d", [B * P, NE8 * NT * 16], F16)
    kt_d = dram("kt_d", [B * H, ROWS_TERM, NT, 2, P], F16)
    vs_d = dram("vs_d", [B, P, NT, 2 * H * 9], F32)
    rvp_d = dram("rvp_d", [512, HD], F32)
    opv_d = dram("opv_d", [B * H, HD + 1, S], F32)
    orl_d = dram("orl_d", [B * H * HD, S], F32)
    xs_d = dram("xs_d", [SORTED * P, ROW], F32)
    ysh_d = dram("ysh_d", [SORTED * P, D], F32)
    x2T_d = dram("x2T_d", [UNITS, P, S], F32)

    with outer:
        def osb(name, shape, dt):
            return outer.enter_context(nc.sbuf_tensor(name, shape, dt))

        ident = osb("ident", [P, P], F32)
        sgu = osb("sgu", [P, 2 * F], F32)
        sdn = osb("sdn", [P, 2, D], F32)
        ones = osb("ones", [P, P], F32)
        iota_e = osb("iota_e", [P, E], F32)
        owner = osb("owner", [P, E], F32)
        WE = osb("WE", [P, E, 2 * F + 2 * D], F32)
        c15 = osb("c15", [P, NT], F32)

        moe_sem = {n: outer.enter_context(nc.semaphore(n)) for n in MOE_SEMS.split()}
        with ctx:
            attention_phase(nc, ctx, locals())
        with ExitStack() as moe_ctx:
            expert_phase(nc, moe_ctx, locals())


def root_guess_step(eng, k, mean_var, half, root):
    if k == 0:
        return eng.tensor_scalar(half[:], mean_var[:, :, 1], EPS, 0.5, ALU.add, ALU.mult)
    if k == 1:
        return eng.tensor_scalar(root[:].bitcast(I32), half[:].bitcast(I32), 1, None, ALU.logical_shift_right)
    return eng.tensor_scalar(root[:].bitcast(I32), root[:].bitcast(I32), -1.0, float(0x5F3759DF - (1 << 22)), ALU.mult, ALU.add)


def newton_step(eng, k, root, half, tmp, c15):
    if k % 4 == 0:
        return eng.tensor_tensor(tmp[:], root[:], root[:], ALU.mult)
    if k % 4 == 1:
        return eng.tensor_tensor(tmp[:], tmp[:], half[:], ALU.mult)
    if k % 4 == 2:
        return eng.tensor_tensor(tmp[:], c15[:], tmp[:], ALU.subtract)
    return eng.tensor_tensor(root[:], root[:], tmp[:], ALU.mult)


def attention_phase(nc, ctx, a):
    (x, Wq, bq, Wk, bk, Wv, bv, Wo, bo, rel_k, rel_v, w_router, w_gate, w_up, w_down) = (
        a[n] for n in "x Wq bq Wk bk Wv bv Wo bo rel_k rel_v w_router w_gate w_up w_down".split())
    (qt_d, qn_d, kt_d, vs_d, rvp_d, opv_d, orl_d, xs_d, ysh_d, x2T_d) = (
        a[n] for n in "qt_d qn_d kt_d vs_d rvp_d opv_d orl_d xs_d ysh_d x2T_d".split())
    ident, sgu, sdn, ones, iota_e, owner, WE, c15 = (a[n] for n in "ident sgu sdn ones iota_e owner WE c15".split())
    gate_up, down, we_ld, scat = a["gate_up"], a["down"], a["moe_sem"]["we_ld"], a["moe_sem"]["scat"]

    def sb(name, shape, dt=F32):
        return ctx.enter_context(nc.sbuf_tensor(name, shape, dt))

    def pb(name, shape, dt=F32):
        return ctx.enter_context(nc.psum_tensor(name, shape, dt))

    def sem(name):
        return ctx.enter_context(nc.semaphore(name))

    wqT, wkT, wvT, woT = (sb(n, [P, P]) for n in ("wqT", "wkT", "wvT", "woT"))
    wrT = sb("wrT", [P, E])
    bq_s = sb("bq_s", [P, 1])
    kb = sb("kb", [P, 3])
    vb = sb("vb", [P, 3, P])
    bo_s = sb("bo_s", [P, P])
    escale = sb("escale", [P, 1])
    Wt = sb("Wt", [ROWS_REL, WT_W + 1], F16)
    Wn = sb("Wn", [P, WN_W + 1], F16)
    Rv = sb("Rv", [P, 32, Z_W // 32, HD])
    hmask = sb("hmask", [P, H])
    KC = [sb(f"KC{j}", [ROWS_CON, 2, 4, 2, P], F16) for j in range(NT)]
    VC = [sb(f"VC{j}", [P, 2, 2, H, 9]) for j in range(NT)]
    QC = [sb(f"QC{r}", [ROWS_CON, 2, 4, 4, P], F16) for r in range(2)]
    QT = [sb(f"QT{r}", [ROWS_REL, NU, 2, H, 32], F16) for r in range(2)]
    w = [sb(f"w{r}", [P, 2, NS, H, NU, NB]) for r in range(2)]
    pv_s = sb("pv_s", [P, 2, 4, P])
    rel_s = sb("rel_s", [P, 2 * H, NU, NB])
    we32 = WE[:].rearrange("p e n -> p (e n)")
    we16 = we32.bitcast(F16)
    n16 = NE8 * H * 32
    Qb = [we16[:, n16 * r:n16 * (r + 1)].rearrange("p (e h q) -> p e h q", e=NE8, h=H) for r in range(2)]
    Qn = we16[:, 2 * n16:4 * n16].rearrange("p (e h k) -> p e h k", e=NE8, h=H)
    kn = [we16[:, 4 * n16 + 3 * S * r:4 * n16 + 3 * S * (r + 1)].rearrange("p (v k) -> p v k", v=3) for r in range(2)]
    at = (4 * n16 + 6 * S) // 2
    xt = [we32[:, at + S * r:at + S * (r + 1)].rearrange("p (t d) -> p t d", t=NT) for r in range(2)]
    qf = we32[:, at + 2 * S:at + 3 * S]
    kf = we32[:, at + 3 * S:at + 5 * S].rearrange("p (v k) -> p v k", v=2)
    assert at + 5 * S == E * (2 * F + 2 * D)
    st = sb("st", [P, NT, 6])
    mv = sb("mv", [P, NT, 2])
    var = sb("var", [P, NT])
    rstd = sb("rstd", [P, NT])
    rtmp = sb("rtmp", [P, NT])
    xn = sb("xn", [P, NT, D])
    xnT = sb("xnT", [P, S])
    qs = sb("qs", [P, 2, S], F16)
    qp = [sb(f"qp{r}", [P, NE8, NT, 16], F16) for r in range(2)]
    ks = sb("ks", [P, 2, NT, 2, P], F16)
    zrow = sb("zrow", [P, ROW])
    number_i = sb("number_i", [P, NT], I32)
    number = sb("number", [P, NT])
    vst = sb("vst", [P, NT, 2, H, 9])
    mx = sb("mx", [P, NT * 16])
    ms = sb("ms", [P, 2, NT * 16], F16)
    oA, oB, oS = (sb(n, [P, S]) for n in ("oA", "oB", "oS"))
    xr = sb("xr", [P, NT, D])
    y = sb("y", [P, NT, D])
    st2 = sb("st2", [P, NT, 6])
    mv2 = sb("mv2", [P, NT, 2])
    var2 = sb("var2", [P, NT])
    rstd2 = sb("rstd2", [P, NT])
    rtmp2 = sb("rtmp2", [P, NT])
    x2T = sb("x2T", [P, S])
    xs = sb("xs", [P, NT, ROW])
    lg = sb("lg", [P, NT, E])
    lmax = sb("lmax", [P, NT])
    cand = sb("cand", [P, NT, E])
    lidx = sb("lidx", [P, NT])
    oh = sb("oh", [P, NT, E], F16)
    tri16 = sb("tri16", [P, P], F16)
    ones16 = sb("ones16", [P, P], F16)
    tau_i = sb("tau_i", [P, 1], I32)
    tau = sb("tau", [P, 1])
    counted = sb("counted", [P, 2, NT, E])
    running = sb("running", [P, NT + 1, E])
    filled = sb("filled", [P, E])
    rounded = sb("rounded", [P, E])
    used = sb("used", [P, 1])
    prefix = [sb(f"prefix{r}", [P, 8 + E]) for r in range(3)]
    first_row = sb("first_row", [P, E])
    jump = sb("jump", [P, E])
    pos = sb("pos", [P, NT, E])
    spot = sb("spot", [P, NT, E])
    spot_t = sb("spot_t", [P, NT])
    spot_u = sb("spot_u", [P, NT], U32)
    spots = sb("spots", [P, UNITS * NT], U32)
    below = [sb(f"below{r}", [P, E]) for r in range(2)]
    sg = sb("sg", [P, NT])
    w_flat = [buf[:].rearrange("p a b c d e -> p (a b c d e)") for buf in w]
    unit_x = [w_flat[0][:, S * r:S * r + S] for r in range(4)]
    unit_act = [w_flat[r][:, 4 * S:6 * S].rearrange("p (c n) -> p c n", c=2) for r in range(2)]
    unit_h = [w_flat[1][:, 2 * S * r:2 * S * (r + 1)].rearrange("p (c n) -> p c n", c=2) for r in range(2)]
    unit_y = [w_flat[r % 2][:, S * (6 + r // 2):S * (7 + r // 2)].rearrange("p (t d) -> p t d", t=NT) for r in range(4)]

    sc = [pb(f"sc{r}", [P, S]) for r in range(2)]
    mix = [pb(f"mix{r}", [P, S]) for r in range(2)]
    pv = [pb(f"pv{r}", [P, S]) for r in range(2)]
    rel = [pb(f"rel{r}", [P, S]) for r in range(2)]

    names = ("w_ld w_ld2 tab pool_set dve_set act_set pe_set sp_set wt_ld rv_ld zeroed "
             "x_ld0 x_ld1 xn_step xn_done xT_ps xnT_rdy q_ps q_ev k_ps k_read k_ev v_ps v_ev qsplit ksplit "
             "qs_st qn_st ks_st vs_st qb_done qn_ld0 qn_ld1 nat_ps mx_done ms_step ms_done ms_st "
             "qc_ld0 qc_ld1 kc_ld0 kc_ld1 kc_ld2 kc_ld3 s_done exp_done pv_done pv_ev rel_ev o_st "
             "o_ld o_step O_rdy op_ps ln_step x1_done xn2_done x2T_ps x2T_ev lg_ps lg_read lg_ev "
             "dve_passed pool_passed sp_passed root root2 top_step sg_done number_step sg_step xs_done oh_rdy cnt_ps cnt_read al_step spot_rdy z_st "
             "x2T_st unit_ld0 unit_ld1 unit_ld2 unit_ld3 unit_gu unit_silu unit_hid unit_dn unit_out unit_st0 unit_st1 unit_st2 unit_st3")
    s = {n: sem(n) for n in names.split()}
    x_ld = [s["x_ld0"], s["x_ld1"]]
    qn_ld = [s["qn_ld0"], s["qn_ld1"]]
    qc_ld = [s["qc_ld0"], s["qc_ld1"]]
    kc_ld = [s[f"kc_ld{j}"] for j in range(NT)]
    unit_ld = [s[f"unit_ld{r}"] for r in range(4)]
    unit_st = [s[f"unit_st{r}"] for r in range(4)]

    def at_least(eng, name, value):
        if not (isinstance(value, int) and value <= 0):
            eng.wait_ge(s[name] if isinstance(name, str) else name, value)

    def turns(eng, body):
        body(0, False, True, True)
        body(1, True, True, True)
        with eng.Fori(2, NP - 2) as i:
            body(i, True, True, True)
        body(NP - 2, True, True, False)
        body(NP - 1, True, False, False)

    shared = []
    for slot in range(SLOTS):
        shared.append(("row max", slot))
        for half in range(2):
            if slot - 64 * half in PREPARE_PE:
                shared.append(("prepare", half, PREPARE_PE[slot - 64 * half]))
        for half in range(2):
            if slot - FINISH[half] in FINISH_PE[half]:
                shared.append(("finish", half, FINISH_PE[half][slot - FINISH[half]]))
    assert len(shared) % 2 == 0
    place = {job: n for n, job in enumerate(shared)}

    def bank(*job):
        return mix[place[job] % 2]

    def finishing(slot, i, prev):
        found = [(i, 0, slot - FINISH[0])]
        if prev:
            found += [(i - 1, 0, slot + SLOTS - FINISH[0]), (i - 1, 1, slot - FINISH[1])]
        return found

    def wait_for_bank(pe, job, i, prev, nxt, nxt2):
        n, turns_back = place[job] - 2, 0
        while True:
            if n < 0:
                if isinstance(i, int) and i == 0:
                    return
                n, turns_back = n + len(shared), 1
                nxt, nxt2 = True, nxt
                prev = not isinstance(i, int) or i > 1
            what, turn = shared[n], i - turns_back
            if what[0] == "row max" and nxt:
                pe.wait_ge(s["mx_done"], 128 * (turn + 1) + what[1] + 1)
                return
            if what[0] == "prepare" and (nxt2 if what[1] else nxt):
                c = 2 * turn + (4 if what[1] else 3)
                pe.wait_ge(s[("xnT_rdy", "q_ev", "k_read", "v_ev")[what[2]]], c + 1)
                return
            if what[0] == "finish" and (prev or what[1] == 0):
                c = 2 * turn - what[1]
                pe.wait_ge(*((s["ln_step"], 12 * c + 1), (s["x2T_ev"], c + 1), (s["lg_read"], c + 1), (s["cnt_read"], c + 1))[what[2]])
                return
            n -= 2

    wraw = [w[0][:, 0].rearrange("p a b c d -> p (a b c d)")[:, P * n:P * n + P] for n in range(4)]
    wg_raw = w[0][:, 1].rearrange("p a b c d -> p (a b c d)")
    wr_raw = wg_raw[0:E, 6 * P:7 * P]
    gu_raw = [wg_raw[:, P * n:P * n + P] for n in range(6)]
    rkT = w[1][0:HD, 0].rearrange("p a b c d -> p (a b c d)")[:, 0:2 * M + 1]
    rpad = w[1][0:HD, 0].rearrange("p a b c d -> p (a b c d)")[:, 512:1024]
    tri = w[1][:, 1].rearrange("p a b c d -> p (a b c d)")[:, 1024:1024 + P]
    rzero = w[1][0:HD, 0].rearrange("p a b c d -> p (a b c d)")[:, 1024:1024 + P]
    rpart = [w[1][0:HD, 0].rearrange("p a b c d -> p (a b c d)")[:, 1280 + 256 * n:1536 + 256 * n].bitcast(F16) for n in range(2)]
    sq = w[1][:, 1].rearrange("p a b c d -> p (a b c d)")
    bnd = sq[:, 256:264]
    bmax = sq[:, 264:272]
    pw = sq[:, 272:280]
    bkr = sq[:, 280:284]
    bqr = sq[:, 284:285]
    vraw = sq[:, 512:1024].rearrange("p (a b) -> p a b", b=P)[:, 0:3]

    LOADS, MORE_LOADS = 2 + 1 + 4, 2 + 6 + 1 + 4

    block = ctx.enter_context(nc.Block())

    @block.sync
    def _(sp):
        def load_x(n, b2):
            at_least(sp, "xn_done", 2 * n + b2 - 1)
            sp.dma_start(xt[b2][:], x[bass.ds(2 * n + b2, 1)].rearrange("o (t p) d -> p (o t) d", p=P)).then_inc(x_ld[b2], 16)

        load_x(0, 0)
        load_x(0, 1)
        with nc.allow_non_contiguous_dma(reason="small tables, once"):
            ld = s["w_ld"]
            for n, W in enumerate((Wq, Wk)):
                sp.dma_start(wraw[n], W).then_inc(ld, 16)
            sp.dma_start(rkT, rel_k.rearrange("r d -> d r")).then_inc(ld, 16)
            sp.dma_start(bqr, bq.rearrange("(p o) -> p o", o=1)).then_inc(ld, 16)
            sp.dma_start(bkr[:, 0:1], bk.rearrange("(p o) -> p o", o=1)).then_inc(ld, 16)
            for n, r in ((1, 0), (2, 2 * M)):
                src = rel_k[r:r + 1, :]
                sp.dma_start(bkr[:, n:n + 1], bass.AP(src.tensor, src.offset, [[0, H], [1, HD], [1, 1]])).then_inc(ld, 16)
            ld = s["w_ld2"]
            for n, W in enumerate((Wv, Wo)):
                sp.dma_start(wraw[2 + n], W).then_inc(ld, 16)
            for n in range(2):
                sp.dma_start(gu_raw[n], w_gate[P * n:P * n + P]).then_inc(ld, 16)
                sp.dma_start(gu_raw[2 + n], w_up[P * n:P * n + P]).then_inc(ld, 16)
                sp.dma_start(gu_raw[4 + n], w_down[:, P * n:P * n + P]).then_inc(ld, 16)
            sp.dma_start(wr_raw, w_router).then_inc(ld, 16)
            sp.dma_start(vraw[:, 0, :], bass.AP(bv.tensor, bv.offset, [[0, P], [1, P]])).then_inc(ld, 16)
            sp.dma_start(bo_s[:], bass.AP(bo.tensor, bo.offset, [[0, P], [1, P]])).then_inc(ld, 16)
            for n, r in ((1, 0), (2, 2 * M)):
                src = rel_v[r:r + 1, :]
                sp.dma_start(vraw[:, n, :].rearrange("p (h d) -> p h d", d=HD),
                             bass.AP(src.tensor, src.offset, [[0, P], [0, H], [1, HD]])).then_inc(ld, 16)
            tab = s["tab"]
            sp.dma_start(rvp_d[127:127 + 2 * M + 1], rel_v).then_inc(tab, 16)
            sp.dma_start(rvp_d[0:127], bass.AP(rel_v.tensor, rel_v.offset, [[0, 127], [1, HD]])).then_inc(tab, 16)
            sp.dma_start(rvp_d[384:512], bass.AP(rel_v.tensor, rel_v.offset + 2 * M * HD, [[0, 128], [1, HD]])).then_inc(tab, 16)
        sp.wait_ge(s["dve_set"], RPART_READY)
        for half in range(2):
            for e in range(NE8):
                c = OFF0 - WN_0 - 16 * e
                sp.dma_start(Wn[64 * half + HD * e:64 * half + HD * e + HD, 0:WN_W], rpart[0][:, c:c + WN_W]).then_inc(s["sp_set"], 16)

        def load_wt():
            for u in range(NU):
                for t, (_, kp) in enumerate(TERMS):
                    r = (u * 3 + t) * HD
                    c = OFF0 - WT_0 - 32 * u
                    sp.dma_start(Wt[r:r + HD, 0:WT_W], rpart[kp][:, c:c + WT_W]).then_inc(s["wt_ld"], 16)

        def load_rv():
            sp.wait_ge(tab, 48)
            for m in range(Z_W // 32):
                sp.dma_start(Rv[:, :, m, :], bass.AP(rvp_d.tensor, rvp_d.offset + 32 * m * HD,
                                                     [[HD, P], [HD, 32], [1, HD]])).then_inc(s["rv_ld"], 16)

        def zero_sorted(sorted_rows, part):
            n = sorted_rows.shape[1]
            rows = sorted_rows.rearrange("(a p) n -> p a n", p=P)
            sp.dma_start(rows[:, part * ZERO_TILES:(part + 1) * ZERO_TILES],
                         zrow[:, 0:n].rearrange("p (o n) -> p o n", o=1).broadcast_to([P, ZERO_TILES, n])).then_inc(s["z_st"], 16)

        def store_q(n, b2):
            c = 2 * n + b2
            sp.wait_ge(s["qsplit"], 3 * c + 3)
            sp.dma_start(qn_d[bass.ds(c * P, P)], qp[b2][:].rearrange("p e t b -> p (e t b)")).then_inc(s["qn_st"], 16)
            for tm, (qpart, _) in enumerate(TERMS):
                sp.dma_start(qt_d[bass.ds(c * H, H), HD * tm:HD * tm + HD, :], qs[:, qpart, :]).then_inc(s["qs_st"], 16)
            sp.wait_ge(s["qn_st"], 16 * (c + 1))
            sp.sem_inc(s["sp_passed"], 1)
            at_least(sp, "nat_ps", 64 * (c - 1))
            sp.sem_inc(s["sp_passed"], 1)
            src = qn_d[bass.ds(c * P, P)].rearrange("(h d) (e k) -> e d h k", d=HD, e=NE8)
            for e in range(NE8):
                row = 64 * b2 + HD * e
                sp.dma_start(Qn[row:row + HD, e, :, :], src[e]).then_inc(qn_ld[b2], 16)

        def store_kv(n, b2):
            c = 2 * n + b2
            sp.wait_ge(s["ksplit"], 2 * c + 2)
            for tm, (_, kpart) in enumerate(TERMS):
                sp.dma_start(kt_d[bass.ds(c * H, H), HD * tm:HD * tm + HD].rearrange("h d t v k -> h d (t v k)"),
                             ks[:, kpart].rearrange("p t v k -> p (t v k)")).then_inc(s["ks_st"], 16)
            sp.wait_ge(s["v_ev"], c + 1)
            sp.dma_start(vs_d[bass.ds(c, 1)].rearrange("o p t n -> p (o t) n"),
                         vst[:].rearrange("p t v h n -> p t (v h n)")).then_inc(s["vs_st"], 16)

        def store_max(n, b2, t):
            group = NT * (2 * n + b2) + t
            sp.wait_ge(s["ms_done"], group + 1)
            sp.sem_inc(s["sp_passed"], 1)
            at_least(sp, "ms_st", 32 * group)
            dst = qt_d[bass.ds((2 * n + b2) * H, H)].rearrange("h r (t e b) -> r t e h b", t=NT, e=NE8)
            for part in range(2):
                sp.dma_start(dst[ROWS_TERM + part, t], ms[:, part, 16 * t:16 * t + 16]).then_inc(s["ms_st"], 16)

        def load_q(n, t):
            r = t % 2
            at_least(sp, "s_done", n * SLOTS + 32 * (t - 1))
            sp.sem_inc(s["sp_passed"], 1)
            if t == 0:
                sp.wait_ge(s["qs_st"], 48 * (2 * n + 2))
            sp.wait_ge(s["ms_st"], 32 * (NT * (2 * n + 1) + t + 1))
            sp.sem_inc(s["sp_passed"], 1)
            src = qt_d[bass.ds(2 * n * H, 2 * H)]
            heads4 = src.rearrange("(bg hh) r q -> hh r bg q", hh=4)
            for hh in range(4):
                row = ROWS_HEAD * hh
                sp.dma_start(QC[r][row:row + ROWS_HEAD, :, :, hh, :].rearrange("r b g q -> r (b g) q"),
                             heads4[hh, :, :, P * t:P * t + P]).then_inc(qc_ld[r], 16)
            heads = src.rearrange("bh r q -> r bh q")
            for u in range(NU):
                row = ROWS_TERM * u
                sp.dma_start(QT[r][row:row + ROWS_TERM, u].rearrange("r b h q -> r (b h) q"),
                             heads[0:ROWS_TERM, :, P * t + 32 * u:P * t + 32 * u + 32]).then_inc(qc_ld[r], 16)

        def load_kv(n, j):
            at_least(sp, "s_done", (n - 1) * SLOTS + 96 + 8 * (j + 1))
            sp.sem_inc(s["sp_passed"], 1)
            at_least(sp, "pv_done", (n - 1) * SLOTS + 96 + 8 * (j + 1))
            sp.sem_inc(s["sp_passed"], 1)
            sp.wait_ge(s["ks_st"], 48 * (2 * n + 2))
            sp.sem_inc(s["sp_passed"], 1)
            sp.wait_ge(s["vs_st"], 16 * (2 * n + 2))
            sp.sem_inc(s["sp_passed"], 1)
            src = kt_d[bass.ds(2 * n * H, 2 * H)].rearrange("(bg hh) r t v k -> hh r bg t (v k)", hh=4)
            for hh in range(4):
                row = ROWS_HEAD * hh
                sp.dma_start(KC[j][row:row + ROWS_TERM].rearrange("r b g v k -> r (b g) (v k)"), src[hh, :, :, j, :]).then_inc(kc_ld[j], 16)
            sp.dma_start(VC[j][:].rearrange("p b v h n -> p b (v h n)"),
                         vs_d[bass.ds(2 * n, 2), :, j, :].rearrange("b p n -> p b n")).then_inc(kc_ld[j], 16)

        def store_o(n, t):
            sp.wait_ge(s["pv_ev"], 2 * (4 * n + t) + 2)
            rows = opv_d[bass.ds(2 * n * H, 2 * H)].rearrange("(b g hh) d q -> b g d hh q", b=2, g=4)
            for b2 in range(2):
                for g in range(4):
                    sp.dma_start(rows[b2, g, :, :, P * t:P * t + P], pv_s[32 * g:32 * g + HD + 1, b2]).then_inc(s["o_st"], 16)
            sp.wait_ge(s["rel_ev"], 2 * (4 * n + t) + 2)
            dst = orl_d[bass.ds(2 * n * P, 2 * P)].rearrange("(bh d) q -> d bh q", d=HD)
            for sb_ in range(NS):
                for u in range(NU):
                    row = 32 * sb_ + HD * (NU - 1 - u)
                    q0 = P * t + 32 * u + NB * sb_
                    sp.dma_start(dst[:, :, q0:q0 + NB], rel_s[row:row + HD, :, u, :]).then_inc(s["o_st"], 16)

        def load_o(n, half):
            c = 2 * n + half
            sp.wait_ge(s["o_st"], O_STORES * (NT * n + 2 * half + 2))
            sp.sem_inc(s["sp_passed"], 1)
            at_least(sp, "op_ps", c)
            at_least(sp, "x1_done", c)
            sp.sem_inc(s["sp_passed"], 1)
            q = slice(S // 2 * half, S // 2 * (half + 1))
            for b2 in range(2):
                cols = slice(S // 2 * b2, S // 2 * (b2 + 1))
                rows = opv_d[bass.ds((2 * n + b2) * H, H)]
                sp.dma_start(oA[:, cols], rows[:, 0:HD, q]).then_inc(s["o_ld"], 16)
                sp.dma_start(oB[:, cols], orl_d[bass.ds((2 * n + b2) * P, P), q]).then_inc(s["o_ld"], 16)
                sp.dma_start(oS[:, cols], rows[:, HD:HD + 1, q].broadcast_to([H, HD, S // 2])).then_inc(s["o_ld"], 16)
                sp.dma_start(xr[:, 2 * b2:2 * b2 + 2, :], x[bass.ds(2 * n + b2, 1), q, :].rearrange("o (t p) d -> p (o t) d", p=P)).then_inc(s["o_ld"], 16)

        def load_experts():
            sp.wait_ge(s["nat_ps"], 128 * NP)
            sp.wait_ge(s["ksplit"], 2 * B)
            sp.wait_ge(s["qsplit"], 3 * B)
            sp.wait_ge(s["k_ev"], B)
            sp.wait_ge(s["xn_done"], B)
            sp.dma_start(WE[:, :, 0:2 * F], gate_up.rearrange("e h f -> h e f")).then_inc(we_ld, 16)
            for c in range(2):
                sp.dma_start(WE[:, :, 2 * F + D * c:2 * F + D * c + D], down[:, P * c:P * c + P, :].rearrange("e f d -> f e d")).then_inc(we_ld, 16)


        def store_x2T(n, half):
            c = 2 * n + half
            sp.wait_ge(s["x2T_ev"], c + 1)
            sp.sem_inc(s["sp_passed"], 1)
            sp.dma_start(x2T_d[bass.ds(c, 1)].rearrange("o p q -> p (o q)"), x2T[:]).then_inc(s["x2T_st"], 16)

        def load_unit(u):
            at_least(sp, "unit_gu", 2 * (u - 3))
            sp.wait_ge(s["pv_done"], SLOTS * (NP - 1) + 8 * 15)
            sp.wait_ge(s["x2T_st"], 16 * min(u + 1, UNITS) if u == UNITS - 1 else 16 * (UNITS - 1))
            sp.dma_start(unit_x[u % 4], x2T_d[u]).then_inc(unit_ld[u % 4], 16)

        def turn(i, prev, nxt, nxt2):
            for slot in range(SLOTS):
                if slot == 1:
                    if prev:
                        store_max(i, 1, NT - 1)
                    load_q(i, 1)
                    load_kv(i, 2)
                if slot in (33, 65):
                    load_q(i, slot // 32 + 1)
                if slot == 9:
                    load_kv(i, 3)
                if slot % 32 == 10 and (prev or slot > 32):
                    t = slot // 32 - 1
                    store_o(i, t) if t >= 0 else store_o(i - 1, NT - 1)
                if nxt2 and slot in (2, 60):
                    load_x(i + 2, slot // 60)
                if nxt:
                    if slot == 18:
                        store_q(i + 1, 1)
                    if slot == 29:
                        store_kv(i + 1, 1)
                    if slot % 16 == 1 and slot > 1:
                        store_max(i + 1, (slot // 16 - 1) // NT, (slot // 16 - 1) % NT)
                    if slot == 100:
                        load_q(i + 1, 0)
                    if slot == 113:
                        load_kv(i + 1, 0)
                    if slot == 124:
                        load_kv(i + 1, 1)
                if nxt2:
                    if slot == 64 + 18:
                        store_q(i + 2, 0)
                    if slot == 64 + 29:
                        store_kv(i + 2, 0)
                for n, half, since in finishing(slot, i, prev):
                    if since == 0:
                        load_o(n, half)
                if slot == 126:
                    store_x2T(i, 0)
                if prev and slot == 72:
                    store_x2T(i - 1, 1)
                if isinstance(i, int) and i < 2 and slot % 16 == 12 and slot // 16 < SORTED // ZERO_TILES:
                    zero_sorted((xs_d, ysh_d)[i], slot // 16)
                if not nxt and slot == 45:
                    load_experts()

        load_x(1, 0)
        sp.wait_ge(s["zeroed"], ZEROED_FIRST)
        store_q(0, 0)
        load_wt()
        store_kv(0, 0)
        store_q(0, 1)
        store_kv(0, 1)
        load_x(1, 1)
        load_rv()
        for t in range(NT):
            store_max(0, 0, t)
        store_max(0, 1, 0)
        sp.wait_ge(s["zeroed"], ZEROED)
        load_q(0, 0)
        load_kv(0, 0)
        load_kv(0, 1)
        store_max(0, 1, 1)
        store_q(1, 0)
        store_max(0, 1, 2)
        store_kv(1, 0)
        store_max(0, 1, 3)
        turns(sp, turn)
        for u in range(4):
            load_unit(u)
        store_o(NP - 1, NT - 1)
        load_o(NP - 1, 1)
        for u in range(4, 11):
            load_unit(u)
        store_x2T(NP - 1, 1)
        for u in range(11, UNITS):
            load_unit(u)
        sp.wait_ge(s["z_st"], 2 * ZERO_STORES)

    @block.tensor
    def _(pe):
        def transpose(out_, in_):
            k = in_.shape[0]
            return nc.tensor.transpose(out_, in_, ident[0:k, 0:k])

        def prep(n, b2, step, mix):
            c = 2 * n + b2
            if step == 0:
                pe.wait_ge(s["xn_done"], c + 1)
                for t in range(NT):
                    mm = transpose(mix[:, P * t:P * t + P], xn[:, t, :])
                mm.then_inc(s["xT_ps"], 1)
            elif step == 1:
                pe.wait_ge(s["xnT_rdy"], c + 1)
                nc.tensor.matmul(mix[:], wqT[:], xnT[:], start=True, stop=True).then_inc(s["q_ps"], 1)
            elif step == 2:
                nc.tensor.matmul(mix[:], wkT[:], xnT[:], start=True, stop=True).then_inc(s["k_ps"], 1)
            else:
                for t in range(NT):
                    mm = nc.tensor.matmul(mix[:, P * t:P * t + P], xnT[:, P * t:P * t + P], wvT[:], start=True, stop=True)
                mm.then_inc(s["v_ps"], 1)

        pe.wait_ge(s["pool_set"], IDENT_READY)
        prep(0, 0, 0, mix[0])
        pe.wait_ge(s["w_ld"], 16 * LOADS)
        pe.wait_ge(s["w_ld2"], 16 * MORE_LOADS)
        pe.wait_ge(s["dve_set"], SCALED)
        for n in range(4):
            mm = transpose(sc[0][:, P * n:P * n + P], wraw[n])
        for n in range(4):
            mm = transpose(sc[1][:, P * n:P * n + P], gu_raw[n])
        for n in range(2):
            mm = transpose(mix[1][:, P * n:P * n + P], gu_raw[4 + n])
        mm = transpose(mix[1][:, 2 * P:2 * P + E], wr_raw)
        mm.then_inc(s["pe_set"], 1)
        pe.wait_ge(s["act_set"], 1)
        pe.wait_ge(s["dve_set"], DVE_SET_DONE)

        def natural(n, b2, k, nat):
            c = 2 * n + b2
            if k == 0:
                pe.wait_ge(s["k_ev"], c + 1)
                pe.wait_ge(qn_ld[b2], QN_LOADS * (n + 1))
            if k % 32 == 0:
                pe.wait_ge(s["qb_done"], 2 * c + k // 32 + 1)
            t, b = k // 16, k % 16
            lo = max(0, P * t + b - (M - 1))
            hi = min(S, P * t + b + 16 * (NE8 - 1) + M)
            lq = Qb[t // 2][:, :, :, 16 * (t % 2) + b].rearrange("p e h -> p (e h)")
            le = Qn[64 * b2:64 * b2 + 64, :, :, k].rearrange("p e h -> p (e h)")
            x0 = WN_0 - P * t - b
            nc.tensor.matmul(nat[:, lo:hi], lq, kn[b2][:, 0, lo:hi], start=True, stop=False, skip_group_check=True)
            mm = nc.tensor.matmul(nat[:, lo:hi], le, Wn[64 * b2:64 * b2 + 64, x0 + lo:x0 + hi], start=False, stop=True, skip_group_check=True)
            if lo > 0:
                mm = nc.tensor.matmul(nat[:, 0:lo], lq, kn[b2][:, 1, 0:lo], start=False, stop=True, skip_group_check=True)
            if hi < S:
                mm = nc.tensor.matmul(nat[:, hi:S], lq, kn[b2][:, 2, hi:S], start=False, stop=True, skip_group_check=True)
            mm.then_inc(s["nat_ps"], 1)

        def scores(i, slot):
            t, j, b2, q8 = slot // 32, slot // 8 % 4, slot // 4 % 2, slot % 4
            if slot % 32 == 0:
                pe.wait_ge(qc_ld[t % 2], QC_LOADS * (2 * i + t // 2 + 1))
            if t == 0 and slot % 8 == 0:
                pe.wait_ge(kc_ld[j], KC_LOADS * (i + 1))
            at_least(pe, "exp_done", SLOTS * i + slot - 1)
            near = abs(t - j) <= 1
            bank = sc[slot % 2]
            qc = QC[t % 2][:, b2].rearrange("p g h (u s b) -> p g h u s b", u=NU, s=NS)
            for g in range(4):
                mm = nc.tensor.matmul(bank[:, P * g:P * g + P], KC[j][:, b2, g, 0 if near else 1, :], qc[:, g, :, :, q8, :],
                                      start=(g == 0), stop=not near, skip_group_check=True)
            if near:
                view = bank[:].rearrange("p (h u b) -> p h u b", h=H, u=NU)
                qt = QT[t % 2][:, :, b2].rearrange("p u h q -> p h u q")
                for b in range(NB):
                    x0 = WT_0 + P * (j - t) - NB * q8 - b
                    mm = nc.tensor.matmul(view[:, :, :, b], Wt[:, x0:x0 + P], qt[:, :, :, NB * q8 + b], start=False, stop=(b == NB - 1), skip_group_check=True)
            mm.then_inc(s["s_done"], 1)

        def values(i, tile, k):
            t, j = tile // 4, tile % 4
            near = abs(t - j) <= 1
            wt = w[tile % 2]
            if k == 0:
                pe.wait_ge(s["exp_done"], SLOTS * i + 8 * (tile + 1))
            if k % 4 == 0:
                done = 2 * (4 * i + t - 1) + k // 4 + 1
                if j == 0:
                    at_least(pe, "pv_ev", done)
                if j == max(0, t - 1):
                    at_least(pe, "rel_ev", done)
            b2, hh = k // 4, k % 4
            for g in range(4):
                h = 4 * g + hh
                mm = nc.tensor.matmul(pv[b2][32 * g:32 * g + 9, P * hh:P * hh + P], VC[j][:, b2, 0 if near else 1, h, :],
                                      wt[:, b2, :, h].rearrange("p s u b -> p u s b"),
                                      start=(j == 0 and hh == 0), stop=(j == NT - 1), skip_group_check=True)
            if near:
                for q8 in range(NS):
                    z0 = Z_0 + P * (j - t) - NB * q8 - k - 32 * (NU - 1)
                    lv = Rv[:, z0 % 32, z0 // 32:z0 // 32 + NU, :].rearrange("p u d -> p (u d)")
                    mm = nc.tensor.matmul(rel[k // 4][32 * q8:32 * q8 + 32, P * (k % 4):P * (k % 4) + P], lv,
                                          wt[:, :, q8, :, :, k], start=(j == max(0, t - 1) and k % 4 == 0),
                                          stop=(j == min(NT - 1, t + 1)), skip_group_check=True)
            mm.then_inc(s["pv_done"], 1)

        def finish(n, b2, step, mix):
            c = 2 * n + b2
            if step == 0:
                pe.wait_ge(s["O_rdy"], c + 1)
                for t in range(NT):
                    mm = nc.tensor.matmul(mix[:, P * t:P * t + P], oA[:, P * t:P * t + P], woT[:], start=True, stop=True)
                mm.then_inc(s["op_ps"], 1)
            elif step == 1:
                pe.wait_ge(s["xn2_done"], c + 1)
                for t in range(NT):
                    mm = transpose(mix[:, P * t:P * t + P], xs[:, t, 0:D])
                mm.then_inc(s["x2T_ps"], 1)
            elif step == 3:
                pe.wait_ge(s["oh_rdy"], c + 1)
                flat = oh[:].rearrange("p t e -> p (t e)")
                nc.tensor.matmul(mix[:, 0:NT * E], tri16[:], flat, start=True, stop=True)
                nc.tensor.matmul(mix[:, NT * E:2 * NT * E], ones16[:], flat, start=True, stop=True).then_inc(s["cnt_ps"], 1)
            else:
                pe.wait_ge(s["x2T_ev"], c + 1)
                for t in range(NT):
                    mm = nc.tensor.matmul(mix[:, E * t:E * t + E], x2T[:, P * t:P * t + P], wrT[:], start=True, stop=True)
                mm.then_inc(s["lg_ps"], 1)

        def turn(i, prev, nxt, nxt2):
            for slot in range(SLOTS):
                scores(i, slot)
                if nxt:
                    wait_for_bank(pe, ("row max", slot), i, prev, nxt, nxt2)
                    natural(i + 1, slot // 64, slot % 64, bank("row max", slot))
                for half in range(2):
                    if (nxt2 if half else nxt) and slot - 64 * half in PREPARE_PE:
                        job = ("prepare", half, PREPARE_PE[slot - 64 * half])
                        wait_for_bank(pe, job, i, prev, nxt, nxt2)
                        prep(i + 1 + half, 1 - half, job[2], bank(*job))
                if slot >= 8:
                    values(i, slot // 8 - 1, slot % 8)
                elif prev:
                    values(i - 1, 15, slot)
                for half in range(2):
                    if (prev or half == 0) and slot - FINISH[half] in FINISH_PE[half]:
                        job = ("finish", half, FINISH_PE[half][slot - FINISH[half]])
                        wait_for_bank(pe, job, i, prev, nxt, nxt2)
                        finish(i - half, half, job[2], bank(*job))

        def prologue(n, b2, step, mix):
            c = 2 * n + b2
            if step == 2:
                pe.wait_ge(s["q_ev"], c + 1)
            if step == 3:
                pe.wait_ge(s["k_read"], c + 1)
            prep(n, b2, step, mix)

        for step in (1, 2, 3):
            prologue(0, 0, step, mix[0])
        pe.wait_ge(s["sp_set"], 16 * TABLE_LOADS)
        pe.wait_ge(s["v_ev"], 1)
        for k in range(128):
            at_least(pe, "mx_done", k - 3)
            natural(0, k // 64, k % 64, (*mix, *sc)[k % 4])
            if k in PROLOGUE_PE[0]:
                prologue(0, 1, PROLOGUE_PE[0][k], pv[0])
            if k in PROLOGUE_PE[1]:
                prologue(1, 0, PROLOGUE_PE[1][k], pv[1])
        pe.wait_ge(s["mx_done"], 128)
        pe.wait_ge(s["v_ev"], 3)
        pe.wait_ge(s["rv_ld"], 16 * (Z_W // 32))
        pe.wait_ge(s["wt_ld"], 16 * NU * len(TERMS))
        turns(pe, turn)
        for k in range(8):
            values(NP - 1, 15, k)

        def gates_and_ups(u):
            pe.wait_ge(unit_ld[u % 4], 16 * (u // 4 + 1))
            for c in range(2):
                if u == 0:
                    pe.wait_ge(s["exp_done"], SLOTS * NP)
                    pe.wait_ge(s["pv_ev"], 2 * NT * NP)
                at_least(pe, "unit_hid", 2 * u + c - 1)
                nc.tensor.matmul(sc[c][:], sgu[:, P * c:P * c + P], unit_x[u % 4], start=True, stop=True)
                nc.tensor.matmul(pv[c][:], sgu[:, F + P * c:F + P * c + P], unit_x[u % 4], start=True, stop=True).then_inc(s["unit_gu"], 1)

        def downs(u):
            pe.wait_ge(s["unit_hid"], 2 * u + 2)
            if u == 0:
                pe.wait_ge(s["rel_ev"], 2 * NT * NP)
            at_least(pe, "unit_out", u - 1)
            for t in range(NT):
                for c in range(2):
                    mm = nc.tensor.matmul(rel[u % 2][:, P * t:P * t + P], unit_h[u % 2][:, c, P * t:P * t + P], sdn[:, c, :],
                                          start=(c == 0), stop=(c == 1), skip_group_check=True)
            mm.then_inc(s["unit_dn"], 1)

        gates_and_ups(0)
        for u in (1, 2, 3):
            gates_and_ups(u)
            downs(u - 1)
        gates_and_ups(4)
        pe.wait_ge(s["cnt_read"], 2 * NP - 1)
        finish(NP - 1, 1, 0, mix[0])
        for u in (5, 6, 7):
            downs(u - 2)
            gates_and_ups(u)
        finish(NP - 1, 1, 1, mix[0])
        downs(6)
        finish(NP - 1, 1, 2, mix[0])
        downs(7)
        finish(NP - 1, 1, 3, mix[0])
        gates_and_ups(8)
        for u in range(9, UNITS):
            gates_and_ups(u)
            downs(u - 1)
        downs(UNITS - 1)

    @block.scalar
    def _(act):
        def prep(n, b2, step, mix):
            c = 2 * n + b2
            if step == 0:
                act.wait_ge(s["xT_ps"], c + 1)
                at_least(act, "v_ps", c)
                nc.scalar.copy(xnT[:], mix[:]).then_inc(s["xnT_rdy"], 1)
            elif step == 1:
                act.wait_ge(s["q_ps"], c + 1)
                at_least(act, "qsplit", 3 * c - 1)
                nc.scalar.activation(qf[:], mix[:], ACT.Identity, bias=bq_s[:, 0:1]).then_inc(s["q_ev"], 1)
            elif step == 2:
                act.wait_ge(s["k_ps"], c + 1)
                at_least(act, "ksplit", 2 * c)
                nc.scalar.activation(kf[:, 0, :], mix[:], ACT.Identity, bias=kb[:, 0:1]).then_inc(s["k_read"], 1)
            elif step == 3:
                act.wait_ge(s["k_read"], c + 1)
                at_least(act, "nat_ps", 64 * (c - 1))
                nc.scalar.copy(kn[b2][:, 0, :], kf[:, 0, :])
            elif step < 6:
                v = step - 3
                nc.scalar.activation(kn[b2][:, v, :], kf[:, 0, :], ACT.Identity, bias=kb[:, v:v + 1])
            else:
                nc.scalar.activation(kf[:, 1, 0:S // 2], kf[:, 0, 0:S // 2], ACT.Identity, bias=kb[:, 1:2])
                nc.scalar.activation(kf[:, 1, S // 2:S], kf[:, 0, S // 2:S], ACT.Identity, bias=kb[:, 2:3]).then_inc(s["k_ev"], 1)

        prep(0, 0, 0, mix[0])
        act.wait_ge(s["pe_set"], 1)
        for dst, src in ((wqT, sc[0][:, 0:P]), (wkT, sc[0][:, P:2 * P]), (wvT, sc[0][:, 2 * P:3 * P]), (woT, sc[0][:, 3 * P:4 * P]),
                         (sgu, sc[1][:]), (sdn, mix[1][:, 0:2 * P]), (wrT, mix[1][:, 2 * P:2 * P + E])):
            view = dst[:].rearrange("p a b -> p (a b)") if len(dst.shape) == 3 else dst[:]
            last_copy = nc.scalar.copy(view, src)
        last_copy.then_inc(s["act_set"], 1)
        act.wait_ge(s["dve_set"], DVE_SET_DONE)

        def by_head(n, b2, half, heads):
            c = 2 * n + b2
            if heads[0] == 0:
                act.wait_ge(s["qsplit"], 3 * c + 3)
                at_least(act, "nat_ps", 64 * (c - 1) + 32 * (half + 1))
            src = qp[b2][:, :, 2 * half:2 * half + 2, :]
            for h in heads:
                ins = nc.scalar.activation(Qb[half][:, :, h, :].rearrange("p e (t b) -> p e t b", t=2), src, ACT.Copy, scale=hmask[:, h:h + 1])
            if heads[-1] == H - 1:
                ins.then_inc(s["qb_done"], 1)

        def exponentials(i, slot):
            tile = slot // 8
            act.wait_ge(s["s_done"], SLOTS * i + slot + 1)
            if slot % 8 == 0:
                at_least(act, "pv_done", SLOTS * i + 8 * (tile - 1))
            nc.scalar.activation(w[tile % 2][:, slot // 4 % 2, slot % 4].rearrange("p h u b -> p (h u b)"), sc[slot % 2][:], ACT.Exp,
                                 scale=escale[:, 0:1]).then_inc(s["exp_done"], 1)

        def outputs(n, t, b2):
            act.wait_ge(s["pv_done"], SLOTS * n + 32 * (t + 1) - (0 if b2 else 4))
            at_least(act, "o_st", O_STORES * (NT * n + t))
            nc.scalar.copy(pv_s[:, b2].rearrange("p h q -> p (h q)"), pv[b2][:]).then_inc(s["pv_ev"], 1)

        def finish(n, b2, step, mix):
            c = 2 * n + b2
            if step == 0:
                act.wait_ge(s["x2T_ps"], c + 1)
                at_least(act, "lg_ps", c)
                at_least(act, "x2T_st", 16 * c)
                nc.scalar.copy(x2T[:], mix[:]).then_inc(s["x2T_ev"], 1)
            else:
                act.wait_ge(s["lg_ev"], c + 1)
                nc.scalar.activation(sg[:], lmax[:], ACT.Exp, scale=-1.0).then_inc(s["sg_done"], 1)

        prep_at = {10: 0, 15: 1, 16: 2, 17: 3, 18: 4, 19: 5, 20: 6}
        finish_at = ({38: 0, 41: 1}, {44: 0, 49: 1})

        def turn(i, prev, nxt, nxt2):
            for slot in range(SLOTS):
                exponentials(i, slot)
                if slot % 32 in OUTPUTS_AT:
                    which = OUTPUTS_AT.index(slot % 32)
                    if slot > 32:
                        outputs(i, slot // 32 - 1, which)
                    elif prev:
                        outputs(i - 1, NT - 1, which)
                for half in range(2):
                    if (nxt2 if half else nxt) and slot - 64 * half in prep_at:
                        step = prep_at[slot - 64 * half]
                        prep(i + 1 + half, 1 - half, step, bank("prepare", half, min(step, 2)))
                head = slot % 32 - BY_HEAD[slot // 32]
                if 0 <= head < H:
                    ahead = slot // 32 + 1
                    if ahead < 4 and nxt:
                        by_head(i + 1, ahead // 2, ahead % 2, (head,))
                    if ahead == 4 and nxt2:
                        by_head(i + 2, 0, 0, (head,))
                for half in range(2):
                    if (prev or half == 0) and slot - FINISH[half] in finish_at[half]:
                        finish(i - half, half, finish_at[half][slot - FINISH[half]], bank("finish", half, 1))

        for step in range(1, 7):
            prep(0, 0, step, mix[0])
        by_head(0, 0, 0, range(H))
        for step in range(2):
            prep(0, 1, step, pv[0])
        by_head(0, 0, 1, range(H))
        for step in range(2, 7):
            prep(0, 1, step, pv[0])
        for half in range(2):
            by_head(0, 1, half, range(H))
        for step in range(7):
            prep(1, 0, step, pv[1])
        by_head(1, 0, 0, range(H))
        turns(act, turn)
        for b2 in range(2):
            outputs(NP - 1, NT - 1, b2)

        def silu(u):
            for c in range(2):
                act.wait_ge(s["unit_gu"], 2 * u + c + 1)
                at_least(act, "unit_hid", 2 * u + c - 3)
                nc.scalar.activation(unit_act[u % 2][:, c, :], sc[c][:], ACT.Silu).then_inc(s["unit_silu"], 1)

        def copy_y(u):
            act.wait_ge(s["unit_dn"], u + 1)
            at_least(act, unit_st[u % 4], 16 * NT * (u // 4))
            nc.scalar.copy(unit_y[u % 4].rearrange("p t d -> p (t d)"), rel[u % 2][:]).then_inc(s["unit_out"], 1)

        silu(0)
        for u in range(1, 7):
            silu(u)
            copy_y(u - 1)
        silu(7)
        finish(NP - 1, 1, 0, mix[0])
        copy_y(6)
        finish(NP - 1, 1, 1, mix[0])
        copy_y(7)
        silu(8)
        for u in range(9, UNITS):
            silu(u)
            copy_y(u - 1)
        copy_y(UNITS - 1)

    @block.vector
    def _(dve):
        count = [0]

        def link(ins):
            count[0] += 1
            ins.then_inc(s["dve_set"], 1)
            dve.wait_ge(s["dve_set"], count[0])

        for zeroed_first in (running, filled, used, *prefix, owner):
            link(nc.vector.memset(zeroed_first[:], 0.0))
        for out_bank in (*pv, *rel):
            link(nc.vector.memset(out_bank[:], 0.0))
        def moments(src, stats, mean_var, half, rs, base, step, part):
            if part == 0:
                for t in range(NT):
                    ins = nc.vector.bn_stats(stats[:, t, :], src[:, t, :])
                ins.then_inc(s[step], 1)
                return
            dve.wait_ge(s[step], base + 1)
            dve.sem_inc(s["dve_passed"], 1)
            for t in range(NT):
                ins = nc.vector.bn_aggr(mean_var[:, t, :], stats[:, t, :])
            ins.then_inc(s[step], 1)
            for k in range(3):
                dve.wait_ge(s[step], base + 2 + k)
                root_guess_step(nc.vector, k, mean_var, half, rs).then_inc(s[step], 1)

        def normalize(dst, src, mean_var, rs, root, roots):
            dve.wait_ge(s[root], NEWTON_STEPS * (roots + 1))
            for t in range(NT):
                ins = nc.vector.tensor_scalar(dst[:, t, :], src[:, t, :], mean_var[:, t, 0:1], rs[:, t:t + 1], ALU.subtract, ALU.mult)
            return ins

        def prep(n, b2, step, mix=None):
            c = 2 * n + b2
            if step < 2:
                if step == 0:
                    dve.wait_ge(x_ld[b2], 16 * (n + 1))
                moments(xt[b2], st, mv, var, rstd, 5 * c, "xn_step", step)
            elif step == 2:
                at_least(dve, "xT_ps", c)
                normalize(xn, xt[b2], mv, rstd, "root", c).then_inc(s["xn_done"], 1)
            else:
                dve.wait_ge(s["v_ps"], c + 1)
                at_least(dve, "vs_st", 16 * c)
                src = mix[:].rearrange("p (t h d) -> p t h d", t=NT, h=H)
                for v, tiles, far in ((0, slice(0, NT), 0), (1, slice(0, 2), 1), (2, slice(2, NT), 1)):
                    nt = tiles.stop - tiles.start
                    bias = vb[:, v:v + 1, :].rearrange("p o (h d) -> p o h d", d=HD).broadcast_to([P, nt, H, HD])
                    ins = nc.vector.tensor_tensor(vst[:, tiles, far, :, 0:HD], src[:, tiles], bias, ALU.add)
                ins.then_inc(s["v_ev"], 1)

        for step in range(3):
            prep(0, 0, step)
        dve.wait_ge(s["w_ld"], 16 * LOADS)
        link(nc.vector.memset(bnd[:], 0.0))
        for n, bias in ((0, bqr), (1, bkr[:, 0:1])):
            link(nc.vector.tensor_reduce(bnd[:, 4:5], wraw[n], AX.X, ALU.add, apply_absolute_value=True))
            link(nc.vector.tensor_reduce(bnd[:, 5:6], bias, AX.X, ALU.max, apply_absolute_value=True))
            link(nc.vector.scalar_tensor_tensor(out=bnd[:, n:n + 1], in0=bnd[:, 4:5], scalar=XMAX, in1=bnd[:, 5:6],
                                                op0=ALU.mult, op1=ALU.add))
        link(nc.vector.tensor_reduce(bnd[0:HD, 2:3], rkT, AX.X, ALU.max, apply_absolute_value=True))
        assert count[0] == BOUNDS
        dve.wait_ge(s["pool_set"], BOUNDS_MAX)
        link(nc.vector.tensor_copy(bnd[:, 4:5], bmax[:, 0:1]))
        link(nc.vector.tensor_tensor(bnd[:, 5:6], bmax[:, 1:2], bmax[:, 2:3], ALU.add))
        link(nc.vector.tensor_scalar(bnd[:, 6:8], bnd[:, 4:6], 2.0 ** -100, 2.0 ** 100, ALU.max, ALU.min))
        link(nc.vector.tensor_scalar(pw[:, 0:2].bitcast(I32), bnd[:, 6:8].bitcast(I32), 0x7F800000, None, ALU.bitwise_and))
        link(nc.vector.tensor_scalar(pw[:, 2:4].bitcast(I32), pw[:, 0:2].bitcast(I32), -1.0, float(266 << 23), ALU.mult, ALU.add))
        link(nc.vector.tensor_scalar(wraw[0], wraw[0], pw[:, 2:3], None, ALU.mult))
        link(nc.vector.tensor_scalar(wraw[1], wraw[1], pw[:, 3:4], None, ALU.mult))
        assert count[0] == SCALED
        link(nc.vector.tensor_scalar(rkT, rkT, pw[0:HD, 3:4], None, ALU.mult))
        link(nc.vector.memset(rzero, 0.0))
        link(nc.vector.tensor_scalar(rpad[:, 0:OFF0 - M], rzero[:, 0:OFF0 - M], rkT[:, 0:1], None, ALU.add))
        link(nc.vector.tensor_copy(rpad[:, OFF0 - M:OFF0 + M + 1], rkT))
        link(nc.vector.tensor_scalar(rpad[:, OFF0 + M + 1:512], rzero[:, 0:512 - OFF0 - M - 1], rkT[:, 2 * M:2 * M + 1], None, ALU.add))
        link(nc.vector.tensor_copy(rpart[0], rpad))
        link(nc.vector.tensor_tensor(rpart[1], rpad, rpart[0], ALU.subtract))
        assert count[0] == RPART_READY
        link(nc.vector.tensor_scalar(bq_s[:], bqr, pw[:, 2:3], None, ALU.mult))
        link(nc.vector.tensor_scalar(kb[:, 0:1], bkr[:, 0:1], pw[:, 3:4], None, ALU.mult))
        link(nc.vector.tensor_scalar(kb[:, 1:3], bkr[:, 1:3], pw[:, 3:4], None, ALU.mult))
        link(nc.vector.tensor_tensor(bnd[:, 3:4], pw[:, 2:3], pw[:, 3:4], ALU.mult))
        link(nc.vector.reciprocal(bnd[:, 4:5], bnd[:, 3:4]))
        link(nc.vector.tensor_scalar(escale[:], bnd[:, 4:5], HD ** -0.5, None, ALU.mult))
        dve.wait_ge(s["w_ld2"], 16 * MORE_LOADS)
        link(nc.vector.tensor_copy(vb[:, 0, :], vraw[:, 0, :]))
        for n in (1, 2):
            link(nc.vector.tensor_tensor(vb[:, n, :], vraw[:, 0, :], vraw[:, n, :], ALU.add))
        link(nc.vector.tensor_copy(number[:], number_i[:]))
        link(nc.vector.tensor_copy(tau[:], tau_i[:]))
        assert count[0] == DVE_SET_DONE

        def row_max(n, b2, k, nat):
            c = 2 * n + b2
            t = k // 16
            if k % 16 == 0:
                at_least(dve, "ms_done", NT * (c - 1) + t + 1)
            dve.wait_ge(s["nat_ps"], 64 * c + k + 1)
            nc.vector.tensor_reduce(mx[:, k:k + 1], nat[:], AX.X, ALU.max).then_inc(s["mx_done"], 1)
            if k % 16 == 15:
                group = NT * c + t
                cols = slice(16 * t, 16 * t + 16)
                dve.wait_ge(s["mx_done"], 64 * c + k + 1)
                at_least(dve, "ms_st", 32 * (group - NT + 1))
                nc.vector.tensor_scalar(ms[:, 0, cols], mx[:, cols], MAXSCALE, None, ALU.mult).then_inc(s["ms_step"], 1)
                dve.wait_ge(s["ms_step"], group + 1)
                nc.vector.scalar_tensor_tensor(out=ms[:, 1, cols], in0=mx[:, cols], scalar=MAXSCALE, in1=ms[:, 0, cols],
                                               op0=ALU.mult, op1=ALU.subtract).then_inc(s["ms_done"], 1)

        def outputs(n, t, half):
            dve.wait_ge(s["pv_done"], SLOTS * n + 32 * (t + 1) - (0 if half else 4))
            at_least(dve, "o_st", O_STORES * (NT * n + t))
            nc.vector.tensor_copy(rel_s[:, :, :, 4 * half:4 * half + 4].rearrange("p h u b -> p (h u) b"),
                                  rel[half][:].rearrange("p (b c) -> p c b", b=4)).then_inc(s["rel_ev"], 1)

        def finish(n, half, step, mix):
            c = 2 * n + half
            base = 12 * c
            if step == 0:
                dve.wait_ge(s["o_ld"], 128 * (c + 1))
                nc.vector.tensor_tensor(oA[:], oA[:], oB[:], ALU.add).then_inc(s["o_step"], 1)
            elif step < 5:
                cols = slice(P * (step - 1), P * step)
                ins = nc.vector.reciprocal(oS[:, cols], oS[:, cols])
                if step == 4:
                    ins.then_inc(s["o_step"], 1)
            elif step == 5:
                dve.wait_ge(s["o_step"], 2 * c + 2)
                nc.vector.tensor_tensor(oA[:], oA[:], oS[:], ALU.mult).then_inc(s["O_rdy"], 1)
            elif step == 6:
                dve.wait_ge(s["op_ps"], c + 1)
                nc.vector.tensor_tensor(y[:], mix[:].rearrange("p (t d) -> p t d", t=NT),
                                        bo_s[:].rearrange("p (o d) -> p o d", o=1).broadcast_to([P, NT, D]), ALU.add).then_inc(s["ln_step"], 1)
            elif step in (7, 8):
                if step == 7:
                    dve.wait_ge(s["ln_step"], base + 1)
                moments(y, st2, mv2, var2, rstd2, base + 1, "ln_step", step - 7)
            elif step == 9:
                normalize(y, y, mv2, rstd2, "root2", 2 * c).then_inc(s["ln_step"], 1)
            elif step == 10:
                dve.wait_ge(s["ln_step"], base + 7)
                at_least(dve, scat, 64 * c)
                nc.vector.tensor_tensor(xs[:, :, HALF:HALF + D], xr[:], y[:], ALU.add).then_inc(s["x1_done"], 1)
            elif step in (11, 12):
                if step == 11:
                    dve.wait_ge(s["x1_done"], c + 1)
                moments(xs[:, :, HALF:HALF + D], st2, mv2, var2, rstd2, base + 7, "ln_step", step - 11)
            elif step == 13:
                normalize(xs[:, :, 0:D], xs[:, :, HALF:HALF + D], mv2, rstd2, "root2", 2 * c + 1).then_inc(s["xn2_done"], 1)
            elif step == 14:
                dve.wait_ge(s["lg_ps"], c + 1)
                base = 4 * c
                lps = mix[:, 0:NT * E].rearrange("p (t e) -> p t e", t=NT)
                nc.vector.tensor_copy(lg[:], lps).then_inc(s["lg_read"], 1)
            elif step == 15:
                base = 3 * c
                dve.wait_ge(s["lg_read"], c + 1)
                nc.vector.tensor_reduce(lmax[:], lg[:], AX.X, ALU.max).then_inc(s["lg_ev"], 1)
                dve.wait_ge(s["lg_ev"], c + 1)
                nc.vector.tensor_tensor(cand[:], lg[:], lmax[:].rearrange("p (t o) -> p t o", o=1).broadcast_to([P, NT, E]), ALU.is_ge).then_inc(s["top_step"], 1)
                dve.wait_ge(s["top_step"], base + 1)
                iota = iota_e[:].rearrange("p (o e) -> p o e", o=1).broadcast_to([P, NT, E])
                nc.vector.tensor_tensor(cand[:], cand[:], iota, ALU.mult).then_inc(s["top_step"], 1)
                dve.wait_ge(s["top_step"], base + 2)
                nc.vector.tensor_reduce(lidx[:], cand[:], AX.X, ALU.min).then_inc(s["top_step"], 1)
                dve.wait_ge(s["top_step"], base + 3)
                nc.vector.tensor_tensor(oh[:], iota, lidx[:].rearrange("p (t o) -> p t o", o=1).broadcast_to([P, NT, E]), ALU.is_equal).then_inc(s["oh_rdy"], 1)
            elif step == 16:
                dve.wait_ge(s["sg_done"], c + 1)
                nc.vector.tensor_scalar(sg[:], sg[:], 1.0, None, ALU.add).then_inc(s["sg_step"], 1)
                dve.wait_ge(s["sg_step"], 2 * c + 1)
                nc.vector.reciprocal(sg[:], sg[:]).then_inc(s["sg_step"], 1)
                dve.wait_ge(s["sg_step"], 2 * c + 2)
                for t in range(NT):
                    nc.vector.tensor_scalar(xs[:, t, 0:D], xs[:, t, 0:D], sg[:, t:t + 1], None, ALU.mult)
                at_least(dve, "number_step", c)
                nc.vector.tensor_copy(xs[:, :, 2 * D], number[:]).then_inc(s["xs_done"], 1)
                dve.wait_ge(s["xs_done"], c + 1)
                nc.vector.tensor_scalar(number[:], number[:], float(S // 2 if half == 0 else 2 * S - S // 2), None, ALU.add).then_inc(s["number_step"], 1)

        def by_expert(x):
            return x.rearrange("p (o e) -> p o e", o=1).broadcast_to([P, NT, E])

        def place_tokens(n, half, part, mix):
            c = 2 * n + half
            done = PLACE_STEPS * c
            vec = nc.vector
            new_rows = prefix[0][:, 8:]

            def link(k, ins):
                ins.then_inc(s["al_step"], 1)

            def running_total(k):
                src, dst = prefix[0 if k == 0 else 1 + (k + 1) % 2], prefix[1 + k % 2]
                back = 8 - (1 << k)
                return vec.tensor_tensor(dst[:, 8:], src[:, 8:], src[:, back:back + E], ALU.add)

            if part > 0:
                at_least(dve, "al_step", done + part - 1)
            if part == 0:
                dve.wait_ge(s["cnt_ps"], c + 1)
                vec.tensor_copy(counted[:].rearrange("p a t e -> p (a t e)"), mix[:, 0:2 * NT * E]).then_inc(s["cnt_read"], 1)
            elif part == 1:
                dve.wait_ge(s["cnt_read"], c + 1)
                link(1, vec.tensor_tensor(running[:, 1, :], running[:, 0, :], counted[:, 1, 0, :], ALU.add))
            elif part == 2:
                link(2, vec.tensor_tensor(running[:, 2, :], running[:, 1, :], counted[:, 1, 1, :], ALU.add))
            elif part == 3:
                link(3, vec.tensor_tensor(running[:, 3, :], running[:, 2, :], counted[:, 1, 2, :], ALU.add))
            elif part == 4:
                link(4, vec.tensor_tensor(running[:, 4, :], running[:, 3, :], counted[:, 1, 3, :], ALU.add))
            elif part == 5:
                link(5, vec.tensor_tensor(pos[:], running[:, 0:NT, :], counted[:, 0], ALU.add))
            elif part == 6:
                link(6, vec.tensor_scalar(rounded[:], running[:, NT, :], P / 2 - 0.5, ROUND, ALU.add, ALU.add))
            elif part == 7:
                link(7, vec.scalar_tensor_tensor(out=new_rows, in0=rounded[:], scalar=ROUND, in1=filled[:], op0=ALU.subtract, op1=ALU.subtract))
            elif part == 8:
                link(8, running_total(0))
            elif part == 9:
                link(9, running_total(1))
            elif part == 10:
                link(10, running_total(2))
            elif part == 11:
                link(11, running_total(3))
            elif part == 12:
                link(12, vec.scalar_tensor_tensor(out=first_row[:], in0=prefix[2][:, 8:], scalar=used[:, 0:1], in1=new_rows, op0=ALU.add, op1=ALU.subtract))
            elif part == 13:
                link(13, vec.tensor_tensor(used[:], used[:], prefix[2][:, 7 + E:8 + E], ALU.add))
            elif part == 14:
                link(14, vec.tensor_tensor(jump[:], first_row[:], filled[:], ALU.subtract))
            elif part == 15:
                link(15, vec.tensor_tensor(spot[:], pos[:], by_expert(filled[:]), ALU.is_ge))
            elif part == 16:
                link(16, vec.tensor_tensor(spot[:], spot[:], by_expert(jump[:]), ALU.mult))
            elif part == 17:
                link(17, vec.tensor_tensor(spot[:], spot[:], pos[:], ALU.add))
            elif part == 18:
                link(18, vec.tensor_tensor(spot[:], spot[:], oh[:], ALU.mult))
            elif part == 19:
                link(19, vec.tensor_reduce(spot_t[:], spot[:], AX.X, ALU.add))
            elif part == 20:
                at_least(dve, scat, 64 * c)
                dve.sem_inc(s["dve_passed"], 1)
                vec.tensor_copy(spot_u[:], spot_t[:])
                vec.tensor_copy(spots[:, bass.ds(NT * c, NT)], spot_t[:]).then_inc(s["spot_rdy"], 1)
                link(20, vec.scalar_tensor_tensor(out=jump[:], in0=new_rows, scalar=0.0, in1=jump[:], op0=ALU.is_gt, op1=ALU.mult))
            elif part == 21:
                link(21, vec.tensor_tensor(running[:, 0, :], running[:, NT, :], jump[:], ALU.add))
            elif part == 22:
                link(22, vec.tensor_tensor(filled[:], filled[:], new_rows, ALU.add))
            elif part == 23:
                link(23, vec.tensor_tensor(filled[:], filled[:], jump[:], ALU.add))
            elif part == 24:
                link(24, vec.tensor_tensor(below[1][:], new_rows, first_row[:], ALU.add))
            elif part == 25:
                link(25, vec.tensor_scalar(below[0][:], first_row[:], tau[:, 0:1], None, ALU.is_le))
            elif part == 26:
                link(26, vec.scalar_tensor_tensor(out=below[0][:], in0=below[1][:], scalar=tau[:, 0:1], in1=below[0][:], op0=ALU.is_le, op1=ALU.subtract))
            elif part == 27:
                link(27, vec.tensor_tensor(owner[:], owner[:], below[0][:], ALU.subtract))

        prep_at = ({1: 0, 2: 1, 7: 2, 21: 3}, {-19: 0, -18: 1, -12: 2, 21: 3})
        finish_at = ({7: 0, 8: 1, 9: 2, 10: 3, 11: 4, 14: 5, 15: 6, 17: 7, 20: 8, 27: 9, 28: 10, 31: 11, 32: 12, 36: 13, 39: 14, 40: 15, 41: 16},
                     {9: 0, 16: 1, 17: 2, 18: 3, 19: 4, 22: 5, 25: 6, 26: 7, 27: 8, 30: 9, 34: 10, 35: 11, 36: 12, 41: 13, 46: 14, 49: 15, 50: 16})
        place_at = ([(41, 0)] + [(42 + part, part) for part in range(1, PLACE_STEPS + 1)],
                    [(54, 0)] + [(54 + part // 2, part) for part in range(1, PLACE_STEPS + 1)])

        def turn(i, prev, nxt, nxt2):
            for slot in range(SLOTS):
                if slot % 32 in OUTPUTS_AT:
                    which = OUTPUTS_AT.index(slot % 32)
                    if slot > 32:
                        outputs(i, slot // 32 - 1, which)
                    elif prev:
                        outputs(i - 1, NT - 1, which)
                if nxt:
                    row_max(i + 1, slot // 64, slot % 64, bank("row max", slot))
                for half in range(2):
                    if (nxt2 if half else nxt) and slot - 64 * half in prep_at[half]:
                        prep(i + 1 + half, 1 - half, prep_at[half][slot - 64 * half], bank("prepare", half, 3))
                for n, half, since in finishing(slot, i, prev):
                    if since in finish_at[half]:
                        step = finish_at[half][since]
                        finish(n, half, step, bank("finish", half, 0 if step == 6 else 2))
                    for at, part in place_at[half]:
                        if since == at:
                            place_tokens(n, half, part, bank("finish", half, 3))

        dve.wait_ge(s["zeroed"], ZEROED_FIRST)
        for step in range(2):
            prep(0, 1, step)
        prep(0, 0, 3, mix[0])
        for k in range(128):
            row_max(0, k // 64, k % 64, (*mix, *sc)[k % 4])
            if k in PROLOGUE_DVE[0]:
                prep(0, 1, PROLOGUE_DVE[0][k], pv[0])
            if k in PROLOGUE_DVE[1]:
                prep(1, 0, PROLOGUE_DVE[1][k], pv[1])
        turns(dve, turn)
        for half in range(2):
            outputs(NP - 1, NT - 1, half)

        def hidden(u):
            for c in range(2):
                dve.wait_ge(s["unit_silu"], 2 * u + c + 1)
                at_least(dve, "unit_dn", u - 1)
                nc.vector.tensor_tensor(unit_h[u % 2][:, c, :], unit_act[u % 2][:, c, :], pv[c][:], ALU.mult).then_inc(s["unit_hid"], 1)

        last = NP - 1
        hidden_at = {14: 0, PLACE_STEPS: 1}
        for since, part in place_at[0]:
            if since >= SLOTS - FINISH[0]:
                place_tokens(last, 0, part, bank("finish", 0, 3))
                if part in hidden_at:
                    hidden(hidden_at[part])
        for u, steps in ((3, range(0, 6)), (4, range(6, 9)), (5, range(9, 13)), (7, range(13, 16))):
            for earlier in range({3: 2, 4: 4, 5: 5, 7: 6}[u], u + 1):
                hidden(earlier)
            for step in steps:
                finish(last, 1, step, mix[0])
        place_tokens(last, 1, 0, mix[0])
        finish(last, 1, 16, mix[0])
        for u in range(8, UNITS):
            hidden(u)
            for part in range(1, PLACE_STEPS + 1):
                if (part - 1) // 9 == u - 8:
                    place_tokens(last, 1, part, None)

    @block.gpsimd
    def _(pool):
        ps_ = s["pool_set"]
        pool.memset(ident[:], 0.0).then_inc(ps_, 1)
        pool.memset(ones[:], 1.0).then_inc(ps_, 1)
        pool.wait_ge(ps_, 2)
        pool.affine_select(out=ident[:], in_=ident[:], compare_op=ALU.not_equal, fill=1.0, base=0,
                           pattern=[[-1, P]], channel_multiplier=1).then_inc(ps_, 1)
        pool.affine_select(out=tri, in_=ones[:], compare_op=ALU.is_gt, fill=0.0, base=0,
                           pattern=[[1, P]], channel_multiplier=-1).then_inc(ps_, 1)
        pool.tensor_copy(ones16[:], ones[:]).then_inc(ps_, 1)
        pool.affine_select(out=hmask[:], in_=ones[:, 0:H], compare_op=ALU.is_ge, fill=0.0, base=0,
                           pattern=[[-HD, H]], channel_multiplier=1).then_inc(ps_, 1)
        pool.wait_ge(ps_, 6)
        pool.tensor_copy(tri16[:], tri).then_inc(ps_, 1)
        pool.iota(tau_i[:], [[0, 1]], base=0, channel_multiplier=P).then_inc(ps_, 1)
        pool.affine_select(out=hmask[:], in_=hmask[:], compare_op=ALU.is_ge, fill=0.0, base=HD - 1,
                           pattern=[[HD, H]], channel_multiplier=-1).then_inc(ps_, 1)
        pool.iota(number_i[:], [[S, 2], [P, NT // 2]], base=1, channel_multiplier=1).then_inc(ps_, 1)
        def split(n, b2):
            c = 2 * n + b2
            pool.wait_ge(s["q_ev"], c + 1)
            at_least(pool, "qs_st", 48 * c)
            at_least(pool, "qn_st", 16 * (c - 1))
            at_least(pool, "qb_done", 2 * (c - 1))
            pool.sem_inc(s["pool_passed"], 1)
            pool.tensor_copy(qs[:, 0, :], qf[:]).then_inc(s["qsplit"], 1)
            pool.wait_ge(s["qsplit"], 3 * c + 1)
            pool.tensor_tensor(qs[:, 1, :], qf[:], qs[:, 0, :], ALU.subtract).then_inc(s["qsplit"], 1)
            pool.tensor_copy(qp[b2][:], qs[:, 0, :].rearrange("p (t e b) -> p e t b", t=NT, e=NE8)).then_inc(s["qsplit"], 1)
            pool.wait_ge(s["k_ev"], c + 1)
            at_least(pool, "ks_st", 48 * c)
            pool.sem_inc(s["pool_passed"], 1)
            src = kf[:].rearrange("p v (t k) -> p t v k", t=NT)
            pool.tensor_copy(ks[:, 0], src).then_inc(s["ksplit"], 1)
            pool.wait_ge(s["ksplit"], 2 * c + 1)
            pool.tensor_tensor(ks[:, 1], src, ks[:, 0], ALU.subtract).then_inc(s["ksplit"], 1)

        def refine(root, ve, tmp, name, n):
            for k in range(NEWTON_STEPS):
                newton_step(pool, k, root, ve, tmp, c15).then_inc(s[name], 1)
                pool.wait_ge(s[name], NEWTON_STEPS * n + k + 1)

        def root(n, b2):
            c = 2 * n + b2
            pool.wait_ge(s["xn_step"], 5 * c + 5)
            refine(rstd, var, rtmp, "root", c)

        def root2(n, half, k):
            c = 2 * n + half
            pool.wait_ge(s["ln_step"], 12 * c + 6 * (k + 1))
            refine(rstd2, var2, rtmp2, "root2", 2 * c + k)

        def roots2(n, half):
            for k in range(2):
                root2(n, half, k)

        def scatter(n, half):
            c = 2 * n + half
            pool.wait_ge(s["z_st"], ZERO_STORES)
            pool.wait_ge(s["xs_done"], c + 1)
            pool.wait_ge(s["spot_rdy"], c + 1)
            pool.sem_inc(s["pool_passed"], 1)
            for t in range(NT):
                pool.indirect_dma_start(xs_d, bass.IndirectOffsetOnAxis(ap=spot_u[:, t:t + 1], axis=0), xs[:, t, :], None).then_inc(scat, 16)

        def prepare(n, b2):
            root(n, b2)
            split(n, b2)

        def turn(i, prev, nxt, nxt2):
            if nxt:
                root(i + 1, 1)
            if nxt:
                split(i + 1, 1)
            if prev:
                scatter(i - 1, 0)
            if nxt2:
                root(i + 2, 0)
            if prev:
                roots2(i - 1, 1)
            if nxt2:
                split(i + 2, 0)
            if prev:
                scatter(i - 1, 1)
            roots2(i, 0)

        z = s["zeroed"]
        pool.memset(c15[:], 1.5).then_inc(z, 1)
        pool.wait_ge(z, 1)
        root(0, 0)
        pool.wait_ge(s["dve_set"], BOUNDS)
        for n in range(3):
            pool.partition_all_reduce(bmax[:, n:n + 1], bnd[:, n:n + 1], P, bass.bass_isa.ReduceOp.max).then_inc(ps_, 1)

        def zeros(buf, value=0.0):
            flat = buf[:].rearrange({5: "p a b c d -> p (a b c d)", 4: "p a b c -> p (a b c)", 3: "p a b -> p (a b)", 2: "p a -> p a"}[len(buf.shape)])
            pool.memset(flat.bitcast(F32) if value == 0.0 else flat, value).then_inc(z, 1)

        zeros(Qn)
        pool.memset(vst[:, :, :, :, HD:HD + 1].rearrange("p a b c o -> p (a b) (c o)"), 1.0).then_inc(z, 1)
        for e in range(E):
            pool.memset(iota_e[:, e:e + 1], float(e - E)).then_inc(z, 1)
        split(0, 0)
        root(0, 1)
        split(0, 1)
        for buf in (*QC, *QT, zrow):
            zeros(buf)
        for j in range(NT):
            zeros(KC[j], -1.0 / MAXSCALE)
        prepare(1, 0)
        turns(pool, turn)
        scatter(NP - 1, 0)

        def scatter_unit(u):
            pool.wait_ge(s["unit_out"], u + 1)
            pool.wait_ge(s["z_st"], 2 * ZERO_STORES)
            for t in range(NT):
                pool.indirect_dma_start(ysh_d, bass.IndirectOffsetOnAxis(ap=spots[:, NT * u + t:NT * u + t + 1], axis=0),
                                        unit_y[u % 4][:, t, :], None).then_inc(unit_st[u % 4], 16)

        for u in range(3):
            scatter_unit(u)
        root2(NP - 1, 1, 0)
        scatter_unit(3)
        root2(NP - 1, 1, 1)
        for u in range(4, 11):
            scatter_unit(u)
        scatter(NP - 1, 1)
        for u in range(11, UNITS):
            scatter_unit(u)
        pool.wait_ge(scat, 64 * 2 * NP)
        for r in range(4):
            pool.wait_ge(unit_st[r], 16 * NT * (UNITS // 4))


IDENT_READY = 3
EARLY = 7 + 4
BOUNDS = EARLY + 8
BOUNDS_MAX = 13
SCALED = BOUNDS + 7
RPART_READY = SCALED + 7
DVE_SET_DONE = RPART_READY + 3 + 3 + 3 + 2
ZEROED_FIRST = 3 + E
ZEROED = ZEROED_FIRST + 5 + NT
NEWTON_STEPS = 12
PLACE_STEPS = 27
ROUND = 1.5 * 2.0 ** 30
QN_LOADS = 16 * NE8
QC_LOADS = 16 * 8
KC_LOADS = 16 * 5
O_STORES = 16 * (8 + 16)
TABLE_LOADS = 2 * NE8
ZERO_TILES = 16
ZERO_STORES = 16 * (SORTED // ZERO_TILES)
PREPARE_PE = {10: 0, 15: 1, 16: 2, 21: 3}
FINISH_PE = ({15: 0, 38: 1, 39: 2, 41: 3}, {25: 0, 44: 1, 46: 2, 54: 3})
PROLOGUE_PE = ({4: 0, 12: 1, 18: 2, 30: 3}, {68: 0, 72: 1, 80: 2, 90: 3})
PROLOGUE_DVE = ({2: 2, 33: 3}, {20: 0, 21: 1, 62: 2, 93: 3})
BY_HEAD = (1, 10, 6, 14)
OUTPUTS_AT = (5, 8)
FINISH = (85, 24)


MOE_SEMS = ("scat we_ld cnt_ps2 cnt_step eid_rdy iotas xs_ld0 xs_ld1 x1_ld0 x1_ld1 ysh_ld0 ysh_ld1 sT_ps sT_ev we_done gu_ps silu_done "
            "h_done y_ps y_ev st_step mv_step dve_passed2 pool_passed2 fin_step root3 oidx_step oidx_rdy out_rdy out_st0 out_st1")
RING = 8
GROUP = 8
GROUPS = SORTED // GROUP
ROW = 2 * D + 1
HALF = D
NOWHERE = 1 << 20


def expert_phase(nc, ctx, a):
    s = a["moe_sem"]
    xs_d, ysh_d, out = a["xs_d"], a["ysh_d"], a["out"]
    ident, ones, iota_e, owner, WE, c15 = (a[n] for n in "ident ones iota_e owner WE c15".split())

    def sb(name, shape, dt=F32):
        return ctx.enter_context(nc.sbuf_tensor(name, shape, dt))

    def pb(name, shape, dt=F32):
        return ctx.enter_context(nc.psum_tensor(name, shape, dt))

    eid_p = sb("eid_p", [P, 1])
    eid_e = sb("eid_e", [P, E])
    diag = sb("diag", [P, P])
    eid = sb("eid", [1, SORTED], I32)
    pad_i = sb("pad_i", [P, GROUP], I32)
    pad = sb("pad", [P, GROUP])
    srow = [sb(f"srow{r}", [P, GROUP, D]) for r in range(2)]
    x1g = [sb(f"x1g{r}", [P, GROUP, D + 1]) for r in range(2)]
    ysh = [sb(f"ysh{r}", [P, GROUP, D]) for r in range(2)]
    sT = [sb(f"sT{r}", [P, P]) for r in range(2)]
    we = [sb(f"we{r}", [P, 2 * F + 2 * D]) for r in range(RING)]
    act_s = [sb(f"act_s{r}", [P, 2, P]) for r in range(2)]
    hT = [sb(f"hT{r}", [P, 2, P]) for r in range(4)]
    yg = [sb(f"yg{r}", [P, GROUP, D]) for r in range(2)]
    st3 = [sb(f"st3{r}", [P, GROUP, 6]) for r in range(2)]
    mv3 = [sb(f"mv3{r}", [P, GROUP, 2]) for r in range(2)]
    var3, rstd3 = ([sb(f"{n}{r}", [P, GROUP]) for r in range(2)] for n in ("var3_", "rstd3_"))
    rtmp3 = sb("rtmp3", [P, GROUP])
    c15g = sb("c15g", [P, GROUP])
    og = [sb(f"og{r}", [P, GROUP, D]) for r in range(2)]
    oidx_f = [sb(f"oidx_f{r}", [P, GROUP]) for r in range(2)]
    oidx = [sb(f"oidx{r}", [P, GROUP], U32) for r in range(2)]

    gu = [pb(f"gu{r}", [P, 4, P]) for r in range(2)]
    tr = [pb(f"tr{r}", [P, P]) for r in range(2)]
    y_p = [pb(f"y_p{r}", [P, D]) for r in range(4)]

    def ring(name, n):
        return [s[f"{name}{r}"] for r in range(n)]

    xs_ld, x1_ld, ysh_ld, out_st = ring("xs_ld", 2), ring("x1_ld", 2), ring("ysh_ld", 2), ring("out_st", 2)

    def at_least(eng, semaphore, value):
        if not (isinstance(value, int) and value <= 0):
            eng.wait_ge(semaphore, value)

    def loop(eng, body):
        body(0, True, False)
        with eng.Fori(1, GROUPS // 2 - 1) as i:
            body(i, False, False)
        body(GROUPS // 2 - 1, False, True)

    def times(g, r, per_group):
        return per_group * (g // 2) if isinstance(g, int) else per_group // 2 * (g - r)

    block = ctx.enter_context(nc.Block())

    @block.sync
    def _(sp):
        def rows(src, g, c0, c1):
            return src[bass.ds(g * GROUP * P, GROUP * P), c0:c1].rearrange("(k p) n -> p k n", p=P)

        def load_rows(g, r):
            at_least(sp, s["sT_ps"], GROUP * (g - 1))
            sp.dma_start(srow[r][:], rows(xs_d, g, 0, D)).then_inc(xs_ld[r], 16)

        def load_ysh(g, r):
            at_least(sp, s["y_ev"], GROUP * (g - 1))
            sp.dma_start(ysh[r][:], rows(ysh_d, g, 0, D)).then_inc(ysh_ld[r], 16)

        def load_x1(g, r):
            at_least(sp, s["out_rdy"], 2 * (g - 1))
            sp.dma_start(x1g[r][:], rows(xs_d, g, D, ROW)).then_inc(x1_ld[r], 16)

        load_rows(0, 0)
        load_ysh(0, 0)

        def groups(i, first, last):
            for r in range(2):
                if not (last and r == 1):
                    load_rows(2 * i + r + 1, 1 - r)
                load_x1(2 * i + r, r)
                if not (last and r == 1):
                    load_ysh(2 * i + r + 1, 1 - r)
        loop(sp, groups)

    @block.gpsimd
    def _(pool):
        pool.iota(pad_i[:], [[P, GROUP]], base=NOWHERE, channel_multiplier=1).then_inc(s["iotas"], 1)
        pool.memset(c15g[:], 1.5).then_inc(s["iotas"], 1)
        def store(g, r):
            pool.wait_ge(s["oidx_rdy"], g + 1)
            pool.sem_inc(s["pool_passed2"], 1)
            for k in range(GROUP):
                if k % (GROUP // 2) == 0:
                    pool.wait_ge(s["out_rdy"], 2 * g + 2 * k // GROUP + 1)
                    pool.sem_inc(s["pool_passed2"], 1)
                pool.indirect_dma_start(out.rearrange("b s d -> (b s) d"), bass.IndirectOffsetOnAxis(ap=oidx[r][:, k:k + 1], axis=0),
                                        og[r][:, k, :], None, bounds_check=TOK - 1, oob_is_err=False).then_inc(out_st[r], 16)

        def groups(i, first, last):
            for r in range(2):
                store(2 * i + r, r)
        loop(pool, groups)
        for r in range(2):
            pool.wait_ge(out_st[r], 16 * GROUP * (GROUPS // 2))

    @block.tensor
    def _(pe):
        pe.wait_ge(s["cnt_step"], 3)
        nc.tensor.matmul(gu[0][:, 0, :], ones[:], diag[:], start=True, stop=True).then_inc(s["cnt_ps2"], 1)
        pe.wait_ge(s["eid_rdy"], 1)

        def transpose_rows(n, m, i):
            k, r = m % GROUP, m // GROUP
            if k == 0:
                pe.wait_ge(xs_ld[r], 16 * (i + 1))
            at_least(pe, s["sT_ev"], n - 1)
            nc.tensor.transpose(tr[k % 2][:], srow[r][:, k, :], ident[:]).then_inc(s["sT_ps"], 1)

        def gates_and_ups(n, m):
            pe.wait_ge(s["sT_ev"], n + 1)
            pe.wait_ge(s["we_done"], n + 1)
            at_least(pe, s["h_done"], n - 1)
            for c in range(4):
                mm = nc.tensor.matmul(gu[m % 2][:, c, :], we[m % RING][:, P * c:P * c + P], sT[m % 2][:], start=True, stop=True)
            mm.then_inc(s["gu_ps"], 1)

        def downs(n, m):
            pe.wait_ge(s["h_done"], n + 1)
            at_least(pe, s["y_ev"], n - 3)
            for c in range(2):
                mm = nc.tensor.matmul(y_p[m % 4][:], hT[m % 4][:, c, :], we[m % RING][:, 2 * F + D * c:2 * F + D * c + D], start=(c == 0), stop=(c == 1))
            mm.then_inc(s["y_ps"], 1)

        transpose_rows(0, 0, 0)

        def groups(i, first, last):
            for m in range(2 * GROUP):
                n = 2 * GROUP * i + m
                if m < 2 * GROUP - 1:
                    transpose_rows(n + 1, m + 1, i)
                elif not last:
                    transpose_rows(n + 1, 0, i + 1)
                gates_and_ups(n, m)
                if not (first and m < 2):
                    downs(n - 2, m - 2)
        loop(pe, groups)
        for n in (SORTED - 2, SORTED - 1):
            downs(n, n)

    @block.scalar
    def _(act):
        act.wait_ge(s["we_ld"], 48)
        act.wait_ge(s["eid_rdy"], 1)

        def weights(n, m):
            at_least(act, s["y_ps"], n - RING + 1)
            e = act.value_load(eid[0:1, bass.ds(n, 1)], min_val=0, max_val=E - 1)
            nc.scalar.copy(we[m % RING][:], WE[:, bass.ds(e, 1), :].rearrange("p o n -> p (o n)")).then_inc(s["we_done"], 1)

        def copy_rows(n, m):
            act.wait_ge(s["sT_ps"], n + 1)
            at_least(act, s["gu_ps"], n - 1)
            nc.scalar.copy(sT[m % 2][:], tr[m % 2][:]).then_inc(s["sT_ev"], 1)

        def silu(n, m):
            act.wait_ge(s["gu_ps"], n + 1)
            at_least(act, s["h_done"], n - 1)
            nc.scalar.activation(act_s[m % 2][:], gu[m % 2][:, 0:2, :], ACT.Silu).then_inc(s["silu_done"], 1)

        for n in range(AHEAD):
            weights(n, n)
        copy_rows(0, 0)

        def groups(i, first, last):
            for m in range(2 * GROUP):
                n = 2 * GROUP * i + m
                if not (last and m == 2 * GROUP - 1):
                    copy_rows(n + 1, m + 1)
                silu(n, m)
                if not (last and m + AHEAD >= 2 * GROUP):
                    weights(n + AHEAD, m + AHEAD)
        loop(act, groups)

    @block.vector
    def _(dve):
        count = [0]

        def link(ins):
            count[0] += 1
            ins.then_inc(s["cnt_step"], 1)
            dve.wait_ge(s["cnt_step"], count[0])

        link(nc.vector.scalar_tensor_tensor(out=eid_e[:], in0=iota_e[:], scalar=float(E), in1=owner[:], op0=ALU.add, op1=ALU.mult))
        link(nc.vector.tensor_reduce(eid_p[:], eid_e[:], AX.X, ALU.add))
        link(nc.vector.tensor_scalar(diag[:], ident[:], eid_p[:, 0:1], None, ALU.mult))
        dve.wait_ge(s["iotas"], 2)
        link(nc.vector.tensor_copy(pad[:], pad_i[:]))
        dve.wait_ge(s["cnt_ps2"], 1)
        nc.vector.tensor_copy(eid[:], gu[0][0:1, 0, 0:SORTED]).then_inc(s["eid_rdy"], 1)

        def hidden(n, m):
            dve.wait_ge(s["silu_done"], n + 1)
            at_least(dve, s["y_ps"], n - 3)
            nc.vector.tensor_tensor(hT[m % 4][:], act_s[m % 2][:], gu[m % 2][:, 2:4, :], ALU.mult).then_inc(s["h_done"], 1)

        def add_shared(n, m, i):
            k, r = m % GROUP, m // GROUP
            if k == 0:
                dve.wait_ge(ysh_ld[r], 16 * (i + 1))
                at_least(dve, s["fin_step"], 4 * (2 * i + r - 2) + 1)
            dve.wait_ge(s["y_ps"], n + 1)
            nc.vector.tensor_tensor(yg[r][:, k, :], y_p[m % 4][:], ysh[r][:, k, :], ALU.add).then_inc(s["y_ev"], 1)

        def moments(n, m):
            k, r = m % GROUP, m // GROUP
            dve.wait_ge(s["y_ev"], n + 1)
            nc.vector.bn_stats(st3[r][:, k, :], yg[r][:, k, :]).then_inc(s["st_step"], 1)

        def mean_and_variance(n, m):
            k, r = m % GROUP, m // GROUP
            dve.wait_ge(s["st_step"], n + 1)
            dve.sem_inc(s["dve_passed2"], 1)
            nc.vector.bn_aggr(mv3[r][:, k, :], st3[r][:, k, :]).then_inc(s["mv_step"], 1)

        def refine(g, r, k):
            if k == 0:
                dve.wait_ge(s["mv_step"], GROUP * (g + 1))
            else:
                dve.wait_ge(s["root3"], REFINE_STEPS * g + k)
            if k < 3:
                ins = root_guess_step(nc.vector, k, mv3[r], var3[r], rstd3[r])
            else:
                ins = newton_step(nc.vector, k - 3, rstd3[r], var3[r], rtmp3, c15g)
            ins.then_inc(s["root3"], 1)

        def places(g, r):
            num = x1g[r][:, :, D]
            dve.wait_ge(x1_ld[r], times(g, r, 16) + 16)
            at_least(dve, out_st[r], times(g, r, 16 * GROUP))
            nc.vector.scalar_tensor_tensor(out=oidx_f[r][:], in0=num, scalar=0.0, in1=pad[:], op0=ALU.is_equal, op1=ALU.mult).then_inc(s["oidx_step"], 1)
            dve.wait_ge(s["oidx_step"], 2 * g + 1)
            nc.vector.scalar_tensor_tensor(out=oidx_f[r][:], in0=num, scalar=1.0, in1=oidx_f[r][:], op0=ALU.subtract, op1=ALU.max).then_inc(s["oidx_step"], 1)
            dve.wait_ge(s["oidx_step"], 2 * g + 2)
            nc.vector.tensor_copy(oidx[r][:], oidx_f[r][:]).then_inc(s["oidx_rdy"], 1)

        def normalize(g, r, quarter):
            if quarter == 0:
                dve.wait_ge(s["root3"], REFINE_STEPS * (g + 1))
                at_least(dve, out_st[r], times(g, r, 16 * GROUP))
            for k in range(GROUP // 4 * quarter, GROUP // 4 * (quarter + 1)):
                ins = nc.vector.tensor_scalar(og[r][:, k, :], yg[r][:, k, :], mv3[r][:, k, 0:1], rstd3[r][:, k:k + 1], ALU.subtract, ALU.mult)
            ins.then_inc(s["fin_step"], 1)

        def residual(g, r, half):
            dve.wait_ge(s["fin_step"], 4 * g + 2 * half + 2)
            tiles = slice(GROUP // 2 * half, GROUP // 2 * (half + 1))
            nc.vector.tensor_tensor(og[r][:, tiles, :], og[r][:, tiles, :], x1g[r][:, tiles, 0:D], ALU.add).then_inc(s["out_rdy"], 1)

        def finish(since, g, r):
            if since == REFINED - 1:
                places(g, r)
            if since == REFINED + 2:
                residual(g, r, 0)
            if since == REFINED + 4:
                residual(g, r, 1)
            if REFINED <= since < REFINED + 4:
                normalize(g, r, since - REFINED)

        def refine_now(since, g, r, third):
            if GROUP + 5 <= since < REFINED:
                refine(g, r, 3 * (since - GROUP - 5) + third)

        def groups(i, first, last):
            for m in range(2 * GROUP):
                n = 2 * GROUP * i + m
                live = [(m % GROUP + GROUP * ago, 2 * i + m // GROUP - ago, (m // GROUP - ago) % 2) for ago in (0, 1, 2)
                        if not (first and m // GROUP < ago)]
                for since, g, r in live:
                    refine_now(since, g, r, 0)
                hidden(n, m)
                for since, g, r in live:
                    refine_now(since, g, r, 1)
                if not (first and m < 3):
                    add_shared(n - 3, (m - 3) % (2 * GROUP), i if m >= 3 else i - 1)
                for since, g, r in live:
                    refine_now(since, g, r, 2)
                    finish(since, g, r)
                if not (first and m < 5):
                    mean_and_variance(n - 5, (m - 5) % (2 * GROUP))
                if not (first and m < 4):
                    moments(n - 4, (m - 4) % (2 * GROUP))
        loop(dve, groups)
        for step in range(2 * GROUP, 4 * GROUP):
            for q in range(2):
                since, g = step - GROUP * q, GROUPS - 2 + q
                for third in range(3):
                    refine_now(since, g, q, third)
                finish(since, g, q)
            for ago, do in ((3, lambda n, m: add_shared(n, m, GROUPS // 2 - 1)), (5, mean_and_variance), (4, moments)):
                if step - ago < 2 * GROUP:
                    do(SORTED - 2 * GROUP + step - ago, step - ago)


AHEAD = 4
REFINE_STEPS = 3 + NEWTON_STEPS
REFINED = GROUP + 5 + REFINE_STEPS // 3


_INS = ["L0_attn_x", "L0_attn_Wq", "L0_attn_bq", "L0_attn_Wk", "L0_attn_bk", "L0_attn_Wv", "L0_attn_bv", "L0_attn_Wo", "L0_attn_bo",
        "L0_attn_rel_k", "L0_attn_rel_v", "L0_ffn_w_router", "L0_ffn_gate_up_proj", "L0_ffn_down_proj",
        "L0_ffn_w_gate", "L0_ffn_w_up", "L0_ffn_w_down"]
_OUTS = [((16, 512, 128), "float32")]


def kernel(**inputs):
    import numpy as _np
    import concourse.bacc as _bacc
    from concourse import mybir as _mybir
    from concourse.bass_utils import run_bass_kernel_spmd as _run

    nc = _bacc.Bacc("TRN2", target_bir_lowering=False, num_devices=1)
    arrays, args = {}, []
    for name in _INS:
        a = _np.ascontiguousarray(inputs[name])
        arrays[f"in_{name}_dram"] = a
        args.append(nc.dram_tensor(f"in_{name}_dram", a.shape, _mybir.dt.from_np(a.dtype), kind="ExternalInput").ap())
    outs = []
    for i, (shape, dtype) in enumerate(_OUTS):
        dt = _mybir.dt.from_np(_np.dtype(dtype))
        outs.append(nc.dram_tensor(f"out_{i}_dram", shape, dt, kind="ExternalOutput").ap())
    attention(nc, *outs, *args)
    r = _run(nc, [arrays], core_ids=[0])
    got = tuple(r.results[0][f"out_{i}_dram"] for i in range(len(_OUTS)))
    return got[0]
```
